# Optimizing a Trainium2 kernel written in Bass

```python
import numpy as np
import jax
import jax.numpy as jnp

def _softmax(x, axis=-1):
    return jax.nn.softmax(x, axis=axis)

def _gelu(x):
    return jax.nn.gelu(x, approximate=True)

def _silu(x):
    return jax.nn.silu(x)

def _sigmoid(x):
    return jax.nn.sigmoid(x)

def _layernorm(x, axis=-1, eps=1e-05):
    m = jnp.mean(x, axis=axis, keepdims=True)
    v = jnp.var(x, axis=axis, keepdims=True)
    return (x - m) / jnp.sqrt(v + eps)

def _scatter_add(tgt, idx, src, axis=0):
    return tgt.at[idx].add(src)

def _segment_sum(src, seg, n):
    return jax.ops.segment_sum(src, seg, n)
kernel_name = 'mk_gnn_resnorm_d1_gnn_r32_4d94bc'

def setup_inputs(seed: int=0):
    np.random.seed(seed)
    _w = jnp.asarray

    def _rec_inputs():
        import jax
        import jax.numpy as jnp
        _gk = jax.random.key(seed)
        x = -0.0001079 + 1 * jax.random.normal(jax.random.fold_in(_gk, 1), (50000, 64), jnp.float32)
        src = jax.random.randint(jax.random.fold_in(_gk, 2), (50000,), 0, 50000, jnp.int32)
        dst = jax.random.randint(jax.random.fold_in(_gk, 3), (50000,), 0, 50000, jnp.int32)
        _o = jnp.argsort(dst, stable=True)
        src = src[_o]
        dst = dst[_o]
        edge_attr_64 = 0.000189758 + 1.00013 * jax.random.normal(jax.random.fold_in(_gk, 11), (50000, 64), jnp.float32)
        return (x, src, dst, edge_attr_64)
    x, src, dst, edge_attr_64 = _rec_inputs()

    def _L0_gnn_setup():
        import jax, jax.numpy as jnp
        import numpy as np
        N_NODES = 50000
        N_EDGES = 25000
        F = 64
        EPS = 1e-05
        key = jax.random.key(seed)
        ks = jax.random.split(key, 10)
        w = lambda k, s: jax.random.normal(k, s, dtype=jnp.float32) * 0.05
        edge_index = jax.random.randint(ks[0], (2, N_EDGES), 0, N_NODES, dtype=jnp.int64)
        return {'x': jax.random.normal(ks[1], (N_NODES, F), dtype=jnp.float32), 'edge_index': edge_index, 'edge_attr': jax.random.normal(ks[2], (N_EDGES, F), dtype=jnp.float32), 'W_e': w(ks[3], (F, F)), 'b_e': jnp.zeros((F,), jnp.float32), 'W_pre': w(ks[4], (3 * F, F)), 'b_pre': jnp.zeros((F,), jnp.float32), 'W_post': w(ks[5], (13 * F, F)), 'b_post': jnp.zeros((F,), jnp.float32), 'W_lin': w(ks[6], (F, F)), 'b_lin': jnp.zeros((F,), jnp.float32)}
    _L0_gnn_all = _L0_gnn_setup()
    _L0_gnn_in = {k: v for k, v in _L0_gnn_all.items() if k in ('W_e', 'b_e', 'W_pre', 'b_pre', 'W_post', 'b_post', 'W_lin', 'b_lin')}
    del _L0_gnn_all
    return {'x': x, 'src': src, 'dst': dst, 'edge_attr_64': edge_attr_64, 'L0_gnn_W_e': _L0_gnn_in['W_e'], 'L0_gnn_b_e': _L0_gnn_in['b_e'], 'L0_gnn_W_pre': _L0_gnn_in['W_pre'], 'L0_gnn_b_pre': _L0_gnn_in['b_pre'], 'L0_gnn_W_post': _L0_gnn_in['W_post'], 'L0_gnn_b_post': _L0_gnn_in['b_post'], 'L0_gnn_W_lin': _L0_gnn_in['W_lin'], 'L0_gnn_b_lin': _L0_gnn_in['b_lin']}

def reference(x, src, dst, edge_attr_64, L0_gnn_W_e, L0_gnn_b_e, L0_gnn_W_pre, L0_gnn_b_pre, L0_gnn_W_post, L0_gnn_b_post, L0_gnn_W_lin, L0_gnn_b_lin):
    import jax
    import jax.numpy as jnp

    def _L0_gnn_ref(x, edge_index, edge_attr, W_e, b_e, W_pre, b_pre, W_post, b_post, W_lin, b_lin):
        import jax, jax.numpy as jnp
        import numpy as np
        N_NODES = 50000
        N_EDGES = 25000
        F = 64
        EPS = 1e-05
        src = edge_index[0]
        dst = edge_index[1]
        e = edge_attr @ W_e + b_e
        h = jnp.concatenate([x[dst], x[src], e], axis=-1)
        m = h @ W_pre + b_pre
        ones = jnp.ones((m.shape[0],), m.dtype)
        deg = jax.ops.segment_sum(ones, dst, num_segments=N_NODES)
        degc = jnp.maximum(deg, 1.0)
        s1 = jax.ops.segment_sum(m, dst, num_segments=N_NODES)
        s2 = jax.ops.segment_sum(m * m, dst, num_segments=N_NODES)
        mean = s1 / degc[:, None]
        var = s2 / degc[:, None] - mean * mean
        std = jnp.sqrt(jax.nn.relu(var) + EPS)
        mx = jax.ops.segment_max(m, dst, num_segments=N_NODES)
        mn = jax.ops.segment_min(m, dst, num_segments=N_NODES)
        has = (deg > 0)[:, None]
        mx = jnp.where(has, mx, 0.0)
        mn = jnp.where(has, mn, 0.0)
        aggr = jnp.concatenate([mean, std, mx, mn], axis=-1)
        avg_log = jnp.mean(jnp.log(deg + 1.0))
        log_deg = jnp.log(degc + 1.0)[:, None]
        out = jnp.concatenate([aggr, aggr * (log_deg / avg_log), aggr * (avg_log / log_deg)], axis=-1)
        out = jnp.concatenate([x, out], axis=-1)
        out = out @ W_post + b_post
        return out @ W_lin + b_lin
    edge_index = jnp.stack([src, dst])
    x = _layernorm(x + _L0_gnn_ref(x, edge_index, edge_attr_64, L0_gnn_W_e, L0_gnn_b_e, L0_gnn_W_pre, L0_gnn_b_pre, L0_gnn_W_post, L0_gnn_b_post, L0_gnn_W_lin, L0_gnn_b_lin), axis=-1)
    return x

_drawn_inputs = setup_inputs


def setup_inputs(seed=0):
    import zlib

    import numpy as np

    out = dict(_drawn_inputs(seed))
    spreads = {'L0_gnn_b_e': (0.0, 0.389),
     'L0_gnn_b_pre': (0.0, 0.1),
     'L0_gnn_b_post': (0.0, 0.1),
     'L0_gnn_b_lin': (0.0, 0.1)}
    factors = {}
    for name, (base, spread) in spreads.items():
        noise = np.random.default_rng([zlib.crc32(name.encode()), seed]).standard_normal(out[name].shape)
        drawn = base * np.exp(spread * noise) if base else spread * noise
        out[name] = jnp.asarray(drawn.astype(out[name].dtype))
    for name, factor in factors.items():
        out[name] = (out[name] * factor).astype(out[name].dtype)
    return out
```

```python
from contextlib import ExitStack

import numpy as np

import concourse.bass as bass
from concourse import mybir

P = 128
F = 64
K = 4
G = P * K
SLOTS = 4
ROW = F + 4
S_, SI_, ONE_, KEY_ = F, F + 1, F + 2, F + 3
WIN = 2 * P
READY = 3
EPS = 1e-5
BIG = 1.5e38
LN2 = float(np.log(2.0))
TA, TB = 25, 16

LAG_Q, LAG_ST, LAG_VAR, LAG_FT, LAG_TT, LAG_STORE = 1, 2, 3, 4, 5, 6
LAG_WIN = LAG_STORE + 1 + READY - 1
LAG_OH, LAG_XS, LAG_XT, LAG_Y, LAG_NORM, LAG_OUT = (LAG_WIN + 1, LAG_WIN + 2, LAG_WIN + 3, LAG_WIN + 4,
                                                    LAG_WIN + 5, LAG_WIN + 6)
AHEAD = 2


class Turn:

    def __init__(self, rnd, slot, ago=0, value=None):
        self.rnd, self.slot, self.ago, self.value = rnd, slot, ago, value

    def back(self, d):
        k, slot = divmod(self.slot - d, SLOTS)
        return Turn(self.rnd, slot, self.ago - k, self.value)

    @property
    def number(self):
        return (self.rnd - self.ago) * SLOTS + self.slot

    def count(self, each):
        if self.value is not None:
            return self.value(each, (1 - self.ago) * each)
        return (self.rnd - self.ago + 1) * each

    def total(self):
        if self.value is not None:
            return self.value(SLOTS, self.slot + 1 - self.ago * SLOTS)
        return self.number + 1

    def within(self, n):
        return self.value is not None or 0 <= self.number < n


def after(eng, signal, turn, each=1):
    v = turn.count(each) if isinstance(signal, list) else turn.total()
    if not isinstance(v, int) or v > 0:
        eng.wait_ge(signal[turn.slot] if isinstance(signal, list) else signal, v)


def registers(eng, r, ahead=()):
    known = {}

    def value(each, more):
        if (each, more) not in known:
            known[each, more] = eng.snap(r * each + more)
        return known[each, more]

    for key in ahead:
        value(*key)
    return value


def run(eng, first_full, last_full, total, step, ahead=()):
    for i in range(first_full):
        step(Turn(i // SLOTS, i % SLOTS))
    with eng.Fori(first_full // SLOTS, last_full // SLOTS) as r:
        value = registers(eng, r, ahead)
        for u in range(SLOTS):
            step(Turn(r, u, 0, value))
    for i in range(last_full, total):
        step(Turn(i // SLOTS, i % SLOTS))


def build(nc, x, src, dst, attr, W_e, b_e, W_pre, b_pre, W_post, b_post, W_lin, b_lin, out):
    f32, bf16, i32 = mybir.dt.float32, mybir.dt.bfloat16, mybir.dt.int32
    ALU, ACT, AX = mybir.AluOpType, mybir.ActivationFunctionType, mybir.AxisListType
    N, E = x.shape[0], src.shape[0]
    NG = -(-max(N, E) // G)
    EP = NG * G
    L = EP // P
    E_TAIL = (E - (NG - 1) * G) // K
    LAST_TILES, LAST_ROWS = divmod(N - (NG - 1) * G, P)
    TOTAL = NG + LAG_OUT
    FULL0, FULL1 = 20, (NG - 1 - AHEAD) // SLOTS * SLOTS

    ctx = ExitStack()
    with ctx:
        def sb(name, shape, dt=f32):
            return ctx.enter_context(nc.sbuf_tensor(name, shape, dt))

        def sem(name):
            return ctx.enter_context(nc.semaphore(name))

        def slot_sems(name):
            return [sem(f"{name}{s}") for s in range(SLOTS)]

        def slots(name, shape, dt=f32):
            return [sb(f"{name}{s}", shape, dt) for s in range(SLOTS)]

        mask_d = nc.dram_tensor("mask_scratch", (2, EP), bf16, kind="Internal").ap()
        esc_d = nc.dram_tensor("edge_scalar_scratch", (EP, 5), f32, kind="Internal").ap()
        rows_d = nc.dram_tensor("row_scratch", (EP + WIN, ROW), f32, kind="Internal").ap()
        lo_d = nc.dram_tensor("window_scratch", (3, TA * TB), i32, kind="Internal").ap()

        ident = sb("ident", [P, P])
        ones = sb("ones", [P, P])
        ones_b = sb("ones_b", [3, G], bf16)
        upper = sb("upper", [TA, TA])
        node_iota = sb("node_iota", [P, K, P])
        group_base = sb("group_base", [P, NG])
        win_limit = sb("win_limit", [TA, TB])
        WP = sb("WP", [P, 6, F])
        WP0 = sb("WP0", [F, F])
        WPT = sb("WPT", [F, 6, P])
        WP0T = sb("WP0T", [F, F])
        WPRE = sb("WPRE", [F, 3, F])
        W11 = sb("W11", [F, P])
        WE = sb("WE", [F, F])
        WET = sb("WET", [F, P])
        WL = sb("WL", [F, F])
        be_c = sb("be_c", [F, 1])
        bpost_c = sb("bpost_c", [F, 1])
        bpre_r = sb("bpre_r", [1, F])
        blin_r = sb("blin_r", [1, F])
        be_3 = sb("be_3", [F, 3])
        bpost_b = sb("bpost_b", [F, P])
        RF = sb("RF", [P, 3, F])
        RM = sb("RM", [P, 3, F])
        RMp = sb("RMp", [P, 3, F])
        LF = sb("LF", [P, P])
        LM = sb("LM", [P, P])
        QW = sb("QW", [P, P])
        WN1 = sb("WN1", [P, F])
        WN2 = sb("WN2", [P, F])
        std0 = sb("std0", [P, P])
        v0 = sb("v0", [P, F])
        split_in = sb("split_in", [3, 4, F])
        split_hi = sb("split_hi", [3, 4, F], bf16)
        split_r1 = sb("split_r1", [3, 4, F])
        split_mid = sb("split_mid", [3, 4, F], bf16)
        split_r2 = sb("split_r2", [3, 4, F])
        split_lo = sb("split_lo", [3, 4, F], bf16)
        split_acc = sb("split_acc", [3, 4, F])
        bias3 = sb("bias3", [3, 4, F], bf16)
        bv = sb("bv", [P, F])
        eps_c = sb("eps_c", [P, 1])

        dst_i = sb("dst_i", [P, L + 2], i32)
        dst_f = sb("dst_f", [P, L + 2])
        shared_x = sb("shared_x", [P, SLOTS, K * 4 * F])
        prep = shared_x[:, :, :].rearrange("p s n -> p (s n)")[:, 0:10 * L].rearrange("p (a l) -> p a l", a=10)
        edge_no, first, ends, starts, run_max, deg, log_deg, tmp = (prep[:, a, :] for a in range(8))
        ta_i, tb_i = (prep[:, a, :].bitcast(i32) for a in (8, 9))
        mask01 = sb("mask01", [P, L], bf16)
        maskB = sb("maskB", [P, L], bf16)
        ta_b = sb("ta_b", [P, L], bf16)
        tb_b = sb("tb_b", [P, L], bf16)
        shared = sb("shared", [P, 2 * SLOTS, K * 2 * P])
        digits = shared[:, :, :].rearrange("p s n -> p (s n)").bitcast(bf16)
        oh_a = digits[:, 0:TA * L].rearrange("p (a l) -> p a l", a=TA)
        oh_b = digits[:, TA * L:(TA + TB) * L].rearrange("p (i b c) -> p i b c", b=TB, c=8)
        esc = sb("esc", [P, L, 5])
        carry_row = sb("carry_row", [1, P + 1])
        carry_in = sb("carry_in", [1, P])
        carry = sb("carry", [P, 1])
        log_sum = sb("log_sum", [P, 1])
        avg = sb("avg", [P, 4])
        m8 = sb("m8", [P, 8])
        sel16 = sb("sel16", [P, TB])
        hist = sb("hist", [P, TA, 8])
        hist_r = sb("hist_r", [P, TA])
        cnt = sb("cnt", [TA, 2, TB])
        cnt_sum = sb("cnt_sum", [TA, 2, TB])
        chunks_i = sb("chunks_i", [TA, TB], i32)
        zeros = sb("zeros", [P, TB])
        lo = sb("lo", [TA, TB])
        lo_read = sb("lo_read", [TA, TB])
        chunk0 = sb("chunk0", [TA, TB])
        lo_i = sb("lo_i", [TA, 3, TB], i32)
        flags = sb("flags", [TA, 2, TB])
        flag1 = sb("flag1", [TA, 1])
        flag_i = sb("flag_i", [1, 1], i32)
        lo_row = sb("lo_row", [1, 3, TA * TB], i32)
        pad_rows = sb("pad_rows", [P, 2 * ROW])
        esc_t = sb("esc_t", [P, NG, K, 5])

        idx = slots("idx", [P, K], i32)
        XA = slots("XA", [P, K, P])
        msk = slots("msk", [P, 2, G], bf16)
        XT = slots("XT", [P, G])
        SQ = slots("SQ", [P, G])
        SS = slots("SS", [P, G])
        MM = slots("MM", [P, G])
        U = slots("U", [P, K, P])
        M2 = slots("M2", [P, K, F])
        V1 = slots("V1", [P, K, F])
        V2 = slots("V2", [P, K, F])
        FT = slots("FT", [P, K, P])
        C = slots("C", [P, K, ROW])
        c1 = sb("c1", [P, K, F])
        c2 = sb("c2", [P, K, F])
        c3 = sb("c3", [P, K, F])
        WINB = slots("WINB", [P, K, 2 * ROW])
        keyl = slots("keyl", [P, K, 2])
        OH = [shared[:, s, :].rearrange("p (q w n) -> p q w n", q=K, w=2) for s in range(SLOTS)]
        SEL = slots("SEL", [P, K, ROW])
        X4 = [shared_x[:, s, :].rearrange("p (k u f) -> p k u f", k=K, u=4) for s in range(SLOTS)]
        XNT = [shared[:, SLOTS + s, :].rearrange("p (h q n) -> p h q n", h=2, q=K) for s in range(SLOTS)]
        Y = slots("Y", [P, K, F])
        stats = slots("stats", [P, K, 6])
        mv = slots("mv", [P, K, 2])
        sd = slots("sd", [P, K])
        rsd = slots("rsd", [P, K])
        O = slots("O", [P, K, F])

        pX = ctx.enter_context(nc.psum_tensor("pX", [P, 512], f32))
        pQ = ctx.enter_context(nc.psum_tensor("pQ", [P, 512], f32))
        pS = ctx.enter_context(nc.psum_tensor("pS", [P, 512], f32))
        pF = ctx.enter_context(nc.psum_tensor("pF", [P, 512], f32))
        pT = ctx.enter_context(nc.psum_tensor("pT", [P, 2, 512], f32))
        pN = ctx.enter_context(nc.psum_tensor("pN", [P, 512], f32))
        pY = ctx.enter_context(nc.psum_tensor("pY", [P, 512], f32))

        s_dpad, s_dst, s_w, s_pool, s_ident = (sem(n) for n in ("dst_pad", "dst_in", "weights_in", "pool_step", "consts_ready"))
        s_esc_out, s_lo_out, s_prep_in, s_pad_out, s_lo_in = (sem(n) for n in (
            "scalars_stored", "windows_stored", "scalars_in", "pad_rows_stored", "windows_in"))
        (masks_made, scalars_made, windows_made, starts_scanned, carries_scanned, degrees_made, digits_made, logs_summed,
         weights_doubled, turned_copied, folded_copied, biases_split, hist_summed, counts_scanned, prep_done,
         carry_row_done, avg_done, weights_turned, weights_folded, node_weights_folded, hist_done, counts_done, prefix_done, flag_summed, carry_done, logs_done) = (sem(n) for n in (
            "masks_made", "scalars_made", "windows_made", "starts_scanned", "carries_scanned", "degrees_made", "digits_made", "logs_summed",
            "weights_doubled", "turned_copied", "folded_copied", "biases_split", "hist_summed", "counts_scanned", "prep_done",
            "carry_row_done", "avg_done", "weights_turned", "weights_folded", "node_weights_folded", "hist_done", "counts_done", "prefix_done", "flag_summed", "carry_done", "logs_done"))
        s_d = sem("dve_prep_step")
        gathers_begun, masks_begun, stats_begun = sem("gathers_begun"), sem("masks_begun"), sem("stats_begun")

        (idx_in, attr_in, msk_in, gathered, c_stored, win_in, x_in, o_stored) = (slot_sems(n) for n in (
            "idx_in", "attr_in", "msk_in", "gathered", "c_stored", "win_in", "x_in", "o_stored"))
        x_turned, xt_copied, q_done, sq_done, sums_done, maxes_done = (sem(n) for n in (
            "x_turned", "xt_copied", "q_done", "sq_done", "sums_done", "maxes_done"))
        s_turned, u_done, m2_done, vmax_done, var_done, std_done = (sem(n) for n in (
            "s_turned", "u_done", "m2_done", "vmax_done", "var_done", "std_done"))
        f_turned, ft_copied, t_done, c_done, key_done, oh_done = (sem(n) for n in (
            "f_turned", "ft_copied", "t_done", "c_done", "key_done", "oh_done"))
        sel_done, sel_copied, xs_done, xna_turned, xna_copied, xnb_turned = (sem(n) for n in (
            "sel_done", "sel_copied", "xs_done", "xna_turned", "xna_copied", "xnb_turned"))
        xnb_copied, c2_done, c3_done, bn_done, rsd_done, y_done = (sem(n) for n in (
            "xnb_copied", "c2_done", "c3_done", "bn_done", "rsd_done", "y_done"))
        y_added, stat_done, sd_done, o_done = (sem(n) for n in (
            "y_added", "stat_done", "sd_done", "o_done"))


        tile_base = sb("tile_base", [P, 1])
        (g_x, g_win, g_stored, g_based, g_zeroed, g_key, g_oh, g_picked, g_sel, g_xs, g_turned, g_xnt, g_y, g_added,
         g_st, g_mv, g_root, g_inv, g_o) = (sem(f"general_{n}") for n in (
            "x_in", "win_in", "stored", "based", "zeroed", "key", "one_hot", "picked", "summed", "xs", "turned",
            "xnt", "y", "added", "stats", "mean_var", "root", "inverse", "out"))
        g_waited = [sem(f"general_waited{n}") for n in range(3)]

        def dram(ap, offset, pattern):
            return bass.AP(ap.tensor, offset, pattern)

        with nc.Block() as block:
            @block.sync
            def _(sp):
                def first_edge(t):
                    return t.number * G if isinstance(t.number, int) else sp.snap(t.number * G)

                def load_edges(t):
                    g = t.number
                    at = first_edge(t)
                    whole = not isinstance(g, int) or g < NG - 1
                    n = P if whole else E_TAIL
                    after(sp, gathered, t.back(SLOTS), 16 * K)
                    sp.dma_start(idx[t.slot][0:n, :], dram(src, at, [[K, n], [1, K]])).then_inc(idx_in[t.slot], 16)
                    after(sp, x_turned, t.back(SLOTS))
                    sp.dma_start(XA[t.slot][0:n, :, F:P],
                                 dram(attr, g * (G * F), [[K * F, n], [F, K], [1, F]])).then_inc(attr_in[t.slot], 16)

                def load_masks(t):
                    at = first_edge(t)
                    after(sp, sums_done, t.back(SLOTS))
                    after(sp, maxes_done, t.back(SLOTS))
                    sp.sem_inc(masks_begun, 1)
                    sp.dma_start(msk[t.slot][:, :, :],
                                 dram(mask_d, at, [[0, P], [EP, 2], [1, G]])).then_inc(msk_in[t.slot], 16)

                load_edges(Turn(0, 0))
                sp.wait_ge(s_dpad, 1)
                sp.dma_start(dst_i[1:P - 1, :], dram(dst, L - 1, [[L, P - 2], [1, L + 2]])).then_inc(s_dst, 16)
                sp.dma_start(dst_i[0:1, 1:L + 2], dram(dst, 0, [[0, 1], [1, L + 1]])).then_inc(s_dst, 16)
                last0 = (P - 1) * L - 1
                sp.dma_start(dst_i[P - 1:P, 0:E - last0], dram(dst, last0, [[0, 1], [1, E - last0]])).then_inc(s_dst, 16)
                load_edges(Turn(0, 1))
                for to, what in ((WP[:, :, :], dram(W_post, F * F, [[F, P], [P * F, 6], [1, F]])),
                                 (WP0[:, :], W_post[0:F, :]),
                                 (WPRE[:, :, :], dram(W_pre, 0, [[F, F], [F * F, 3], [1, F]])),
                                 (WE[:, :], W_e), (WL[:, :], W_lin),
                                 (be_c[:, :], dram(b_e, 0, [[1, F], [1, 1]])),
                                 (bpost_c[:, :], dram(b_post, 0, [[1, F], [1, 1]])),
                                 (bpre_r[:, :], dram(b_pre, 0, [[0, 1], [1, F]])),
                                 (blin_r[:, :], dram(b_lin, 0, [[0, 1], [1, F]]))):
                    sp.dma_start(to, what).then_inc(s_w, 16)
                sp.wait_ge(masks_made, 1)
                sp.dma_start(dram(mask_d, 0, [[L, P], [1, L]]), mask01[:, :]).then_inc(s_esc_out, 16)
                sp.dma_start(dram(mask_d, EP, [[L, P], [1, L]]), maskB[:, :]).then_inc(s_esc_out, 16)
                sp.wait_ge(s_esc_out, 32)
                load_masks(Turn(0, 0))
                load_masks(Turn(0, 1))
                sp.wait_ge(scalars_made, 1)
                sp.dma_start(dram(esc_d, 0, [[L * 5, P], [1, L * 5]]), esc[:, :, :].rearrange("p l c -> p (l c)")).then_inc(s_esc_out, 16)
                sp.dma_start(dram(rows_d, EP * ROW, [[2 * ROW, P], [1, 2 * ROW]]), pad_rows[:, :]).then_inc(s_pad_out, 16)
                sp.wait_ge(s_esc_out, 48)
                sp.dma_start(esc_t[:, :, :, :].rearrange("p g k c -> p g (k c)"),
                             dram(esc_d, 0, [[5 * K, P], [5 * G, NG], [1, 5 * K]])).then_inc(s_prep_in, 16)
                sp.wait_ge(windows_made, 1)
                sp.dma_start(dram(lo_d, 0, [[TB, TA], [TA * TB, 3], [1, TB]]), lo_i[:, :, :]).then_inc(s_lo_out, 16)
                sp.wait_ge(s_lo_out, 16)
                sp.dma_start(lo_row[:, :, :], dram(lo_d, 0, [[0, 1], [TA * TB, 3], [1, TA * TB]])).then_inc(s_lo_in, 16)
                sp.wait_ge(s_lo_in, 16)
                sp.wait_ge(s_pad_out, 16)

                AHEAD_SP = ()

                def step(i):
                    t = i.back(-AHEAD)
                    if t.within(NG):
                        load_edges(t)
                        load_masks(t)
                    t = i.back(LAG_STORE)
                    if t.within(NG):
                        after(sp, c_done, t)
                        sp.dma_start(dram(rows_d, t.number * (G * ROW), [[K * ROW, P], [1, K * ROW]]),
                                     C[t.slot][:, :, :].rearrange("p k c -> p (k c)")).then_inc(c_stored[t.slot], 16)
                    t = i.back(LAG_WIN)
                    if t.within(NG):
                        _, los = nc.values_load_multi_w_load_instructions(
                            lo_row[0:1, 0, bass.ds(t.number * K, K)], engines=[mybir.EngineType.SP],
                            min_val=0, max_val=EP, skip_runtime_bounds_check_because="clamped on the chip")
                        after(sp, y_done, t.back(SLOTS))
                        newest = i.back(LAG_STORE + 1)
                        if newest.within(NG):
                            after(sp, c_stored, newest, 16)
                        for q in range(K):
                            sp.dma_start(WINB[t.slot][:, q, :],
                                         dram(rows_d, los[q] * ROW, [[2 * ROW, P], [1, 2 * ROW]])).then_inc(win_in[t.slot], 16)
                        after(sp, xnb_turned, t.back(SLOTS))
                        n = t.number
                        if not isinstance(n, int) or n < NG - 1:
                            sp.dma_start(X4[t.slot][:, :, 0, :], dram(x, n * (G * F), [[F, P], [P * F, K], [1, F]])).then_inc(x_in[t.slot], 32)
                        else:
                            sp.dma_start(X4[t.slot][:, 0:LAST_TILES, 0, :],
                                         dram(x, n * G * F, [[F, P], [P * F, LAST_TILES], [1, F]])).then_inc(x_in[t.slot], 16)
                            sp.dma_start(X4[t.slot][0:LAST_ROWS, LAST_TILES, 0, :],
                                         dram(x, (n * G + LAST_TILES * P) * F, [[F, LAST_ROWS], [1, F]])).then_inc(x_in[t.slot], 16)
                    t = i.back(LAG_OUT)
                    if t.within(NG):
                        n = t.number
                        after(sp, o_done, t)
                        if not isinstance(n, int) or n < NG - 1:
                            sp.dma_start(dram(out, n * (G * F), [[F, P], [P * F, K], [1, F]]), O[t.slot][:, :, :]).then_inc(o_stored[t.slot], 32)
                        else:
                            sp.dma_start(dram(out, n * G * F, [[F, P], [P * F, LAST_TILES], [1, F]]),
                                         O[t.slot][:, 0:LAST_TILES, :]).then_inc(o_stored[t.slot], 16)
                            sp.dma_start(dram(out, (n * G + LAST_TILES * P) * F, [[F, LAST_ROWS], [1, F]]),
                                         O[t.slot][0:LAST_ROWS, LAST_TILES, :]).then_inc(o_stored[t.slot], 16)

                run(sp, FULL0, FULL1, TOTAL, step, AHEAD_SP)
                for s in range(SLOTS):
                    sp.wait_ge(o_stored[s], 32 * len(range(s, NG, SLOTS)))

            @block.gpsimd
            def _(pool):
                nc.gpsimd.memset(ident[:, :], 1.0).then_inc(s_pool, 1)
                nc.gpsimd.memset(upper[:, :], 1.0).then_inc(s_pool, 1)
                pool.wait_ge(s_pool, 2)
                nc.gpsimd.affine_select(out=ident[:, :], in_=ident[:, :], compare_op=ALU.is_equal, fill=0.0, base=0,
                                        pattern=[[-1, P]], channel_multiplier=1).then_inc(s_ident, 1)
                nc.gpsimd.affine_select(out=upper[:, :], in_=upper[:, :], compare_op=ALU.is_gt, fill=0.0, base=0,
                                        pattern=[[1, TA]], channel_multiplier=-1).then_inc(s_ident, 1)
                nc.gpsimd.iota(edge_no[:, :], [[1, L]], base=0, channel_multiplier=L,
                               allow_small_or_imprecise_dtypes=True).then_inc(s_ident, 1)
                def gather(t):
                    after(pool, idx_in, t, 16)
                    after(pool, x_turned, t.back(SLOTS))
                    pool.wait_ge(s_ident, 3)
                    pool.sem_inc(gathers_begun, 1)
                    for k in range(K):
                        pool.indirect_dma_start(
                            out=XA[t.slot][:, k, 0:F], out_offset=None, in_=x[:, :],
                            in_offset=bass.IndirectOffsetOnAxis(ap=idx[t.slot][:, k:k + 1], axis=0)).then_inc(gathered[t.slot], 16)

                gather(Turn(0, 0))
                nc.gpsimd.iota(win_limit[:, :].rearrange("p (a b) -> p a b", a=TB // K), [[G, TB // K], [0, K]],
                               base=G * READY - WIN, channel_multiplier=TB // K * G,
                               allow_small_or_imprecise_dtypes=True).then_inc(s_ident, 1)
                nc.gpsimd.iota(node_iota[:, :, :].rearrange("p a b -> p (a b)"), [[1, G]], base=0, channel_multiplier=0,
                               allow_small_or_imprecise_dtypes=True).then_inc(s_ident, 1)
                nc.gpsimd.iota(group_base[:, :], [[G, NG]], base=0, channel_multiplier=0,
                               allow_small_or_imprecise_dtypes=True).then_inc(s_ident, 1)
                for g in range(1, SLOTS):
                    gather(Turn(0, g))
                with pool.Fori(1, NG // SLOTS) as r:
                    value = registers(pool, r)
                    for u in range(SLOTS):
                        gather(Turn(r, u, 0, value))
                for g in range(NG // SLOTS * SLOTS, NG):
                    gather(Turn(g // SLOTS, g % SLOTS))

            @block.vector
            def _(dve):
                seen = [0]

                def link(ins):
                    seen[0] += 1
                    ins.then_inc(s_d, 1)
                    dve.wait_ge(s_d, seen[0])

                def mark(event):
                    V.engine_nop().then_inc(event, 1)

                V = nc.vector
                V.memset(dst_i[:, :], -1).then_inc(s_dpad, 1)
                link(V.memset(ones[:, :], 1.0))
                link(V.memset(ones_b[:, :], 1.0))
                link(V.memset(zeros[:, :], 0.0))
                link(V.memset(eps_c[:, :], EPS))
                link(V.memset(std0[0:F, :], 0.0))
                link(V.memset(std0[F:P, :], float(np.sqrt(np.float32(EPS)))))
                link(V.memset(pad_rows[:, :], -1.0))
                link(V.memset(carry_row[:, 0:1], 0.0))
                link(V.memset(SS[SLOTS - 1][:, G - 1:G], 0.0))
                link(V.memset(MM[SLOTS - 1][:, G - 1:G], 0.0))
                link(V.memset(esc[:, :, 2:3], 1.0))
                dve.wait_ge(s_ident, 3)
                link(V.tensor_reduce(m8[:, :], ident[:, :].rearrange("p (b c) -> p c b", c=8), AX.X, ALU.add))
                link(V.tensor_reduce(sel16[:, :], ident[:, :].rearrange("p (b c) -> p b c", c=8), AX.X, ALU.add))
                dve.wait_ge(s_dst, 48)
                link(V.tensor_copy(dst_f[:, :], dst_i[:, :]))
                link(V.tensor_tensor(first[:, :], dst_f[:, 1:L + 1], dst_f[:, 0:L], ALU.not_equal))
                link(V.tensor_scalar(mask01[:, :], first[:, :], -1.0, 1.0, ALU.mult, ALU.add))
                link(V.tensor_scalar(maskB[:, :], first[:, :], -2 * BIG, BIG, ALU.mult, ALU.add))
                mark(masks_made)
                link(V.tensor_tensor(starts[:, :], first[:, :], edge_no[:, :], ALU.mult))
                link(V.tensor_tensor_scan(run_max[:, :], starts[:, :], starts[:, :], 0.0, ALU.max, ALU.max))
                mark(starts_scanned)
                link(V.tensor_tensor(ends[:, :], dst_f[:, 1:L + 1], dst_f[:, 2:L + 2], ALU.not_equal))
                link(V.scalar_tensor_tensor(tmp[:, :], dst_f[:, 1:L + 1], 1.0, ends[:, :], ALU.add, ALU.mult))
                link(V.tensor_scalar(esc[:, :, 3], tmp[:, :], 1.0, None, ALU.subtract))
                dve.wait_ge(carry_row_done, 1)
                link(V.tensor_copy(carry_in[:, :], pX[0:1, 0:P]))
                link(V.tensor_tensor_scan(carry_row[:, 1:P + 1], carry_in[:, :], carry_in[:, :], 0.0, ALU.max, ALU.max))
                mark(carries_scanned)
                link(V.tensor_scalar(ta_i[:, :], dst_i[:, 1:L + 1], 11, None, ALU.arith_shift_right))
                link(V.tensor_scalar(tb_i[:, :], dst_i[:, 1:L + 1], 7, TB - 1, ALU.arith_shift_right, ALU.bitwise_and))
                link(V.tensor_copy(ta_b[:, :], ta_i[:, :]))
                link(V.tensor_copy(tb_b[:, :], tb_i[:, :]))
                dve.wait_ge(carry_done, 1)
                link(V.tensor_copy(carry[:, :], pX[:, 0:1]))
                link(V.tensor_scalar(starts[:, :], run_max[:, :], carry[:, :], None, ALU.max))
                link(V.scalar_tensor_tensor(deg[:, :], edge_no[:, :], 1.0, starts[:, :], ALU.add, ALU.subtract))
                mark(degrees_made)
                link(V.reciprocal(esc[:, :, 4], deg[:, :]))
                for a in range(TA):
                    link(V.tensor_scalar(oh_a[:, a, :], ta_b[:, :], float(a), None, ALU.is_equal))
                for b in range(TB):
                    link(V.tensor_scalar(oh_b[:, :, b, :], tb_b[:, :].rearrange("p (i c) -> p i c", c=8), float(b), None, ALU.is_equal))
                mark(digits_made)
                dve.wait_ge(logs_done, 1)
                link(V.tensor_tensor(tmp[:, :], log_deg[:, :], ends[:, :], ALU.mult))
                link(V.reduce_sum(log_sum[:, :], tmp[:, :], axis=AX.X))
                mark(logs_summed)
                link(V.reciprocal(tmp[:, :], log_deg[:, :]))
                dve.wait_ge(avg_done, 1)
                link(V.tensor_scalar(avg[:, 0:1], pX[:, 0:1], 1.0 / N, None, ALU.mult))
                link(V.reciprocal(avg[:, 1:2], avg[:, 0:1]))
                link(V.tensor_scalar(avg[:, 2:3], avg[:, 1:2], LN2, None, ALU.mult))
                link(V.tensor_scalar(avg[:, 3:4], avg[:, 0:1], 1.0 / LN2, None, ALU.mult))
                link(V.tensor_scalar(esc[:, :, 0], log_deg[:, :], avg[:, 1:2], None, ALU.mult))
                link(V.tensor_scalar(esc[:, :, 1], tmp[:, :], avg[:, 0:1], None, ALU.mult))
                mark(scalars_made)

                dve.wait_ge(s_w, 16 * 9)
                link(V.tensor_copy(W11[:, 0:F], WPRE[:, 0, :]))
                link(V.tensor_copy(W11[:, F:P], WPRE[:, 0, :]))
                link(V.tensor_copy(be_3[:, :], be_c[:, :].broadcast_to([F, 3])))
                link(V.tensor_copy(bpost_b[:, :], bpost_c[:, :].broadcast_to([F, P])))
                mark(weights_doubled)
                dve.wait_ge(weights_turned, 1)
                link(V.tensor_copy(WPT[:, 0:3, :], pT[0:F, 0, 0:3 * P].rearrange("p (a b) -> p a b", a=3)))
                link(V.tensor_copy(WPT[:, 3:6, :], pT[0:F, 1, 0:3 * P].rearrange("p (a b) -> p a b", a=3)))
                link(V.tensor_copy(WP0T[:, :], pF[0:F, 0:F]))
                for h in range(2):
                    link(V.tensor_copy(WET[:, h * F:h * F + F], pF[0:F, F:2 * F]))
                    link(V.tensor_copy(LM[:, h * F:h * F + F], pF[:, 2 * F:3 * F]))
                link(V.memset(LF[:, :], 0.0))
                link(V.tensor_copy(LF[0:F, :], LM[0:F, :]))
                mark(turned_copied)
                dve.wait_ge(weights_folded, 1)
                for u in range(3):
                    link(V.tensor_copy(RF[:, u, :], pT[:, 0, 2 * u * F:(2 * u + 1) * F]))
                    link(V.tensor_copy(RMp[:, u, :], pT[:, 0, (2 * u + 1) * F:(2 * u + 2) * F]))
                link(V.tensor_copy(RM[0:F, :, :], RMp[0:F, :, :]))
                link(V.tensor_scalar(RM[F:P, :, :], RMp[F:P, :, :], -1.0, None, ALU.mult))
                link(V.tensor_tensor(WN1[0:F, :], pF[0:F, 0:F], ident[0:F, 0:F], ALU.add))
                link(V.tensor_copy(QW[0:F, 0:F], WPRE[:, 1, :]))
                link(V.tensor_scalar(QW[0:F, F:P], WPRE[:, 1, :], -1.0, None, ALU.mult))
                link(V.tensor_copy(QW[F:P, 0:F], pF[F:P, F:2 * F]))
                link(V.tensor_scalar(QW[F:P, F:P], pF[F:P, F:2 * F], -1.0, None, ALU.mult))
                link(V.tensor_copy(split_in[:, 0, :], pF[0:3, 2 * F:3 * F]))
                link(V.tensor_scalar(split_in[:, 1, :], pF[0:3, 2 * F:3 * F], -1.0, None, ALU.mult))
                mark(folded_copied)
                dve.wait_ge(node_weights_folded, 1)
                link(V.tensor_copy(WN1[F:P, :], pT[F:P, 0, F:2 * F]))
                link(V.tensor_copy(WN2[0:F, :], pT[0:F, 0, 0:F]))
                link(V.tensor_copy(WN2[F:P, :], pT[F:P, 0, 2 * F:3 * F]))
                link(V.tensor_scalar(v0[:, :], pF[:, F:2 * F], avg[:, 2:3], None, ALU.mult))
                link(V.tensor_scalar(bv[:, :], pF[:, 2 * F:3 * F], avg[:, 3:4], None, ALU.mult))
                link(V.tensor_tensor(v0[:, :], v0[:, :], bv[:, :], ALU.add))
                link(V.tensor_tensor(v0[:, :], v0[:, :], pF[:, 0:F], ALU.add))
                link(V.tensor_scalar(split_in[:, 2, :], v0[0:3, :], -1.0, None, ALU.mult))
                link(V.tensor_tensor(split_in[:, 3, :], pF[0:3, 3 * F:4 * F], v0[0:3, :], ALU.add))
                link(V.tensor_copy(split_hi[:, :, :], split_in[:, :, :]))
                link(V.tensor_tensor(split_r1[:, :, :], split_in[:, :, :], split_hi[:, :, :], ALU.subtract))
                link(V.tensor_copy(split_mid[:, :, :], split_r1[:, :, :]))
                link(V.tensor_tensor(split_r2[:, :, :], split_r1[:, :, :], split_mid[:, :, :], ALU.subtract))
                link(V.tensor_scalar(split_acc[:, :, :], split_hi[:, :, :], ident[0:3, 0:1], None, ALU.mult))
                link(V.scalar_tensor_tensor(split_in[:, :, :], split_mid[:, :, :], ident[0:3, 1:2], split_acc[:, :, :], ALU.mult, ALU.add))
                link(V.tensor_copy(split_lo[:, :, :], split_r2[:, :, :]))
                link(V.scalar_tensor_tensor(bias3[:, :, :], split_lo[:, :, :], ident[0:3, 2:3], split_in[:, :, :], ALU.mult, ALU.add))
                mark(biases_split)
                dve.wait_ge(hist_done, 1)
                link(V.tensor_tensor(hist[:, :, :], pS[:, 0:TA * 8].rearrange("p (a c) -> p a c", c=8),
                                     m8[:, :].unsqueeze(1).broadcast_to([P, TA, 8]), ALU.mult))
                link(V.tensor_reduce(hist_r[:, :], hist[:, :, :], AX.X, ALU.add))
                mark(hist_summed)
                dve.wait_ge(counts_done, 1)
                link(V.tensor_copy(cnt[:, 0, :], pS[0:TA, 0:TB]))
                link(V.tensor_scalar(lo[:, :], cnt[:, 0, :], float(P - 1), None, ALU.add))
                link(V.tensor_copy(chunks_i[:, :], lo[:, :]))
                link(V.tensor_scalar(chunks_i[:, :], chunks_i[:, :], 7, None, ALU.arith_shift_right))
                link(V.tensor_copy(cnt[:, 1, :], chunks_i[:, :]))
                link(V.tensor_scalar(cnt[:, 1, :], cnt[:, 1, :], 1.0, None, ALU.max))
                for a in range(2):
                    link(V.tensor_tensor_scan(cnt_sum[:, a, :], zeros[0:TA, :], cnt[:, a, :], 0.0, ALU.add, ALU.add))
                mark(counts_scanned)
                dve.wait_ge(prefix_done, 1)
                dve.wait_ge(s_ident, 6)
                link(V.tensor_tensor(lo[:, :], cnt_sum[:, 0, :], cnt[:, 0, :], ALU.subtract))
                link(V.tensor_scalar(lo[:, :], lo[:, :], pS[0:TA, 0:1], None, ALU.add))
                link(V.tensor_tensor(chunk0[:, :], cnt_sum[:, 1, :], cnt[:, 1, :], ALU.subtract))
                link(V.tensor_scalar(chunk0[:, :], chunk0[:, :], pS[0:TA, 1:2], None, ALU.add))
                link(V.tensor_scalar(lo_read[:, :], win_limit[:, :], float(EP), None, ALU.min))
                link(V.tensor_tensor(lo_read[:, :], lo_read[:, :], lo[:, :], ALU.min))
                link(V.tensor_copy(lo_i[:, 0, :], lo_read[:, :]))
                link(V.tensor_copy(lo_i[:, 1, :], lo[:, :]))
                link(V.tensor_copy(lo_i[:, 2, :], chunk0[:, :]))
                link(V.tensor_tensor(flags[:, 0, :], lo_read[:, :], lo[:, :], ALU.not_equal))
                link(V.tensor_scalar(flags[:, 1, :], cnt[:, 0, :], float(WIN), None, ALU.is_gt))
                link(V.tensor_reduce(flag1[:, :], flags[:, :, :], AX.XY, ALU.add))
                mark(windows_made)
                dve.wait_ge(flag_summed, 1)
                link(V.tensor_copy(flag_i[:, :], pS[0:1, 0:1]))
                mark(prep_done)
                dve.wait_ge(s_prep_in, 16)

                def step(i):
                    t = i.back(LAG_VAR)
                    if t.within(NG):
                        after(dve, m2_done, t)
                        after(dve, std_done, t.back(SLOTS))
                        V.tensor_tensor(V1[t.slot][:, :, :], U[t.slot][:, :, F:P], M2[t.slot][:, :, :], ALU.max).then_inc(vmax_done, 1)
                        after(dve, vmax_done, t)
                        V.tensor_tensor(V2[t.slot][:, :, :], V1[t.slot][:, :, :], M2[t.slot][:, :, :], ALU.subtract).then_inc(var_done, 1)
                    t = i.back(LAG_Q)
                    if t.within(NG):
                        after(dve, msk_in, t, 16)
                        after(dve, q_done, t)
                        after(dve, sq_done, t)
                        after(dve, t_done, t.back(SLOTS))
                        before = t.back(1)
                        after(dve, maxes_done, before)
                        V.tensor_tensor_scan(MM[t.slot][:, :], msk[t.slot][:, 1, :], pQ[:, :], MM[before.slot][:, G - 1:G],
                                             ALU.min, ALU.max).then_inc(maxes_done, 1)
                        after(dve, s_turned, t.back(SLOTS))
                        after(dve, sums_done, before)
                        V.tensor_tensor_scan(SS[t.slot][:, :], msk[t.slot][:, 0, :], SQ[t.slot][:, :], SS[before.slot][:, G - 1:G],
                                             ALU.mult, ALU.add).then_inc(sums_done, 1)
                    t = i.back(LAG_OH)
                    if t.within(NG):
                        after(dve, win_in, t, 16 * K)
                        after(dve, y_done, t.back(SLOTS))
                        j = t.number
                        V.tensor_scalar(keyl[t.slot][:, :, :], WINB[t.slot][:, :, KEY_::ROW],
                                        group_base[:, bass.ds(j, 1)], None, ALU.subtract).then_inc(key_done, 1)
                        after(dve, key_done, t)
                        for q in range(K):
                            for w in range(2):
                                last = V.tensor_scalar(OH[t.slot][:, q, w, :], node_iota[:, q, :], keyl[t.slot][:, q, w:w + 1],
                                                       None, ALU.is_equal)
                        last.then_inc(oh_done, 1)
                    t = i.back(LAG_ST)
                    if t.within(NG):
                        g = t.number
                        after(dve, s_turned, t)
                        after(dve, f_turned, t.back(SLOTS))
                        V.tensor_tensor(U[t.slot][:, :, :], pS[:, :].rearrange("p (k f) -> p k f", k=K),
                                        esc_t[:, bass.ds(g, 1), :, 4].rearrange("p o k -> p (o k)").unsqueeze(2).broadcast_to([P, K, P]),
                                        ALU.mult).then_inc(u_done, 1)
                    t = i.back(LAG_TT)
                    if t.within(NG):
                        g = t.number
                        after(dve, c_stored, t.back(SLOTS), 16)
                        V.tensor_copy(C[t.slot][:, :, F:ROW], esc_t[:, bass.ds(g, 1), :, 0:4].rearrange("p o k c -> p (o k) c"))
                        after(dve, t_done, t)
                        T = pT[:, :, 0:6 * F].rearrange("p b (k c) -> p b k c", c=3 * F)

                        def scal(c):
                            return esc_t[:, bass.ds(g, 1), :, c].rearrange("p o (b k) -> p (o b) k", b=2).unsqueeze(3).broadcast_to([P, 2, 2, F])

                        def four(a):
                            return a[:, :, :].rearrange("p (b k) c -> p b k c", b=2)
                        V.tensor_tensor(four(c1), T[:, :, :, F:2 * F], scal(0), ALU.mult)
                        V.tensor_tensor(four(c2), T[:, :, :, 2 * F:3 * F], scal(1), ALU.mult).then_inc(c2_done, 1)
                        after(dve, c2_done, t)
                        V.tensor_tensor(four(c3), T[:, :, :, 0:F], four(c1), ALU.add).then_inc(c3_done, 1)
                        after(dve, c3_done, t)
                        V.tensor_tensor(C[t.slot][:, :, 0:F], c2[:, :, :], c3[:, :, :], ALU.add).then_inc(c_done, 1)
                    t = i.back(LAG_XS)
                    if t.within(NG):
                        after(dve, x_in, t, 32)
                        after(dve, sel_copied, t)
                        for u, c in ((1, S_), (2, ONE_), (3, SI_)):
                            last = V.tensor_tensor(X4[t.slot][:, :, u, :], X4[t.slot][:, :, 0, :],
                                                   SEL[t.slot][:, :, c].unsqueeze(2).broadcast_to([P, K, F]), ALU.mult)
                        last.then_inc(xs_done, 1)
                    t = i.back(LAG_Y)
                    if t.within(NG):
                        after(dve, y_done, t)
                        after(dve, o_done, t.back(SLOTS))
                        V.tensor_tensor(Y[t.slot][:, :, :], pY[:, 0:K * F].rearrange("p (k f) -> p k f", k=K),
                                        SEL[t.slot][:, :, 0:F], ALU.add).then_inc(y_added, 1)
                        after(dve, sd_done, t.back(SLOTS))
                        after(dve, y_added, t)
                        for q in range(K):
                            last = V.bn_stats(stats[t.slot][:, q, :], Y[t.slot][:, q, :])
                        last.then_inc(bn_done, 1)
                        after(dve, bn_done, t)
                        dve.sem_inc(stats_begun, 1)
                        for q in range(K):
                            last = V.bn_aggr(mv[t.slot][:, q, :], stats[t.slot][:, q, :])
                        last.then_inc(stat_done, 1)
                    t = i.back(LAG_NORM)
                    if t.within(NG):
                        after(dve, sd_done, t)
                        V.reciprocal(rsd[t.slot][:, :], sd[t.slot][:, :]).then_inc(rsd_done, 1)
                        after(dve, rsd_done, t)
                        after(dve, o_stored, t.back(SLOTS), 32)
                        for q in range(K):
                            last = V.tensor_scalar(O[t.slot][:, q, :], Y[t.slot][:, q, :], mv[t.slot][:, q, 0:1],
                                                   rsd[t.slot][:, q:q + 1], ALU.subtract, ALU.mult)
                        last.then_inc(o_done, 1)

                run(dve, FULL0, FULL1, TOTAL, step)

            @block.tensor
            def _(pe):
                mm, tr = nc.tensor.matmul, nc.tensor.transpose
                pe.wait_ge(s_ident, 3)
                pe.wait_ge(starts_scanned, 1)
                tr(pX[0:1, 0:P], run_max[:, L - 1:L], ident[:, :]).then_inc(carry_row_done, 1)
                pe.wait_ge(carries_scanned, 1)
                tr(pX[:, 0:1], carry_row[0:1, 0:P], ident[0:1, 0:1]).then_inc(carry_done, 1)
                pe.wait_ge(logs_summed, 1)
                mm(pX[:, 0:1], ones[:, :], log_sum[:, :], start=True, stop=True).then_inc(avg_done, 1)
                pe.wait_ge(s_w, 16 * 9)
                pe.wait_ge(weights_doubled, 1)
                for c in range(6):
                    tr(pT[0:F, c // 3, (c % 3) * P:(c % 3 + 1) * P], WP[:, c, :], ident[:, :])
                tr(pF[0:F, 0:F], WP0[:, :], ident[0:F, 0:F])
                tr(pF[0:F, F:2 * F], WE[:, :], ident[0:F, 0:F])
                tr(pF[:, 2 * F:3 * F], W11[:, :], ident[0:F, 0:F]).then_inc(weights_turned, 1)
                pe.wait_ge(turned_copied, 1)
                for c in range(6):
                    mm(pT[:, 0, c * F:(c + 1) * F], WPT[:, c, :], WL[:, :], start=True, stop=True)
                mm(pF[0:F, 0:F], WP0T[:, :], WL[:, :], start=True, stop=True)
                mm(pF[:, F:2 * F], WET[:, :], WPRE[:, 2, :], start=True, stop=True)
                mm(pF[0:3, 2 * F:3 * F], be_3[:, :], WPRE[:, 2, :], start=True, stop=False)
                mm(pF[0:3, 2 * F:3 * F], ones[0:1, 0:3], bpre_r[:, :], start=False, stop=True).then_inc(weights_folded, 1)
                pe.wait_ge(folded_copied, 1)
                mm(pT[:, 0, 0:3 * F], LF[:, :], RF[:, :, :].rearrange("p a b -> p (a b)"), start=True, stop=False)
                mm(pT[:, 0, 0:3 * F], LM[:, :], RMp[:, :, :].rearrange("p a b -> p (a b)"), start=False, stop=True)
                mm(pF[:, 0:3 * F], std0[:, :], RF[:, :, :].rearrange("p a b -> p (a b)"), start=True, stop=True)
                mm(pF[:, 3 * F:4 * F], bpost_b[:, :], WL[:, :], start=True, stop=False)
                mm(pF[:, 3 * F:4 * F], ones[0:1, :], blin_r[:, :], start=False, stop=True).then_inc(node_weights_folded, 1)
                pe.wait_ge(digits_made, 1)
                for c in range(L // 8):
                    last = mm(pS[:, 0:TA * 8], oh_b[:, c, :, :].rearrange("p b c -> p (b c)"), oh_a[:, :, 8 * c:8 * c + 8],
                              start=(c == 0), stop=(c == L // 8 - 1))
                last.then_inc(hist_done, 1)
                pe.wait_ge(hist_summed, 1)
                mm(pS[0:TA, 0:TB], hist_r[:, :], sel16[:, :], start=True, stop=True).then_inc(counts_done, 1)
                pe.wait_ge(counts_scanned, 1)
                mm(pS[0:TA, 0:2], upper[:, :], cnt_sum[:, :, TB - 1], start=True, stop=True).then_inc(prefix_done, 1)
                pe.wait_ge(windows_made, 1)
                mm(pS[0:1, 0:1], flag1[:, :], ones[0:TA, 0:1], start=True, stop=True).then_inc(flag_summed, 1)
                pe.wait_ge(prep_done, 1)

                def step(i):
                    t = i.back(LAG_TT)
                    if t.within(NG):
                        after(pe, ft_copied, t)
                        after(pe, maxes_done, t)
                        after(pe, c_done, t.back(1))
                        for k in range(K):
                            o = pT[:, k // 2, (k % 2) * 3 * F:(k % 2 + 1) * 3 * F]
                            mm(o, MM[t.slot][:, k::K], RM[:, :, :].rearrange("p a b -> p (a b)"), start=True, stop=False)
                            mm(o, FT[t.slot][:, k, :], RF[:, :, :].rearrange("p a b -> p (a b)"), start=False, stop=False)
                            last = mm(o[:, 0:F], ones_b[:, 0:P], bias3[:, 2, :], start=False, stop=True)
                        last.then_inc(t_done, 1)
                    t = i
                    if t.within(NG):
                        after(pe, gathered, t, 16 * K)
                        after(pe, attr_in, t, 16)
                        after(pe, xt_copied, t.back(1))
                        if i.back(LAG_OH + 1).within(NG):
                            after(pe, sel_copied, i.back(LAG_OH + 1))
                        for k in range(K):
                            last = tr(pX[:, k * P:(k + 1) * P], XA[t.slot][:, k, :], ident[:, :])
                        last.then_inc(x_turned, 1)
                    t = i.back(LAG_Q)
                    if t.within(NG):
                        after(pe, xt_copied, t)
                        after(pe, maxes_done, t.back(1))
                        mm(pQ[:, :], QW[:, :], XT[t.slot][:, :], start=True, stop=False)
                        mm(pQ[:, :], bias3[:, 0:2, :].rearrange("p a b -> p (a b)"), ones_b[:, :], start=False, stop=True).then_inc(q_done, 1)
                    t = i.back(LAG_XT)
                    if t.within(NG):
                        after(pe, xs_done, t)
                        after(pe, xnb_copied, t.back(1))
                        for q in range(K):
                            last = tr(pN[:, q * P:(q + 1) * P], X4[t.slot][:, q, 0:2, :].rearrange("p a b -> p (a b)"), ident[:, :])
                        last.then_inc(xna_turned, 1)
                    t = i.back(LAG_ST)
                    if t.within(NG):
                        after(pe, sums_done, t)
                        after(pe, u_done, t.back(1))
                        for k in range(K):
                            last = tr(pS[:, k * P:(k + 1) * P], SS[t.slot][:, k::K], ident[:, :])
                        last.then_inc(s_turned, 1)
                    t = i.back(LAG_FT)
                    if t.within(NG):
                        after(pe, std_done, t)
                        after(pe, ft_copied, t.back(1))
                        for k in range(K):
                            last = tr(pF[:, k * P:(k + 1) * P], U[t.slot][:, k, :], ident[:, :])
                        last.then_inc(f_turned, 1)
                    t = i.back(LAG_XT)
                    if t.within(NG):
                        after(pe, xna_copied, t)
                        for q in range(K):
                            last = tr(pN[:, q * P:(q + 1) * P], X4[t.slot][:, q, 2:4, :].rearrange("p a b -> p (a b)"), ident[:, :])
                        last.then_inc(xnb_turned, 1)
                    t = i.back(LAG_Y)
                    if t.within(NG):
                        after(pe, xnb_copied, t)
                        after(pe, y_added, t.back(1))
                        for q in range(K):
                            o = pY[:, q * F:(q + 1) * F]
                            mm(o, XNT[t.slot][:, 0, q, :], WN1[:, :], start=True, stop=False)
                            mm(o, XNT[t.slot][:, 1, q, :], WN2[:, :], start=False, stop=False)
                            last = mm(o, ones_b[:, 0:P], bias3[:, 3, :], start=False, stop=True)
                        last.then_inc(y_done, 1)
                    t = i.back(LAG_OH)
                    if t.within(NG):
                        after(pe, oh_done, t)
                        if i.within(NG):
                            after(pe, xt_copied, i)
                        else:
                            after(pe, sel_copied, t.back(1))
                        for q in range(K):
                            o = pX[:, q * ROW:(q + 1) * ROW]
                            for w in range(2):
                                last = mm(o, OH[t.slot][:, q, w, :], WINB[t.slot][:, q, w * ROW:(w + 1) * ROW],
                                          start=(w == 0), stop=(w == 1))
                        last.then_inc(sel_done, 1)

                run(pe, FULL0, FULL1, TOTAL, step)

            @block.scalar
            def _(act):
                A = nc.scalar.activation
                act.wait_ge(degrees_made, 1)
                A(log_deg[:, :], deg[:, :], ACT.Ln, bias=1.0).then_inc(logs_done, 1)
                act.wait_ge(prep_done, 1)

                def own_wait():
                    act.wait_ge(s_ident, 3)

                def step(i):
                    t = i
                    if t.within(NG):
                        after(act, q_done, t.back(SLOTS))
                        after(act, x_turned, t)
                        own_wait()
                        A(XT[t.slot][:, :].rearrange("f (p k) -> f k p", k=K), pX[:, :].rearrange("f (k p) -> f k p", k=K),
                          ACT.Copy).then_inc(xt_copied, 1)
                    t = i.back(LAG_Q)
                    if t.within(NG):
                        after(act, sums_done, t.back(SLOTS))
                        after(act, q_done, t)
                        own_wait()
                        A(SQ[t.slot][0:F, :], pQ[0:F, :], ACT.Copy)
                        A(SQ[t.slot][F:P, :], pQ[F:P, :], ACT.Square).then_inc(sq_done, 1)
                    t = i.back(LAG_VAR)
                    if t.within(NG):
                        after(act, var_done, t.back(SLOTS))
                        after(act, u_done, t)
                        own_wait()
                        A(M2[t.slot][:, :, :], U[t.slot][:, :, 0:F], ACT.Square).then_inc(m2_done, 1)
                    t = i.back(LAG_XT)
                    if t.within(NG):
                        after(act, y_done, t.back(SLOTS))
                        after(act, xna_turned, t)
                        own_wait()
                        A(XNT[t.slot][:, 0, :, :].rearrange("p a b -> p (a b)"), pN[:, :], ACT.Copy).then_inc(xna_copied, 1)
                    t = i.back(LAG_FT)
                    if t.within(NG):
                        after(act, t_done, t.back(SLOTS))
                        after(act, f_turned, t)
                        own_wait()
                        A(FT[t.slot][:, :, :].rearrange("p a b -> p (a b)"), pF[:, :], ACT.Copy).then_inc(ft_copied, 1)
                    t = i.back(LAG_VAR)
                    if t.within(NG):
                        after(act, var_done, t)
                        own_wait()
                        A(U[t.slot][:, :, F:P], V2[t.slot][:, :, :], ACT.Sqrt, bias=eps_c[:, :]).then_inc(std_done, 1)
                    t = i.back(LAG_XT)
                    if t.within(NG):
                        after(act, xnb_turned, t)
                        own_wait()
                        A(XNT[t.slot][:, 1, :, :].rearrange("p a b -> p (a b)"), pN[:, :], ACT.Copy).then_inc(xnb_copied, 1)
                    t = i.back(LAG_OH)
                    if t.within(NG):
                        after(act, y_added, t.back(SLOTS))
                        after(act, sel_done, t)
                        own_wait()
                        A(SEL[t.slot][:, :, :].rearrange("p a b -> p (a b)"), pX[:, 0:K * ROW], ACT.Copy).then_inc(sel_copied, 1)
                    t = i.back(LAG_Y)
                    if t.within(NG):
                        after(act, stat_done, t)
                        own_wait()
                        A(sd[t.slot][:, :], mv[t.slot][:, :, 1], ACT.Sqrt, bias=eps_c[:, :]).then_inc(sd_done, 1)

                run(act, FULL0, FULL1, TOTAL, step)

        TILES = -(-N // P)
        win, oh, sel, x4, xnt = WINB[0][:, 0, 0:ROW], OH[0][:, 0, 0, :], SEL[0][:, 0, :], X4[0][:, 0, :, :], XNT[0][:, :, 0, :]
        key, y, st, mean_var, root, inv, o = (keyl[0][:, 0, 0:1], Y[0][:, 0, :], stats[0][:, 0, :], mv[0][:, 0, :],
                                              sd[0][:, 0:1], rsd[0][:, 0:1], O[0][:, 0, :])

        def tiles(eng, needs, start, chunk, end):
            flag = eng.value_load(flag_i[0:1, 0:1], min_val=0, max_val=2 * TA * TB)
            with eng.If(flag > 0):
                def tile(t, rows):
                    first = eng.value_load(lo_row[0:1, 2, bass.ds(t, 1)], min_val=0, max_val=4 * TA * TB)
                    past = eng.value_load(lo_row[0:1, 2, bass.ds(t + 1, 1)], min_val=0, max_val=4 * TA * TB)
                    low = eng.value_load(lo_row[0:1, 1, bass.ds(t, 1)], min_val=0, max_val=E) if needs else None
                    start(t, rows)
                    with eng.Fori(first, past) as c:
                        chunk(t, c, low, first)
                    end(t, rows)
                with eng.Fori(0, TILES - 1) as t:
                    tile(t, P)
                tile(TILES - 1, N - (TILES - 1) * P)

        nothing = lambda *_: None

        with nc.Block() as block:
            @block.sync
            def _(sp):
                def start(t, rows):
                    sp.wait_ge(g_turned, t)
                    sp.sem_inc(g_waited[0], 1)
                    sp.dma_start(x4[0:rows, 0, :], dram(x, t * (P * F), [[F, rows], [1, F]])).then_inc(g_x, 16)

                def chunk(t, c, low, first):
                    sp.wait_ge(g_picked, c)
                    sp.sem_inc(g_waited[0], 1)
                    sp.dma_start(win, dram(rows_d, (low + (c - first) * P) * ROW, [[ROW, P], [1, ROW]])).then_inc(g_win, 16)

                def end(t, rows):
                    sp.wait_ge(g_o, t + 1)
                    sp.sem_inc(g_waited[0], 1)
                    sp.dma_start(dram(out, t * (P * F), [[F, rows], [1, F]]), o[0:rows, :]).then_inc(g_stored, 16)
                    sp.wait_ge(g_stored, t * 16 + 16)
                    sp.sem_inc(g_waited[0], 1)
                tiles(sp, True, start, chunk, end)

            @block.vector
            def _(dve):
                V = nc.vector
                V.memset(tile_base[:, :], 0.0).then_inc(g_based, 1)

                def start(t, rows):
                    V.memset(sel, 0.0).then_inc(g_zeroed, 1)
                    dve.wait_ge(g_zeroed, t + 1)
                    dve.sem_inc(g_waited[1], 1)

                def chunk(t, c, low, first):
                    dve.wait_ge(g_win, c * 16 + 16)
                    dve.wait_ge(g_based, t + 1)
                    V.tensor_scalar(key, win[:, KEY_:KEY_ + 1], tile_base[:, :], None, ALU.subtract).then_inc(g_key, 1)
                    dve.wait_ge(g_key, c + 1)
                    V.tensor_scalar(oh, node_iota[:, 0, :], key, None, ALU.is_equal).then_inc(g_oh, 1)
                    dve.wait_ge(g_picked, c + 1)
                    V.tensor_tensor(sel, pX[:, 0:ROW], sel, ALU.add).then_inc(g_sel, 1)
                    dve.wait_ge(g_sel, c + 1)

                def end(t, rows):
                    V.tensor_scalar(tile_base[:, :], tile_base[:, :], float(P), None, ALU.add).then_inc(g_based, 1)
                    dve.wait_ge(g_x, t * 16 + 16)
                    for u, c in ((1, S_), (2, ONE_), (3, SI_)):
                        last = V.tensor_scalar(x4[:, u, :], x4[:, 0, :], sel[:, c:c + 1], None, ALU.mult)
                    last.then_inc(g_xs, 1)
                    dve.wait_ge(g_turned, t + 1)
                    V.tensor_copy(xnt, pN[:, 0:2 * P].rearrange("p (a b) -> p a b", a=2)).then_inc(g_xnt, 1)
                    dve.wait_ge(g_y, t + 1)
                    V.tensor_tensor(y, pY[:, 0:F], sel[:, 0:F], ALU.add).then_inc(g_added, 1)
                    dve.wait_ge(g_added, t + 1)
                    V.bn_stats(st, y).then_inc(g_st, 1)
                    dve.wait_ge(g_st, t + 1)
                    dve.sem_inc(g_waited[1], 1)
                    V.bn_aggr(mean_var, st).then_inc(g_mv, 1)
                    dve.wait_ge(g_root, t + 1)
                    V.reciprocal(inv, root).then_inc(g_inv, 1)
                    dve.wait_ge(g_inv, t + 1)
                    V.tensor_scalar(o, y, mean_var[:, 0:1], inv, ALU.subtract, ALU.mult).then_inc(g_o, 1)
                    dve.wait_ge(g_stored, t * 16 + 16)
                    dve.sem_inc(g_waited[1], 1)
                tiles(dve, False, start, chunk, end)

            @block.tensor
            def _(pe):
                def chunk(t, c, low, first):
                    pe.wait_ge(g_sel, c)
                    pe.wait_ge(g_oh, c + 1)
                    nc.tensor.matmul(pX[:, 0:ROW], oh, win, start=True, stop=True).then_inc(g_picked, 1)

                def end(t, rows):
                    pe.wait_ge(g_xs, t + 1)
                    nc.tensor.transpose(pN[:, 0:P], x4[:, 0:2, :].rearrange("p a b -> p (a b)"), ident[:, :])
                    nc.tensor.transpose(pN[:, P:2 * P], x4[:, 2:4, :].rearrange("p a b -> p (a b)"), ident[:, :]).then_inc(g_turned, 1)
                    pe.wait_ge(g_xnt, t + 1)
                    nc.tensor.matmul(pY[:, 0:F], xnt[:, 0, :], WN1[:, :], start=True, stop=False)
                    nc.tensor.matmul(pY[:, 0:F], xnt[:, 1, :], WN2[:, :], start=False, stop=False)
                    nc.tensor.matmul(pY[:, 0:F], ones_b[:, 0:P], bias3[:, 3, :], start=False, stop=True).then_inc(g_y, 1)
                tiles(pe, False, nothing, chunk, end)

            @block.scalar
            def _(act):
                def end(t, rows):
                    act.wait_ge(g_mv, t + 1)
                    act.sem_inc(g_waited[2], 1)
                    nc.scalar.activation(root, mean_var[:, 1:2], ACT.Sqrt, bias=eps_c[:, :]).then_inc(g_root, 1)
                flag = act.value_load(flag_i[0:1, 0:1], min_val=0, max_val=2 * TA * TB)
                with act.If(flag > 0):
                    with act.Fori(0, TILES) as t:
                        end(t, P)


_INS = ["x", "src", "dst", "edge_attr_64", "L0_gnn_W_e", "L0_gnn_b_e", "L0_gnn_W_pre", "L0_gnn_b_pre",
        "L0_gnn_W_post", "L0_gnn_b_post", "L0_gnn_W_lin", "L0_gnn_b_lin"]


def kernel(**inputs):
    import numpy as _np
    import concourse.bacc as _bacc
    from concourse import mybir as _mybir
    from concourse.bass_utils import run_bass_kernel_spmd as _run

    nc = _bacc.Bacc("TRN2", target_bir_lowering=False, num_devices=1)
    arrays, args = {}, []
    for name in _INS:
        a = _np.ascontiguousarray(inputs[name])
        arrays[f"in_{name}"] = a
        args.append(nc.dram_tensor(f"in_{name}", a.shape, _mybir.dt.from_np(a.dtype), kind="ExternalInput").ap())
    shape = inputs["x"].shape
    out = nc.dram_tensor("out_0", shape, _mybir.dt.float32, kind="ExternalOutput").ap()
    build(nc, *args, out)
    return _run(nc, [arrays], core_ids=[0]).results[0]["out_0"]
```

```python
from contextlib import ExitStack

import numpy as np

import concourse.bass as bass
from concourse import mybir

P = 128
F = 64
K = 4
G = P * K
SLOTS = 4
KEY_ = 3 * F // 2 + 5
ROW = KEY_ + 1
SC = 3 * F
PICK = SC + 9
WIN = 2 * P
READY = 3
EPS = 1e-5
BIG = 1.5e38
LN2 = float(np.log(2.0))
TA, TB = 25, 16

LAG_Q, LAG_MEAN, LAG_STD, LAG_TT, LAG_STORE = 1, 2, 3, 4, 5
LAG_WIN = LAG_STORE + 1 + READY - 1
LAG_OH, LAG_XS, LAG_Y, LAG_NORM, LAG_OUT = LAG_WIN + 1, LAG_WIN + 2, LAG_WIN + 3, LAG_WIN + 4, LAG_WIN + 5
AHEAD = 2


class Turn:

    def __init__(self, rnd, slot, ago=0, value=None):
        self.rnd, self.slot, self.ago, self.value = rnd, slot, ago, value

    def back(self, d):
        k, slot = divmod(self.slot - d, SLOTS)
        return Turn(self.rnd, slot, self.ago - k, self.value)

    @property
    def number(self):
        return (self.rnd - self.ago) * SLOTS + self.slot

    def count(self, each):
        if self.value is not None:
            return self.value(each, (1 - self.ago) * each)
        return (self.rnd - self.ago + 1) * each

    def total(self):
        if self.value is not None:
            return self.value(SLOTS, self.slot + 1 - self.ago * SLOTS)
        return self.number + 1

    def within(self, n):
        return self.value is not None or 0 <= self.number < n


def after(eng, signal, turn, each=1):
    v = turn.count(each) if isinstance(signal, list) else turn.total()
    if not isinstance(v, int) or v > 0:
        eng.wait_ge(signal[turn.slot] if isinstance(signal, list) else signal, v)


def registers(eng, r, ahead=()):
    known = {}

    def value(each, more):
        if (each, more) not in known:
            known[each, more] = eng.snap(r * each + more)
        return known[each, more]

    for key in ahead:
        value(*key)
    return value


def run(eng, first_full, last_full, total, step, ahead=()):
    for i in range(first_full):
        step(Turn(i // SLOTS, i % SLOTS))
    with eng.Fori(first_full // SLOTS, last_full // SLOTS) as r:
        value = registers(eng, r, ahead)
        for u in range(SLOTS):
            step(Turn(r, u, 0, value))
    for i in range(last_full, total):
        step(Turn(i // SLOTS, i % SLOTS))


def build(nc, x, src, dst, attr, W_e, b_e, W_pre, b_pre, W_post, b_post, W_lin, b_lin, out):
    f32, bf16, i32 = mybir.dt.float32, mybir.dt.bfloat16, mybir.dt.int32
    ALU, ACT, AX = mybir.AluOpType, mybir.ActivationFunctionType, mybir.AxisListType
    N, E = x.shape[0], src.shape[0]
    NG = -(-max(N, E) // G)
    EP = NG * G
    L = EP // P
    E_TAIL = (E - (NG - 1) * G) // K
    LAST_TILES, LAST_ROWS = divmod(N - (NG - 1) * G, P)
    TOTAL = NG + LAG_OUT
    FULL0, FULL1 = 20, (NG - 1 - AHEAD) // SLOTS * SLOTS

    ctx = ExitStack()
    with ctx:
        def sb(name, shape, dt=f32):
            return ctx.enter_context(nc.sbuf_tensor(name, shape, dt))

        def sem(name):
            return ctx.enter_context(nc.semaphore(name))

        def slot_sems(name):
            return [sem(f"{name}{s}") for s in range(SLOTS)]

        def slots(name, shape, dt=f32):
            return [sb(f"{name}{s}", shape, dt) for s in range(SLOTS)]

        mask_d = nc.dram_tensor("mask_scratch", (EP, 2), f32, kind="Internal").ap()
        esc_d = nc.dram_tensor("edge_scalar_scratch", (EP, 8), f32, kind="Internal").ap()
        rows_d = nc.dram_tensor("row_scratch", (EP + WIN, ROW), f32, kind="Internal").ap()
        lo_d = nc.dram_tensor("window_scratch", (3, TA * TB), i32, kind="Internal").ap()

        ident = sb("ident", [P, P])
        ones = sb("ones", [P, P])
        ones_b = sb("ones_b", [3, G], bf16)
        upper = sb("upper", [TA, TA])
        tile_base_c = sb("tile_base_c", [P, NG, K])
        win_limit = sb("win_limit", [TA, TB])
        WP = sb("WP", [P, 6, F])
        WP0 = sb("WP0", [F, F])
        WPT = sb("WPT", [F, 6, P])
        WP0T = sb("WP0T", [F, F])
        WPRE = sb("WPRE", [F, 3, F])
        W11 = sb("W11", [F, P])
        WE = sb("WE", [F, F])
        WET = sb("WET", [F, P])
        WL = sb("WL", [F, F])
        WL_raw = sb("WL_raw", [F, F])
        WL_mean = sb("WL_mean", [F, 1])
        blin_mean = sb("blin_mean", [1, 1])
        blin_raw = sb("blin_raw", [1, F])
        ident_c = sb("ident_c", [F, F])
        be_c = sb("be_c", [F, 1])
        bpost_c = sb("bpost_c", [F, 1])
        bpre_r = sb("bpre_r", [1, F])
        blin_r = sb("blin_r", [1, F])
        be_3 = sb("be_3", [F, 3])
        bpost_b = sb("bpost_b", [F, P])
        RF = sb("RF", [P, 3, F])
        RM = sb("RM", [P, 3, F])
        RMp = sb("RMp", [P, 3, F])
        LF = sb("LF", [P, P])
        LM = sb("LM", [P, P])
        QW = sb("QW", [P, P])
        WN1 = sb("WN1", [P, F])
        WN2 = sb("WN2", [P, F])
        std0 = sb("std0", [P, P])
        v0 = sb("v0", [P, F])
        split_in = sb("split_in", [3, 4, F])
        split_hi = sb("split_hi", [3, 4, F], bf16)
        split_r1 = sb("split_r1", [3, 4, F])
        split_mid = sb("split_mid", [3, 4, F], bf16)
        split_r2 = sb("split_r2", [3, 4, F])
        split_lo = sb("split_lo", [3, 4, F], bf16)
        split_acc = sb("split_acc", [3, 4, F])
        bias3 = sb("bias3", [3, 4, F], bf16)
        bv = sb("bv", [P, F])
        eps_c = sb("eps_c", [P, 1])

        dst_i = sb("dst_i", [P, L + 2], i32)
        dst_f = sb("dst_f", [P, L + 2])
        shared_x = sb("shared_x", [P, SLOTS, K * 4 * F])
        prep = shared_x[:, :, :].rearrange("p s n -> p (s n)")[:, 0:10 * L].rearrange("p (a l) -> p a l", a=10)
        edge_no, first, ends, starts, run_max, deg, log_deg, tmp = (prep[:, a, :] for a in range(8))
        ta_i, tb_i = (prep[:, a, :].bitcast(i32) for a in (8, 9))
        masks = sb("masks", [P, L, 2])
        masks_b = masks[:, :, :].bitcast(bf16)
        ta_b = sb("ta_b", [P, L], bf16)
        tb_b = sb("tb_b", [P, L], bf16)
        shared = sb("shared", [P, 2 * SLOTS, K * 2 * P])
        digits = shared[:, :, :].rearrange("p s n -> p (s n)").bitcast(bf16)
        oh_a = digits[:, 0:TA * L].rearrange("p (a l) -> p a l", a=TA)
        oh_b = digits[:, TA * L:(TA + TB) * L].rearrange("p (i b c) -> p i b c", b=TB, c=8)
        win_all = sb("win_all", [P, SLOTS, K * 2 * ROW])
        esc = win_all[:, :, :].rearrange("p s n -> p (s n)")[:, 0:8 * L].rearrange("p (l c) -> p l c", c=8)
        esc_b = esc.bitcast(bf16)
        carry_row = sb("carry_row", [1, P + 1])
        carry_in = sb("carry_in", [1, P])
        carry = sb("carry", [P, 1])
        log_sum = sb("log_sum", [P, 1])
        avg = sb("avg", [P, 4])
        m8 = sb("m8", [P, 8])
        sel16 = sb("sel16", [P, TB])
        hist = sb("hist", [P, TA, 8])
        hist_r = sb("hist_r", [P, TA])
        cnt = sb("cnt", [TA, 2, TB])
        cnt_sum = sb("cnt_sum", [TA, 2, TB])
        chunks_i = sb("chunks_i", [TA, TB], i32)
        zeros = sb("zeros", [P, TB])
        lo = sb("lo", [TA, TB])
        lo_read = sb("lo_read", [TA, TB])
        chunk0 = sb("chunk0", [TA, TB])
        lo_i = sb("lo_i", [TA, 3, TB], i32)
        flags = sb("flags", [TA, 2, TB])
        flag1 = sb("flag1", [TA, 1])
        flag_i = sb("flag_i", [1, 1], i32)
        lo_row = sb("lo_row", [1, 3, TA * TB], i32)
        pad_rows = sb("pad_rows", [P, 2 * ROW])
        esc_t = sb("esc_t", [P, NG, K, 8])

        idx = slots("idx", [P, K], i32)
        XA = slots("XA", [P, K, P])
        EM = slots("EM", [P, G, 2])
        EMB = [b[:, :, :].bitcast(bf16) for b in EM]
        XT = slots("XT", [P, G])
        SQ = slots("SQ", [P, G])
        SS = slots("SS", [P, G])
        MM = slots("MM", [P, G])
        MU = [shared[:, SLOTS // 2 + s // 2, (s % 2) * G:(s % 2 + 1) * G] for s in range(SLOTS)]
        VV = slots("VV", [P, G])
        Z = sb("Z", [P, K, 2, F])
        Z2 = sb("Z2", [P, K, F])
        C = slots("C", [P, K, 2, F])
        CB = [b[:, :, :, :].rearrange("p k a f -> p k (a f)").bitcast(bf16) for b in C]
        R = slots("R", [P, K, ROW])
        RB = [b[:, :, :].bitcast(bf16) for b in R]
        WINB = [win_all[:, s, :].rearrange("p (k c) -> p k c", k=K) for s in range(SLOTS)]
        WINH = [w.bitcast(bf16) for w in WINB]
        keyl = slots("keyl", [P, K, 2], bf16)
        OH = [shared[:, s // 2, (s % 2) * G:(s % 2 + 1) * G].bitcast(bf16).rearrange("p (q w n) -> p q w n", q=K, w=2)
              for s in range(SLOTS)]
        node_iota_b = sb("node_iota_b", [P, P], bf16)
        S3 = slots("S3", [P, K, 3])
        X4 = [shared_x[:, s, :].rearrange("p (k u f) -> p k u f", k=K, u=4) for s in range(SLOTS)]
        XNT = [shared[:, SLOTS + s, :].rearrange("p (h q n) -> p h q n", h=2, q=K) for s in range(SLOTS)]
        YSQ = slots("YSQ", [P, K, F])
        ss = slots("ss", [P, K])
        sd = slots("sd", [P, K])
        rsd = slots("rsd", [P, K])
        O = slots("O", [P, K, F])

        pX = ctx.enter_context(nc.psum_tensor("pX", [P, 512], f32))
        pQ = ctx.enter_context(nc.psum_tensor("pQ", [P, 512], f32))
        pT = ctx.enter_context(nc.psum_tensor("pT", [P, 2, 512], f32))
        T = pT[:, :, :].rearrange("p b (k c) -> p (b k) c", k=K // 2)     
        pN = ctx.enter_context(nc.psum_tensor("pN", [P, 2, 512], f32))
        pL = ctx.enter_context(nc.psum_tensor("pL", [P, 512], f32))
        pY = ctx.enter_context(nc.psum_tensor("pY", [P, 512], f32))

        s_dpad, s_dst, s_w, s_pool, s_ident = (sem(n) for n in ("dst_pad", "dst_in", "weights_in", "pool_step", "consts_ready"))
        s_esc_out, s_lo_out, s_prep_in, s_pad_out, s_lo_in = (sem(n) for n in (
            "scalars_stored", "windows_stored", "scalars_in", "pad_rows_stored", "windows_in"))
        (masks_made, scalars_made, windows_made, starts_scanned, carries_scanned, degrees_made, digits_made, logs_summed,
         weights_doubled, turned_copied, folded_copied, biases_split, hist_summed, counts_scanned, prep_done,
         carry_row_done, avg_done, weights_turned, weights_folded, node_weights_folded, hist_done, counts_done, prefix_done, flag_summed, carry_done, logs_done) = (sem(n) for n in (
            "masks_made", "scalars_made", "windows_made", "starts_scanned", "carries_scanned", "degrees_made", "digits_made", "logs_summed",
            "weights_doubled", "turned_copied", "folded_copied", "biases_split", "hist_summed", "counts_scanned", "prep_done",
            "carry_row_done", "avg_done", "weights_turned", "weights_folded", "node_weights_folded", "hist_done", "counts_done", "prefix_done", "flag_summed", "carry_done", "logs_done"))
        s_d = sem("dve_prep_step")
        gathers_begun, masks_begun = sem("gathers_begun"), sem("masks_begun")

        (idx_in, attr_in, masks_in, gathered, c_stored, win_in, x_in, o_stored) = (slot_sems(n) for n in (
            "idx_in", "attr_in", "masks_in", "gathered", "c_stored", "win_in", "x_in", "o_stored"))
        x_turned, xt_copied, q_done, sq_done, sums_done, maxes_done = (sem(n) for n in (
            "x_turned", "xt_copied", "q_done", "sq_done", "sums_done", "maxes_done"))
        mean_done, m2_done, var_done, relu_done, std_done, packed = (sem(n) for n in (
            "mean_done", "m2_done", "var_done", "relu_done", "std_done", "packed"))
        t_done, z_done, z2_done, c_done, rest_done, row_done, key_done, oh_done = (sem(n) for n in (
            "t_done", "z_done", "z2_done", "c_done", "rest_done", "row_done", "key_done", "oh_done"))
        sel_done, s3_done, xs_done, xn_turned, xn_copied = (sem(n) for n in (
            "sel_done", "s3_done", "xs_done", "xn_turned", "xn_copied"))
        y_done, ysq_done, ss_done, sd_done, rsd_done, o_done = (sem(n) for n in (
            "y_done", "ysq_done", "ss_done", "sd_done", "rsd_done", "o_done"))

        tile_base = sb("tile_base", [P, 1])
        g_key1 = sb("g_key1", [P, 1])
        g_row = sb("g_row", [P, PICK])
        g_c = sb("g_c", [P, F])
        g_s3 = sb("g_s3", [P, 3])
        g_iota = sb("g_iota", [P, P])
        g_y1 = sb("g_y1", [P, F])
        g_stats = sb("g_stats", [P, 6])
        g_mean_var = sb("g_mean_var", [P, 2])
        (g_x, g_win, g_stored, g_based, g_zeroed, g_key, g_oh, g_picked, g_sel, g_xs, g_turned, g_xnt, g_y, g_added,
         g_st, g_mv, g_root, g_inv, g_o) = (sem(f"general_{n}") for n in (
            "x_in", "win_in", "stored", "based", "zeroed", "key", "one_hot", "picked", "summed", "xs", "turned",
            "xnt", "y", "added", "stats", "mean_var", "root", "inverse", "out"))
        g_parts = sem("general_parts_summed")
        g_waited = [sem(f"general_waited{n}") for n in range(3)]

        def dram(ap, offset, pattern):
            return bass.AP(ap.tensor, offset, pattern)

        with nc.Block() as block:
            @block.sync
            def _(sp):
                def first_edge(t):
                    return t.number * G if isinstance(t.number, int) else sp.snap(t.number * G)

                def load_edges(t):
                    g = t.number
                    at = first_edge(t)
                    whole = not isinstance(g, int) or g < NG - 1
                    n = P if whole else E_TAIL
                    after(sp, gathered, t.back(SLOTS), 16 * K)
                    sp.dma_start(idx[t.slot][0:n, :], dram(src, at, [[K, n], [1, K]])).then_inc(idx_in[t.slot], 16)
                    after(sp, x_turned, t.back(SLOTS))
                    sp.dma_start(XA[t.slot][0:n, :, F:P],
                                 dram(attr, g * (G * F), [[K * F, n], [F, K], [1, F]])).then_inc(attr_in[t.slot], 16)

                def load_masks(t):
                    at = first_edge(t)
                    after(sp, mean_done, t.back(SLOTS))
                    after(sp, sums_done, t.back(SLOTS))
                    after(sp, maxes_done, t.back(SLOTS))
                    sp.sem_inc(masks_begun, 1)
                    sp.dma_start(EM[t.slot][:, :, :].rearrange("p e c -> p (e c)"),
                                 dram(mask_d, at * 2, [[0, P], [1, 2 * G]])).then_inc(masks_in[t.slot], 16)

                load_edges(Turn(0, 0))
                sp.wait_ge(s_dpad, 1)
                sp.dma_start(dst_i[1:P - 1, :], dram(dst, L - 1, [[L, P - 2], [1, L + 2]])).then_inc(s_dst, 16)
                sp.dma_start(dst_i[0:1, 1:L + 2], dram(dst, 0, [[0, 1], [1, L + 1]])).then_inc(s_dst, 16)
                last0 = (P - 1) * L - 1
                sp.dma_start(dst_i[P - 1:P, 0:E - last0], dram(dst, last0, [[0, 1], [1, E - last0]])).then_inc(s_dst, 16)
                load_edges(Turn(0, 1))
                for to, what in ((WP[:, :, :], dram(W_post, F * F, [[F, P], [P * F, 6], [1, F]])),
                                 (WP0[:, :], W_post[0:F, :]),
                                 (WPRE[:, :, :], dram(W_pre, 0, [[F, F], [F * F, 3], [1, F]])),
                                 (WE[:, :], W_e), (WL_raw[:, :], W_lin),
                                 (be_c[:, :], dram(b_e, 0, [[1, F], [1, 1]])),
                                 (bpost_c[:, :], dram(b_post, 0, [[1, F], [1, 1]])),
                                 (bpre_r[:, :], dram(b_pre, 0, [[0, 1], [1, F]])),
                                 (blin_raw[:, :], dram(b_lin, 0, [[0, 1], [1, F]]))):
                    sp.dma_start(to, what).then_inc(s_w, 16)
                sp.wait_ge(masks_made, 1)
                sp.dma_start(dram(mask_d, 0, [[2 * L, P], [1, 2 * L]]), masks[:, :, :].rearrange("p l c -> p (l c)")).then_inc(s_esc_out, 16)
                sp.wait_ge(s_esc_out, 16)
                load_masks(Turn(0, 0))
                load_masks(Turn(0, 1))
                sp.wait_ge(scalars_made, 1)
                sp.dma_start(dram(esc_d, 0, [[L * 8, P], [1, L * 8]]), esc[:, :, :].rearrange("p l c -> p (l c)")).then_inc(s_esc_out, 16)
                sp.dma_start(dram(rows_d, EP * ROW, [[2 * ROW, P], [1, 2 * ROW]]), pad_rows[:, :]).then_inc(s_pad_out, 16)
                sp.wait_ge(s_esc_out, 32)
                sp.dma_start(esc_t[:, :, :, :].rearrange("p g k c -> p g (k c)"),
                             dram(esc_d, 0, [[8 * K, P], [8 * G, NG], [1, 8 * K]])).then_inc(s_prep_in, 16)
                sp.wait_ge(windows_made, 1)
                sp.dma_start(dram(lo_d, 0, [[TB, TA], [TA * TB, 3], [1, TB]]), lo_i[:, :, :]).then_inc(s_lo_out, 16)
                sp.wait_ge(s_lo_out, 16)
                sp.dma_start(lo_row[:, :, :], dram(lo_d, 0, [[0, 1], [TA * TB, 3], [1, TA * TB]])).then_inc(s_lo_in, 16)
                sp.wait_ge(s_lo_in, 16)
                sp.wait_ge(s_pad_out, 16)

                AHEAD_SP = ()

                def step(i):
                    t = i.back(-AHEAD)
                    if t.within(NG):
                        load_edges(t)
                        load_masks(t)
                    t = i.back(LAG_STORE)
                    if t.within(NG):
                        after(sp, row_done, t)
                        after(sp, packed, t)
                        sp.dma_start(dram(rows_d, t.number * (G * ROW), [[K * ROW, P], [1, K * ROW]]),
                                     R[t.slot][:, :, :].rearrange("p k c -> p (k c)")).then_inc(c_stored[t.slot], 16)
                    t = i.back(LAG_WIN)
                    if t.within(NG):
                        _, los = nc.values_load_multi_w_load_instructions(
                            lo_row[0:1, 0, bass.ds(t.number * K, K)], engines=[mybir.EngineType.SP],
                            min_val=0, max_val=EP, skip_runtime_bounds_check_because="clamped on the chip")
                        after(sp, y_done, t.back(SLOTS))
                        newest = i.back(LAG_STORE + 1)
                        if newest.within(NG):
                            after(sp, c_stored, newest, 16)
                        for q in range(K):
                            sp.dma_start(WINB[t.slot][:, q, :],
                                         dram(rows_d, los[q] * ROW, [[2 * ROW, P], [1, 2 * ROW]])).then_inc(win_in[t.slot], 16)
                        after(sp, xn_turned, t.back(SLOTS))
                        n = t.number
                        if not isinstance(n, int) or n < NG - 1:
                            sp.dma_start(X4[t.slot][:, :, 0, :], dram(x, n * (G * F), [[F, P], [P * F, K], [1, F]])).then_inc(x_in[t.slot], 32)
                        else:
                            sp.dma_start(X4[t.slot][:, 0:LAST_TILES, 0, :],
                                         dram(x, n * G * F, [[F, P], [P * F, LAST_TILES], [1, F]])).then_inc(x_in[t.slot], 16)
                            sp.dma_start(X4[t.slot][0:LAST_ROWS, LAST_TILES, 0, :],
                                         dram(x, (n * G + LAST_TILES * P) * F, [[F, LAST_ROWS], [1, F]])).then_inc(x_in[t.slot], 16)
                    t = i.back(LAG_OUT)
                    if t.within(NG):
                        n = t.number
                        after(sp, o_done, t)
                        if not isinstance(n, int) or n < NG - 1:
                            sp.dma_start(dram(out, n * (G * F), [[F, P], [P * F, K], [1, F]]), O[t.slot][:, :, :]).then_inc(o_stored[t.slot], 32)
                        else:
                            sp.dma_start(dram(out, n * G * F, [[F, P], [P * F, LAST_TILES], [1, F]]),
                                         O[t.slot][:, 0:LAST_TILES, :]).then_inc(o_stored[t.slot], 16)
                            sp.dma_start(dram(out, (n * G + LAST_TILES * P) * F, [[F, LAST_ROWS], [1, F]]),
                                         O[t.slot][0:LAST_ROWS, LAST_TILES, :]).then_inc(o_stored[t.slot], 16)

                run(sp, FULL0, FULL1, TOTAL, step, AHEAD_SP)
                for s in range(SLOTS):
                    sp.wait_ge(o_stored[s], 32 * len(range(s, NG, SLOTS)))

            @block.gpsimd
            def _(pool):
                nc.gpsimd.memset(ident[:, :], 1.0).then_inc(s_pool, 1)
                nc.gpsimd.memset(upper[:, :], 1.0).then_inc(s_pool, 1)
                pool.wait_ge(s_pool, 2)
                nc.gpsimd.affine_select(out=ident[:, :], in_=ident[:, :], compare_op=ALU.is_equal, fill=0.0, base=0,
                                        pattern=[[-1, P]], channel_multiplier=1).then_inc(s_ident, 1)
                nc.gpsimd.affine_select(out=upper[:, :], in_=upper[:, :], compare_op=ALU.is_gt, fill=0.0, base=0,
                                        pattern=[[1, TA]], channel_multiplier=-1).then_inc(s_ident, 1)
                nc.gpsimd.iota(edge_no[:, :], [[1, L]], base=0, channel_multiplier=L,
                               allow_small_or_imprecise_dtypes=True).then_inc(s_ident, 1)
                def gather(t):
                    after(pool, idx_in, t, 16)
                    after(pool, x_turned, t.back(SLOTS))
                    pool.wait_ge(s_ident, 3)
                    pool.sem_inc(gathers_begun, 1)
                    for k in range(K):
                        pool.indirect_dma_start(
                            out=XA[t.slot][:, k, 0:F], out_offset=None, in_=x[:, :],
                            in_offset=bass.IndirectOffsetOnAxis(ap=idx[t.slot][:, k:k + 1], axis=0)).then_inc(gathered[t.slot], 16)

                gather(Turn(0, 0))
                nc.gpsimd.iota(win_limit[:, :].rearrange("p (a b) -> p a b", a=TB // K), [[G, TB // K], [0, K]],
                               base=G * READY - WIN, channel_multiplier=TB // K * G,
                               allow_small_or_imprecise_dtypes=True).then_inc(s_ident, 1)
                nc.gpsimd.iota(g_iota[:, :], [[1, P]], base=0, channel_multiplier=0,
                               allow_small_or_imprecise_dtypes=True).then_inc(s_ident, 1)
                nc.gpsimd.iota(tile_base_c[:, :, :].rearrange("p a b -> p (a b)"), [[P, NG * K]], base=0, channel_multiplier=0,
                               allow_small_or_imprecise_dtypes=True).then_inc(s_ident, 1)
                for g in range(1, SLOTS):
                    gather(Turn(0, g))
                with pool.Fori(1, NG // SLOTS) as r:
                    value = registers(pool, r)
                    for u in range(SLOTS):
                        gather(Turn(r, u, 0, value))
                for g in range(NG // SLOTS * SLOTS, NG):
                    gather(Turn(g // SLOTS, g % SLOTS))

            @block.vector
            def _(dve):
                seen = [0]

                def link(ins):
                    seen[0] += 1
                    ins.then_inc(s_d, 1)
                    dve.wait_ge(s_d, seen[0])

                def mark(event):
                    V.engine_nop().then_inc(event, 1)

                V = nc.vector
                V.memset(dst_i[:, :], -1).then_inc(s_dpad, 1)
                link(V.memset(ones[:, :], 1.0))
                link(V.memset(ones_b[:, :], 1.0))
                link(V.memset(zeros[:, :], 0.0))
                link(V.memset(eps_c[:, :], EPS))
                link(V.memset(std0[0:F, :], 0.0))
                link(V.memset(std0[F:P, :], float(np.sqrt(np.float32(EPS)))))
                link(V.memset(pad_rows[:, :], -1.0))
                link(V.memset(carry_row[:, 0:1], 0.0))
                link(V.memset(SS[SLOTS - 1][:, G - 1:G], 0.0))
                link(V.memset(MM[SLOTS - 1][:, G - 1:G], 0.0))
                link(V.memset(esc_b[:, :, 1:2], 1.0))
                link(V.memset(esc_b[:, :, 4:5], 0.0))
                link(V.memset(esc_b[:, :, 7:8], 0.0))
                link(V.memset(esc_b[:, :, 9:10], 0.0))
                dve.wait_ge(s_ident, 3)
                link(V.tensor_reduce(m8[:, :], ident[:, :].rearrange("p (b c) -> p c b", c=8), AX.X, ALU.add))
                link(V.tensor_reduce(sel16[:, :], ident[:, :].rearrange("p (b c) -> p b c", c=8), AX.X, ALU.add))
                dve.wait_ge(s_dst, 48)
                link(V.tensor_copy(dst_f[:, :], dst_i[:, :]))
                link(V.tensor_tensor(first[:, :], dst_f[:, 1:L + 1], dst_f[:, 0:L], ALU.not_equal))
                link(V.tensor_scalar(masks_b[:, :, 2], first[:, :], -1.0, 1.0, ALU.mult, ALU.add))
                link(V.tensor_scalar(masks_b[:, :, 3], first[:, :], -2 * BIG, BIG, ALU.mult, ALU.add))
                link(V.tensor_tensor(starts[:, :], first[:, :], edge_no[:, :], ALU.mult))
                link(V.tensor_tensor_scan(run_max[:, :], starts[:, :], starts[:, :], 0.0, ALU.max, ALU.max))
                mark(starts_scanned)
                link(V.tensor_tensor(ends[:, :], dst_f[:, 1:L + 1], dst_f[:, 2:L + 2], ALU.not_equal))
                link(V.scalar_tensor_tensor(tmp[:, :], dst_f[:, 1:L + 1], 1.0, ends[:, :], ALU.add, ALU.mult))
                link(V.tensor_scalar(esc[:, :, 5], tmp[:, :], 1.0, None, ALU.subtract))
                dve.wait_ge(carry_row_done, 1)
                link(V.tensor_copy(carry_in[:, :], pX[0:1, 0:P]))
                link(V.tensor_tensor_scan(carry_row[:, 1:P + 1], carry_in[:, :], carry_in[:, :], 0.0, ALU.max, ALU.max))
                mark(carries_scanned)
                link(V.tensor_scalar(ta_i[:, :], dst_i[:, 1:L + 1], 11, None, ALU.arith_shift_right))
                link(V.tensor_scalar(tb_i[:, :], dst_i[:, 1:L + 1], 7, TB - 1, ALU.arith_shift_right, ALU.bitwise_and))
                link(V.tensor_copy(ta_b[:, :], ta_i[:, :]))
                link(V.tensor_copy(tb_b[:, :], tb_i[:, :]))
                dve.wait_ge(carry_done, 1)
                link(V.tensor_copy(carry[:, :], pX[:, 0:1]))
                link(V.tensor_scalar(starts[:, :], run_max[:, :], carry[:, :], None, ALU.max))
                link(V.scalar_tensor_tensor(deg[:, :], edge_no[:, :], 1.0, starts[:, :], ALU.add, ALU.subtract))
                mark(degrees_made)
                link(V.reciprocal(masks[:, :, 0], deg[:, :]))
                mark(masks_made)
                for a in range(TA):
                    link(V.tensor_scalar(oh_a[:, a, :], ta_b[:, :], float(a), None, ALU.is_equal))
                for b in range(TB):
                    link(V.tensor_scalar(oh_b[:, :, b, :], tb_b[:, :].rearrange("p (i c) -> p i c", c=8), float(b), None, ALU.is_equal))
                mark(digits_made)
                dve.wait_ge(logs_done, 1)
                link(V.tensor_tensor(tmp[:, :], log_deg[:, :], ends[:, :], ALU.mult))
                link(V.reduce_sum(log_sum[:, :], tmp[:, :], axis=AX.X))
                mark(logs_summed)
                link(V.reciprocal(tmp[:, :], log_deg[:, :]))
                dve.wait_ge(avg_done, 1)
                link(V.tensor_scalar(avg[:, 0:1], pX[:, 0:1], 1.0 / N, None, ALU.mult))
                link(V.reciprocal(avg[:, 1:2], avg[:, 0:1]))
                link(V.tensor_scalar(avg[:, 2:3], avg[:, 1:2], LN2, None, ALU.mult))
                link(V.tensor_scalar(avg[:, 3:4], avg[:, 0:1], 1.0 / LN2, None, ALU.mult))
                link(V.tensor_scalar(esc[:, :, 6], log_deg[:, :], avg[:, 1:2], None, ALU.mult))
                link(V.tensor_scalar(esc[:, :, 7], tmp[:, :], avg[:, 0:1], None, ALU.mult))
                tmp_b = tmp.bitcast(bf16)
                for u, w in ((0, 6), (2, 7)):
                    link(V.tensor_copy(esc_b[:, :, u], esc_b[:, :, 2 * w + 1]))
                    link(V.tensor_tensor(tmp[:, :], esc[:, :, w], esc_b[:, :, 2 * w + 1], ALU.subtract))
                    link(V.tensor_copy(esc_b[:, :, 3 + u], tmp_b[:, 1::2]))
                    link(V.tensor_tensor(esc_b[:, :, 6 + u], tmp[:, :], tmp_b[:, 1::2], ALU.subtract))
                mark(scalars_made)

                dve.wait_ge(s_w, 16 * 9)
                link(V.reduce_sum(WL_mean[:, :], WL_raw[:, :], axis=AX.X))
                link(V.tensor_scalar(WL_mean[:, :], WL_mean[:, :], 1.0 / F, None, ALU.mult))
                link(V.tensor_scalar(WL[:, :], WL_raw[:, :], WL_mean[:, :], None, ALU.subtract))
                link(V.reduce_sum(blin_mean[:, :], blin_raw[:, :], axis=AX.X))
                link(V.tensor_scalar(blin_mean[:, :], blin_mean[:, :], 1.0 / F, None, ALU.mult))
                link(V.tensor_scalar(blin_r[:, :], blin_raw[:, :], blin_mean[:, :], None, ALU.subtract))
                link(V.tensor_scalar(ident_c[:, :], ident[0:F, 0:F], 1.0 / F, None, ALU.subtract))
                link(V.tensor_copy(W11[:, 0:F], WPRE[:, 0, :]))
                link(V.tensor_copy(W11[:, F:P], WPRE[:, 0, :]))
                link(V.tensor_copy(be_3[:, :], be_c[:, :].broadcast_to([F, 3])))
                link(V.tensor_copy(bpost_b[:, :], bpost_c[:, :].broadcast_to([F, P])))
                mark(weights_doubled)
                dve.wait_ge(weights_turned, 1)
                link(V.tensor_copy(WPT[:, 0:3, :], pT[0:F, 0, 0:3 * P].rearrange("p (a b) -> p a b", a=3)))
                link(V.tensor_copy(WPT[:, 3:6, :], pT[0:F, 1, 0:3 * P].rearrange("p (a b) -> p a b", a=3)))
                link(V.tensor_copy(WP0T[:, :], pN[0:F, 0, 0:F]))
                for h in range(2):
                    link(V.tensor_copy(WET[:, h * F:h * F + F], pN[0:F, 0, F:2 * F]))
                    link(V.tensor_copy(LM[:, h * F:h * F + F], pN[:, 0, 2 * F:3 * F]))
                link(V.memset(LF[:, :], 0.0))
                link(V.tensor_copy(LF[0:F, :], LM[0:F, :]))
                mark(turned_copied)
                dve.wait_ge(weights_folded, 1)
                for u in range(3):
                    link(V.tensor_copy(RF[:, u, :], pT[:, 0, 2 * u * F:(2 * u + 1) * F]))
                    link(V.tensor_copy(RMp[:, u, :], pT[:, 0, (2 * u + 1) * F:(2 * u + 2) * F]))
                link(V.tensor_copy(RM[0:F, :, :], RMp[0:F, :, :]))
                link(V.tensor_scalar(RM[F:P, :, :], RMp[F:P, :, :], -1.0, None, ALU.mult))
                link(V.tensor_tensor(WN1[0:F, :], pN[0:F, 0, 0:F], ident_c[:, :], ALU.add))
                link(V.tensor_copy(QW[0:F, 0:F], WPRE[:, 1, :]))
                link(V.tensor_scalar(QW[0:F, F:P], WPRE[:, 1, :], -1.0, None, ALU.mult))
                link(V.tensor_copy(QW[F:P, 0:F], pN[F:P, 0, F:2 * F]))
                link(V.tensor_scalar(QW[F:P, F:P], pN[F:P, 0, F:2 * F], -1.0, None, ALU.mult))
                link(V.tensor_copy(split_in[:, 0, :], pN[0:3, 0, 2 * F:3 * F]))
                link(V.tensor_scalar(split_in[:, 1, :], pN[0:3, 0, 2 * F:3 * F], -1.0, None, ALU.mult))
                mark(folded_copied)
                dve.wait_ge(node_weights_folded, 1)
                link(V.tensor_copy(WN1[F:P, :], pT[F:P, 0, F:2 * F]))
                link(V.tensor_copy(WN2[0:F, :], pT[0:F, 0, 0:F]))
                link(V.tensor_copy(WN2[F:P, :], pT[F:P, 0, 2 * F:3 * F]))
                link(V.tensor_scalar(v0[:, :], pN[:, 0, F:2 * F], avg[:, 2:3], None, ALU.mult))
                link(V.tensor_scalar(bv[:, :], pN[:, 0, 2 * F:3 * F], avg[:, 3:4], None, ALU.mult))
                link(V.tensor_tensor(v0[:, :], v0[:, :], bv[:, :], ALU.add))
                link(V.tensor_tensor(v0[:, :], v0[:, :], pN[:, 0, 0:F], ALU.add))
                link(V.tensor_scalar(split_in[:, 2, :], v0[0:3, :], -1.0, None, ALU.mult))
                link(V.tensor_tensor(split_in[:, 3, :], pN[0:3, 0, 3 * F:4 * F], v0[0:3, :], ALU.add))
                link(V.tensor_copy(split_hi[:, :, :], split_in[:, :, :]))
                link(V.tensor_tensor(split_r1[:, :, :], split_in[:, :, :], split_hi[:, :, :], ALU.subtract))
                link(V.tensor_copy(split_mid[:, :, :], split_r1[:, :, :]))
                link(V.tensor_tensor(split_r2[:, :, :], split_r1[:, :, :], split_mid[:, :, :], ALU.subtract))
                link(V.tensor_scalar(split_acc[:, :, :], split_hi[:, :, :], ident[0:3, 0:1], None, ALU.mult))
                link(V.scalar_tensor_tensor(split_in[:, :, :], split_mid[:, :, :], ident[0:3, 1:2], split_acc[:, :, :], ALU.mult, ALU.add))
                link(V.tensor_copy(split_lo[:, :, :], split_r2[:, :, :]))
                link(V.scalar_tensor_tensor(bias3[:, :, :], split_lo[:, :, :], ident[0:3, 2:3], split_in[:, :, :], ALU.mult, ALU.add))
                mark(biases_split)
                dve.wait_ge(hist_done, 1)
                link(V.tensor_tensor(hist[:, :, :], pL[:, 0:TA * 8].rearrange("p (a c) -> p a c", c=8),
                                     m8[:, :].unsqueeze(1).broadcast_to([P, TA, 8]), ALU.mult))
                link(V.tensor_reduce(hist_r[:, :], hist[:, :, :], AX.X, ALU.add))
                mark(hist_summed)
                dve.wait_ge(counts_done, 1)
                link(V.tensor_copy(cnt[:, 0, :], pL[0:TA, 0:TB]))
                link(V.tensor_scalar(lo[:, :], cnt[:, 0, :], float(P - 1), None, ALU.add))
                link(V.tensor_copy(chunks_i[:, :], lo[:, :]))
                link(V.tensor_scalar(chunks_i[:, :], chunks_i[:, :], 7, None, ALU.arith_shift_right))
                link(V.tensor_copy(cnt[:, 1, :], chunks_i[:, :]))
                link(V.tensor_scalar(cnt[:, 1, :], cnt[:, 1, :], 1.0, None, ALU.max))
                for a in range(2):
                    link(V.tensor_tensor_scan(cnt_sum[:, a, :], zeros[0:TA, :], cnt[:, a, :], 0.0, ALU.add, ALU.add))
                mark(counts_scanned)
                dve.wait_ge(prefix_done, 1)
                dve.wait_ge(s_ident, 6)
                link(V.tensor_tensor(lo[:, :], cnt_sum[:, 0, :], cnt[:, 0, :], ALU.subtract))
                link(V.tensor_scalar(lo[:, :], lo[:, :], pL[0:TA, 0:1], None, ALU.add))
                link(V.tensor_tensor(chunk0[:, :], cnt_sum[:, 1, :], cnt[:, 1, :], ALU.subtract))
                link(V.tensor_scalar(chunk0[:, :], chunk0[:, :], pL[0:TA, 1:2], None, ALU.add))
                link(V.tensor_scalar(lo_read[:, :], win_limit[:, :], float(EP), None, ALU.min))
                link(V.tensor_tensor(lo_read[:, :], lo_read[:, :], lo[:, :], ALU.min))
                link(V.tensor_copy(lo_i[:, 0, :], lo_read[:, :]))
                link(V.tensor_copy(lo_i[:, 1, :], lo[:, :]))
                link(V.tensor_copy(lo_i[:, 2, :], chunk0[:, :]))
                link(V.tensor_tensor(flags[:, 0, :], lo_read[:, :], lo[:, :], ALU.not_equal))
                link(V.tensor_scalar(flags[:, 1, :], cnt[:, 0, :], float(WIN), None, ALU.is_gt))
                link(V.tensor_reduce(flag1[:, :], flags[:, :, :], AX.XY, ALU.add))
                mark(windows_made)
                dve.wait_ge(flag_summed, 1)
                link(V.tensor_copy(flag_i[:, :], pL[0:1, 0:1]))
                mark(prep_done)
                link(V.tensor_copy(node_iota_b[:, :], g_iota[:, :]))
                dve.wait_ge(s_prep_in, 16)

                def step(i):
                    t = i.back(LAG_NORM)
                    if t.within(NG):
                        after(dve, sd_done, t)
                        after(dve, o_done, t.back(SLOTS))
                        V.reciprocal(rsd[t.slot][:, :], sd[t.slot][:, :]).then_inc(rsd_done, 1)
                    t = i.back(LAG_MEAN)
                    if t.within(NG):
                        after(dve, sums_done, t)
                        after(dve, t_done, t.back(SLOTS))
                        V.tensor_tensor(MU[t.slot], SS[t.slot][:, :], EM[t.slot][:, :, 0], ALU.mult).then_inc(mean_done, 1)
                    t = i.back(LAG_OH)
                    if t.within(NG):
                        j = t.number
                        after(dve, win_in, t, 16 * K)
                        after(dve, oh_done, t.back(SLOTS))
                        V.tensor_tensor(keyl[t.slot][:, :, :], WINB[t.slot][:, :, KEY_::ROW],
                                        tile_base_c[:, bass.ds(j, 1), :].rearrange("p o k -> p (o k)").unsqueeze(2).broadcast_to([P, K, 2]),
                                        ALU.subtract).then_inc(key_done, 1)
                    t = i.back(LAG_NORM)
                    if t.within(NG):
                        after(dve, rsd_done, t)
                        after(dve, o_stored, t.back(SLOTS), 32)
                        V.tensor_tensor(O[t.slot][:, :, :], pY[:, 0:K * F].rearrange("p (k f) -> p k f", k=K),
                                        rsd[t.slot][:, :].unsqueeze(2).broadcast_to([P, K, F]), ALU.mult).then_inc(o_done, 1)
                    t = i.back(LAG_XS)
                    if t.within(NG):
                        after(dve, sel_done, t)
                        after(dve, xs_done, t.back(SLOTS))
                        V.tensor_reduce(S3[t.slot][:, :, :], pL[:, 0:9 * K].rearrange("p (q a u) -> p q u a", q=K, a=3),
                                        AX.X, ALU.add).then_inc(s3_done, 1)
                    t = i.back(LAG_OH)
                    if t.within(NG):
                        after(dve, key_done, t)
                        after(dve, y_done, t.back(SLOTS))
                        V.tensor_tensor(OH[t.slot], node_iota_b[:, :].unsqueeze(1).broadcast_to([P, 2 * K, P]).rearrange("p (q w) n -> p q w n", q=K),
                                        keyl[t.slot][:, :, :].unsqueeze(3).broadcast_to([P, K, 2, P]),
                                        ALU.is_equal).then_inc(oh_done, 1)
                    x = i.back(LAG_XS)
                    if x.within(NG):
                        after(dve, x_in, x, 32)
                        after(dve, s3_done, x)
                        V.tensor_tensor(X4[x.slot][:, :, 1:4, :], X4[x.slot][:, :, 0, :].unsqueeze(2).broadcast_to([P, K, 3, F]),
                                        S3[x.slot][:, :, :].unsqueeze(3).broadcast_to([P, K, 3, F]), ALU.mult).then_inc(xs_done, 1)
                    c = i.back(LAG_TT)
                    if c.within(NG):
                        g = c.number
                        after(dve, c_stored, c.back(SLOTS), 16)
                        V.tensor_copy(R[c.slot][:, :, SC // 2:ROW], esc_t[:, bass.ds(g, 1), :, 0:6].rearrange("p o k c -> p (o k) c"))
                        after(dve, t_done, c)
                        V.tensor_tensor(Z[:, :, :, :], T[:, :, F:3 * F].rearrange("p k (j f) -> p k j f", j=2),
                                        esc_t[:, bass.ds(g, 1), :, 6:8].rearrange("p o k c -> p (o k) c").unsqueeze(3).broadcast_to([P, K, 2, F]),
                                        ALU.mult).then_inc(z_done, 1)
                    t = i.back(LAG_MEAN)
                    if t.within(NG):
                        after(dve, m2_done, t)
                        V.tensor_tensor(VV[t.slot][F:P, :], MU[t.slot][F:P, :], VV[t.slot][F:P, :], ALU.subtract).then_inc(var_done, 1)
                    if c.within(NG):
                        after(dve, z_done, c)
                        V.tensor_tensor(Z2[:, :, :], T[:, :, 0:F], Z[:, :, 0, :], ALU.add).then_inc(z2_done, 1)
                    t = i.back(LAG_Q)
                    if t.within(NG):
                        after(dve, masks_in, t, 16)
                        after(dve, sq_done, t)
                        after(dve, t_done, t.back(SLOTS))
                        before = t.back(1)
                        after(dve, maxes_done, before)
                        V.tensor_tensor_scan(MM[t.slot][:, :], EMB[t.slot][:, :, 3], pQ[:, :], MM[before.slot][:, G - 1:G],
                                             ALU.min, ALU.max).then_inc(maxes_done, 1)
                    if c.within(NG):
                        after(dve, z2_done, c)
                        after(dve, packed, c.back(SLOTS))
                        V.tensor_tensor(C[c.slot][:, :, 0, :], Z[:, :, 1, :], Z2[:, :, :], ALU.add).then_inc(c_done, 1)
                    if t.within(NG):
                        after(dve, sums_done, before)
                        V.tensor_tensor_scan(SS[t.slot][:, :], EMB[t.slot][:, :, 2], SQ[t.slot][:, :], SS[before.slot][:, G - 1:G],
                                             ALU.mult, ALU.add).then_inc(sums_done, 1)
                    if c.within(NG):
                        after(dve, c_done, c)
                        V.tensor_tensor(C[c.slot][:, :, 1, :], C[c.slot][:, :, 0, :], CB[c.slot][:, :, 1:2 * F:2], ALU.subtract).then_inc(rest_done, 1)
                    t = i.back(LAG_Y)
                    if t.within(NG):
                        after(dve, ysq_done, t)
                        after(dve, sd_done, t.back(SLOTS))
                        V.tensor_reduce(ss[t.slot][:, :], YSQ[t.slot][:, :, :], AX.X, ALU.add).then_inc(ss_done, 1)
                    if c.within(NG):
                        after(dve, rest_done, c)
                        V.tensor_tensor(RB[c.slot][:, :, 2 * F:3 * F], C[c.slot][:, :, 1, :], CB[c.slot][:, :, 2 * F + 1:4 * F:2],
                                        ALU.subtract).then_inc(row_done, 1)

                run(dve, FULL0, FULL1, TOTAL, step)

            @block.tensor
            def _(pe):
                mm, tr = nc.tensor.matmul, nc.tensor.transpose
                pe.wait_ge(s_ident, 3)
                pe.wait_ge(starts_scanned, 1)
                tr(pX[0:1, 0:P], run_max[:, L - 1:L], ident[:, :]).then_inc(carry_row_done, 1)
                pe.wait_ge(carries_scanned, 1)
                tr(pX[:, 0:1], carry_row[0:1, 0:P], ident[0:1, 0:1]).then_inc(carry_done, 1)
                pe.wait_ge(logs_summed, 1)
                mm(pX[:, 0:1], ones[:, :], log_sum[:, :], start=True, stop=True).then_inc(avg_done, 1)
                pe.wait_ge(s_w, 16 * 9)
                pe.wait_ge(weights_doubled, 1)
                for c in range(6):
                    tr(pT[0:F, c // 3, (c % 3) * P:(c % 3 + 1) * P], WP[:, c, :], ident[:, :])
                tr(pN[0:F, 0, 0:F], WP0[:, :], ident[0:F, 0:F])
                tr(pN[0:F, 0, F:2 * F], WE[:, :], ident[0:F, 0:F])
                tr(pN[:, 0, 2 * F:3 * F], W11[:, :], ident[0:F, 0:F]).then_inc(weights_turned, 1)
                pe.wait_ge(turned_copied, 1)
                for c in range(6):
                    mm(pT[:, 0, c * F:(c + 1) * F], WPT[:, c, :], WL[:, :], start=True, stop=True)
                mm(pN[0:F, 0, 0:F], WP0T[:, :], WL[:, :], start=True, stop=True)
                mm(pN[:, 0, F:2 * F], WET[:, :], WPRE[:, 2, :], start=True, stop=True)
                mm(pN[0:3, 0, 2 * F:3 * F], be_3[:, :], WPRE[:, 2, :], start=True, stop=False)
                mm(pN[0:3, 0, 2 * F:3 * F], ones[0:1, 0:3], bpre_r[:, :], start=False, stop=True).then_inc(weights_folded, 1)
                pe.wait_ge(folded_copied, 1)
                mm(pT[:, 0, 0:3 * F], LF[:, :], RF[:, :, :].rearrange("p a b -> p (a b)"), start=True, stop=False)
                mm(pT[:, 0, 0:3 * F], LM[:, :], RMp[:, :, :].rearrange("p a b -> p (a b)"), start=False, stop=True)
                mm(pN[:, 0, 0:3 * F], std0[:, :], RF[:, :, :].rearrange("p a b -> p (a b)"), start=True, stop=True)
                mm(pN[:, 0, 3 * F:4 * F], bpost_b[:, :], WL[:, :], start=True, stop=False)
                mm(pN[:, 0, 3 * F:4 * F], ones[0:1, :], blin_r[:, :], start=False, stop=True).then_inc(node_weights_folded, 1)
                pe.wait_ge(digits_made, 1)
                for c in range(L // 8):
                    last = mm(pL[:, 0:TA * 8], oh_b[:, c, :, :].rearrange("p b c -> p (b c)"), oh_a[:, :, 8 * c:8 * c + 8],
                              start=(c == 0), stop=(c == L // 8 - 1))
                last.then_inc(hist_done, 1)
                pe.wait_ge(hist_summed, 1)
                mm(pL[0:TA, 0:TB], hist_r[:, :], sel16[:, :], start=True, stop=True).then_inc(counts_done, 1)
                pe.wait_ge(counts_scanned, 1)
                mm(pL[0:TA, 0:2], upper[:, :], cnt_sum[:, :, TB - 1], start=True, stop=True).then_inc(prefix_done, 1)
                pe.wait_ge(windows_made, 1)
                mm(pL[0:1, 0:1], flag1[:, :], ones[0:TA, 0:1], start=True, stop=True).then_inc(flag_summed, 1)
                pe.wait_ge(prep_done, 1)

                def step(i):
                    t = i.back(LAG_TT)
                    if t.within(NG):
                        after(pe, std_done, t)
                        after(pe, maxes_done, t)
                        after(pe, z2_done, t.back(1))
                        for k in range(K):
                            o = T[:, k, 0:3 * F]
                            mm(o, MM[t.slot][:, k::K], RM[:, :, :].rearrange("p a b -> p (a b)"), start=True, stop=False)
                            mm(o, MU[t.slot][:, k::K], RF[:, :, :].rearrange("p a b -> p (a b)"), start=False, stop=False)
                            last = mm(o[:, 0:F], ones_b[:, 0:P], bias3[:, 2, :], start=False, stop=True)
                        last.then_inc(t_done, 1)
                    t = i
                    if t.within(NG):
                        after(pe, gathered, t, 16 * K)
                        after(pe, attr_in, t, 16)
                        after(pe, xt_copied, t.back(1))
                        for k in range(K):
                            last = tr(pX[:, k * P:(k + 1) * P], XA[t.slot][:, k, :], ident[:, :])
                        last.then_inc(x_turned, 1)
                    t = i.back(LAG_Q)
                    if t.within(NG):
                        after(pe, xt_copied, t)
                        after(pe, maxes_done, t.back(1))
                        mm(pQ[:, :], QW[:, :], XT[t.slot][:, :], start=True, stop=False)
                        mm(pQ[:, :], bias3[:, 0:2, :].rearrange("p a b -> p (a b)"), ones_b[:, :], start=False, stop=True).then_inc(q_done, 1)
                    t = i.back(LAG_Y)
                    if t.within(NG):
                        after(pe, xn_copied, t)
                        after(pe, o_done, t.back(1))
                        for q in range(K):
                            o = pY[:, q * F:(q + 1) * F]
                            for w in range(2):
                                for a in range(3):
                                    h = (w * ROW) * 2 + a * F
                                    mm(o, OH[t.slot][:, q, w, :], WINH[t.slot][:, q, h:h + F], start=(w == 0 and a == 0), stop=False)
                            mm(o, XNT[t.slot][:, 0, q, :], WN1[:, :], start=False, stop=False)
                            mm(o, XNT[t.slot][:, 1, q, :], WN2[:, :], start=False, stop=False)
                            last = mm(o, ones_b[:, 0:P], bias3[:, 3, :], start=False, stop=True)
                        last.then_inc(y_done, 1)
                    t = i.back(LAG_XS)
                    if t.within(NG):
                        after(pe, xs_done, t)
                        after(pe, xn_copied, t.back(1))
                        for h in range(2):
                            for q in range(K):
                                last = tr(pN[:, h, q * P:(q + 1) * P], X4[t.slot][:, q, 2 * h:2 * h + 2, :].rearrange("p a b -> p (a b)"), ident[:, :])
                        last.then_inc(xn_turned, 1)
                    t = i.back(LAG_OH)
                    if t.within(NG):
                        after(pe, oh_done, t)
                        after(pe, s3_done, t.back(1))
                        for q in range(K):
                            for w in range(2):
                                h = (w * ROW) * 2 + SC
                                last = mm(pL[:, q * 9:(q + 1) * 9], OH[t.slot][:, q, w, :], WINH[t.slot][:, q, h:h + 9],
                                          start=(w == 0), stop=(w == 1))
                        last.then_inc(sel_done, 1)

                run(pe, FULL0, FULL1, TOTAL, step)

            @block.scalar
            def _(act):
                A = nc.scalar.activation
                act.wait_ge(degrees_made, 1)
                A(log_deg[:, :], deg[:, :], ACT.Ln, bias=1.0).then_inc(logs_done, 1)
                act.wait_ge(prep_done, 1)

                def own_wait():
                    act.wait_ge(s_ident, 3)

                def step(i):
                    t = i.back(LAG_STORE)
                    if t.within(NG):
                        after(act, c_stored, t.back(SLOTS), 16)
                        after(act, rest_done, t)
                        own_wait()
                        A(RB[t.slot][:, :, 0:2 * F], CB[t.slot][:, :, 1::2], ACT.Copy).then_inc(packed, 1)
                    t = i.back(LAG_STD)
                    if t.within(NG):
                        after(act, var_done, t)
                        own_wait()
                        A(VV[t.slot][F:P, :], VV[t.slot][F:P, :], ACT.Relu).then_inc(relu_done, 1)
                    t = i
                    if t.within(NG):
                        after(act, q_done, t.back(SLOTS))
                        after(act, x_turned, t)
                        own_wait()
                        A(XT[t.slot][:, :].rearrange("f (p k) -> f k p", k=K), pX[:, :].rearrange("f (k p) -> f k p", k=K),
                          ACT.Copy).then_inc(xt_copied, 1)
                    t = i.back(LAG_STD)
                    if t.within(NG):
                        after(act, relu_done, t)
                        own_wait()
                        A(MU[t.slot][F:P, :], VV[t.slot][F:P, :], ACT.Sqrt, bias=eps_c[F:P, :]).then_inc(std_done, 1)
                    t = i.back(LAG_MEAN)
                    if t.within(NG):
                        after(act, std_done, t.back(SLOTS))
                        after(act, mean_done, t)
                        own_wait()
                        A(VV[t.slot][F:P, :], MU[t.slot][0:F, :], ACT.Square).then_inc(m2_done, 1)
                    t = i.back(LAG_Q)
                    if t.within(NG):
                        after(act, sums_done, t.back(SLOTS))
                        after(act, q_done, t)
                        own_wait()
                        A(SQ[t.slot][0:F, :], pQ[0:F, :], ACT.Copy)
                        A(SQ[t.slot][F:P, :], pQ[F:P, :], ACT.Square).then_inc(sq_done, 1)
                    t = i.back(LAG_Y)
                    if t.within(NG):
                        after(act, ss_done, t.back(SLOTS))
                        after(act, y_done, t)
                        own_wait()
                        A(YSQ[t.slot][:, :, :].rearrange("p a b -> p (a b)"), pY[:, 0:K * F], ACT.Square).then_inc(ysq_done, 1)
                    t = i.back(LAG_XS)
                    if t.within(NG):
                        after(act, y_done, t.back(SLOTS))
                        after(act, xn_turned, t)
                        own_wait()
                        A(XNT[t.slot][:, 0, :, :].rearrange("p a b -> p (a b)"), pN[:, 0, :], ACT.Copy)
                        A(XNT[t.slot][:, 1, :, :].rearrange("p a b -> p (a b)"), pN[:, 1, :], ACT.Copy).then_inc(xn_copied, 1)
                    t = i.back(LAG_Y)
                    if t.within(NG):
                        after(act, rsd_done, t.back(SLOTS))
                        after(act, ss_done, t)
                        own_wait()
                        A(sd[t.slot][:, :], ss[t.slot][:, :], ACT.Sqrt, bias=eps_c[:, :], scale=1.0 / F).then_inc(sd_done, 1)

                run(act, FULL0, FULL1, TOTAL, step)

        TILES = -(-N // P)
        win, win_b, oh, sel = WINB[0][:, 0, 0:ROW], WINH[0][:, 0, 0:PICK], OH[0][:, 0, 0, :], g_row[:, :]
        x4, xnt = X4[0][:, 0, :, :], XNT[0][:, :, 0, :]
        key, y, st, mean_var, root, inv, o = (g_key1[:, :], g_y1[:, :], g_stats[:, :], g_mean_var[:, :],
                                              sd[0][:, 0:1], rsd[0][:, 0:1], O[0][:, 0, :])

        def tiles(eng, needs, start, chunk, end):
            flag = eng.value_load(flag_i[0:1, 0:1], min_val=0, max_val=2 * TA * TB)
            with eng.If(flag > 0):
                def tile(t, rows):
                    first = eng.value_load(lo_row[0:1, 2, bass.ds(t, 1)], min_val=0, max_val=4 * TA * TB)
                    past = eng.value_load(lo_row[0:1, 2, bass.ds(t + 1, 1)], min_val=0, max_val=4 * TA * TB)
                    low = eng.value_load(lo_row[0:1, 1, bass.ds(t, 1)], min_val=0, max_val=E) if needs else None
                    start(t, rows)
                    with eng.Fori(first, past) as c:
                        chunk(t, c, low, first)
                    end(t, rows)
                with eng.Fori(0, TILES - 1) as t:
                    tile(t, P)
                tile(TILES - 1, N - (TILES - 1) * P)

        nothing = lambda *_: None

        with nc.Block() as block:
            @block.sync
            def _(sp):
                def start(t, rows):
                    sp.wait_ge(g_turned, t + 1)
                    sp.sem_inc(g_waited[0], 1)
                    sp.dma_start(x4[0:rows, 0, :], dram(x, t * (P * F), [[F, rows], [1, F]])).then_inc(g_x, 16)

                def chunk(t, c, low, first):
                    sp.wait_ge(g_picked, c + 1)
                    sp.sem_inc(g_waited[0], 1)
                    sp.dma_start(win, dram(rows_d, (low + (c - first) * P) * ROW, [[ROW, P], [1, ROW]])).then_inc(g_win, 16)

                def end(t, rows):
                    sp.wait_ge(g_o, t + 1)
                    sp.sem_inc(g_waited[0], 1)
                    sp.dma_start(dram(out, t * (P * F), [[F, rows], [1, F]]), o[0:rows, :]).then_inc(g_stored, 16)
                    sp.wait_ge(g_stored, t * 16 + 16)
                    sp.sem_inc(g_waited[0], 1)
                tiles(sp, True, start, chunk, end)

            @block.vector
            def _(dve):
                V = nc.vector
                dve.sem_inc(g_sel, 1)
                V.memset(tile_base[:, :], 0.0).then_inc(g_based, 1)

                def start(t, rows):
                    V.memset(sel, 0.0).then_inc(g_zeroed, 1)
                    dve.wait_ge(g_zeroed, t + 1)
                    dve.sem_inc(g_waited[1], 1)

                def chunk(t, c, low, first):
                    dve.wait_ge(g_win, c * 16 + 16)
                    dve.wait_ge(g_based, t + 1)
                    V.tensor_scalar(key, win[:, KEY_:KEY_ + 1], tile_base[:, :], None, ALU.subtract).then_inc(g_key, 1)
                    dve.wait_ge(g_key, c + 1)
                    V.tensor_scalar(oh, g_iota[:, :], key, None, ALU.is_equal).then_inc(g_oh, 1)
                    dve.wait_ge(g_picked, c + 2)
                    V.tensor_tensor(sel, pX[:, 0:PICK], sel, ALU.add).then_inc(g_sel, 1)
                    dve.wait_ge(g_sel, c + 2)

                def end(t, rows):
                    V.tensor_scalar(tile_base[:, :], tile_base[:, :], float(P), None, ALU.add).then_inc(g_based, 1)
                    dve.wait_ge(g_x, t * 16 + 16)
                    V.tensor_reduce(g_c[:, :], sel[:, 0:SC].rearrange("p (a f) -> p f a", a=3), AX.X, ALU.add)
                    V.tensor_reduce(g_s3[:, :], sel[:, SC:PICK].rearrange("p (a u) -> p u a", a=3), AX.X, ALU.add).then_inc(g_parts, 1)
                    dve.wait_ge(g_parts, t + 1)
                    for u in range(3):
                        last = V.tensor_scalar(x4[:, u + 1, :], x4[:, 0, :], g_s3[:, u:u + 1], None, ALU.mult)
                    last.then_inc(g_xs, 1)
                    dve.wait_ge(g_turned, t + 2)
                    V.tensor_copy(xnt, pN[:, 0, 0:2 * P].rearrange("p (a b) -> p a b", a=2)).then_inc(g_xnt, 1)
                    dve.wait_ge(g_y, t + 1)
                    V.tensor_tensor(y, pY[:, 0:F], g_c[:, :], ALU.add).then_inc(g_added, 1)
                    dve.wait_ge(g_added, t + 1)
                    V.bn_stats(st, y).then_inc(g_st, 1)
                    dve.wait_ge(g_st, t + 1)
                    dve.sem_inc(g_waited[1], 1)
                    V.bn_aggr(mean_var, st).then_inc(g_mv, 1)
                    dve.wait_ge(g_root, t + 1)
                    V.reciprocal(inv, root).then_inc(g_inv, 1)
                    dve.wait_ge(g_inv, t + 1)
                    V.tensor_scalar(o, y, mean_var[:, 0:1], inv, ALU.subtract, ALU.mult).then_inc(g_o, 1)
                    dve.wait_ge(g_stored, t * 16 + 16)
                    dve.sem_inc(g_waited[1], 1)
                tiles(dve, False, start, chunk, end)

            @block.tensor
            def _(pe):
                pe.sem_inc(g_turned, 1)
                pe.sem_inc(g_picked, 1)

                def chunk(t, c, low, first):
                    pe.wait_ge(g_sel, c + 1)
                    pe.wait_ge(g_oh, c + 1)
                    nc.tensor.matmul(pX[:, 0:PICK], oh, win_b, start=True, stop=True).then_inc(g_picked, 1)

                def end(t, rows):
                    pe.wait_ge(g_xs, t + 1)
                    nc.tensor.transpose(pN[:, 0, 0:P], x4[:, 0:2, :].rearrange("p a b -> p (a b)"), ident[:, :])
                    nc.tensor.transpose(pN[:, 0, P:2 * P], x4[:, 2:4, :].rearrange("p a b -> p (a b)"), ident[:, :]).then_inc(g_turned, 1)
                    pe.wait_ge(g_xnt, t + 1)
                    nc.tensor.matmul(pY[:, 0:F], xnt[:, 0, :], WN1[:, :], start=True, stop=False)
                    nc.tensor.matmul(pY[:, 0:F], xnt[:, 1, :], WN2[:, :], start=False, stop=False)
                    nc.tensor.matmul(pY[:, 0:F], ones_b[:, 0:P], bias3[:, 3, :], start=False, stop=True).then_inc(g_y, 1)
                tiles(pe, False, nothing, chunk, end)

            @block.scalar
            def _(act):
                def end(t, rows):
                    act.wait_ge(g_mv, t + 1)
                    act.sem_inc(g_waited[2], 1)
                    nc.scalar.activation(root, mean_var[:, 1:2], ACT.Sqrt, bias=eps_c[:, :]).then_inc(g_root, 1)
                flag = act.value_load(flag_i[0:1, 0:1], min_val=0, max_val=2 * TA * TB)
                with act.If(flag > 0):
                    with act.Fori(0, TILES) as t:
                        end(t, P)


_INS = ["x", "src", "dst", "edge_attr_64", "L0_gnn_W_e", "L0_gnn_b_e", "L0_gnn_W_pre", "L0_gnn_b_pre",
        "L0_gnn_W_post", "L0_gnn_b_post", "L0_gnn_W_lin", "L0_gnn_b_lin"]


def kernel(**inputs):
    import numpy as _np
    import concourse.bacc as _bacc
    from concourse import mybir as _mybir
    from concourse.bass_utils import run_bass_kernel_spmd as _run

    nc = _bacc.Bacc("TRN2", target_bir_lowering=False, num_devices=1)
    arrays, args = {}, []
    for name in _INS:
        a = _np.ascontiguousarray(inputs[name])
        arrays[f"in_{name}"] = a
        args.append(nc.dram_tensor(f"in_{name}", a.shape, _mybir.dt.from_np(a.dtype), kind="ExternalInput").ap())
    shape = inputs["x"].shape
    out = nc.dram_tensor("out_0", shape, _mybir.dt.float32, kind="ExternalOutput").ap()
    build(nc, *args, out)
    return _run(nc, [arrays], core_ids=[0]).results[0]["out_0"]
```

```python
from contextlib import ExitStack

import numpy as np

import concourse.bass as bass
from concourse import mybir

P = 128
F = 64
K = 4
G = P * K
SLOTS = 4
KEY_ = 3 * F // 2 + 5
ROW = KEY_ + 1
SC = 3 * F
PICK = SC + 9
WIN = 2 * P
READY = 3
EPS = 1e-5
BIG = 1.5e38
LN2 = float(np.log(2.0))
TA, TB = 25, 16

LAG_Q, LAG_MEAN, LAG_VAR, LAG_STD, LAG_TT, LAG_STORE = 1, 2, 3, 4, 5, 6
LAG_WIN = LAG_STORE + READY
LAG_OH, LAG_XS, LAG_Y, LAG_SUM, LAG_NORM, LAG_OUT = (LAG_WIN + 1, LAG_WIN + 2, LAG_WIN + 3, LAG_WIN + 4,
                                                     LAG_WIN + 5, LAG_WIN + 6)
HIST = 2
AHEAD = 2


class Turn:

    def __init__(self, rnd, slot, ago=0, value=None):
        self.rnd, self.slot, self.ago, self.value = rnd, slot, ago, value

    def back(self, d):
        k, slot = divmod(self.slot - d, SLOTS)
        return Turn(self.rnd, slot, self.ago - k, self.value)

    @property
    def number(self):
        return (self.rnd - self.ago) * SLOTS + self.slot

    def count(self, each):
        if self.value is not None:
            return self.value(each, (1 - self.ago) * each)
        return (self.rnd - self.ago + 1) * each

    def total(self):
        if self.value is not None:
            return self.value(SLOTS, self.slot + 1 - self.ago * SLOTS)
        return self.number + 1

    def within(self, n):
        return self.value is not None or 0 <= self.number < n


def after(eng, signal, turn, each=1):
    v = turn.count(each) if isinstance(signal, list) else turn.total()
    if not isinstance(v, int) or v > 0:
        eng.wait_ge(signal[turn.slot] if isinstance(signal, list) else signal, v)


def registers(eng, r, ahead=()):
    known = {}

    def value(each, more):
        if (each, more) not in known:
            known[each, more] = eng.snap(r * each + more)
        return known[each, more]

    for key in ahead:
        value(*key)
    return value


def run(eng, first_full, last_full, total, step, ahead=()):
    for i in range(first_full):
        step(Turn(i // SLOTS, i % SLOTS))
    with eng.Fori(first_full // SLOTS, last_full // SLOTS) as r:
        value = registers(eng, r, ahead)
        for u in range(SLOTS):
            step(Turn(r, u, 0, value))
    for i in range(last_full, total):
        step(Turn(i // SLOTS, i % SLOTS))


def build(nc, x, src, dst, attr, W_e, b_e, W_pre, b_pre, W_post, b_post, W_lin, b_lin, out):
    f32, bf16, i32 = mybir.dt.float32, mybir.dt.bfloat16, mybir.dt.int32
    ALU, ACT, AX = mybir.AluOpType, mybir.ActivationFunctionType, mybir.AxisListType
    N, E = x.shape[0], src.shape[0]
    NG = -(-max(N, E) // G)
    EP = NG * G
    L = EP // P
    E_TAIL = (E - (NG - 1) * G) // K
    LAST_TILES, LAST_ROWS = divmod(N - (NG - 1) * G, P)
    TOTAL = NG + LAG_OUT
    FULL0, FULL1 = 20, (NG - 2 - AHEAD) // SLOTS * SLOTS

    ctx = ExitStack()
    with ctx:
        def sb(name, shape, dt=f32):
            return ctx.enter_context(nc.sbuf_tensor(name, shape, dt))

        def sem(name):
            return ctx.enter_context(nc.semaphore(name))

        def slot_sems(name):
            return [sem(f"{name}{s}") for s in range(SLOTS)]

        def slots(name, shape, dt=f32):
            return [sb(f"{name}{s}", shape, dt) for s in range(SLOTS)]

        mask_d = nc.dram_tensor("mask_scratch", (EP, 2), f32, kind="Internal").ap()
        esc_d = nc.dram_tensor("edge_scalar_scratch", (EP, 8), f32, kind="Internal").ap()
        rows_d = nc.dram_tensor("row_scratch", (EP + WIN, ROW), f32, kind="Internal").ap()
        lo_d = nc.dram_tensor("window_scratch", (3, TA * TB), i32, kind="Internal").ap()

        ident = sb("ident", [P, P])
        ones = sb("ones", [P, P])
        ones_b = sb("ones_b", [3, G], bf16)
        upper = sb("upper", [TA, TA])
        tile_base_c = sb("tile_base_c", [P, NG, K])
        win_limit = sb("win_limit", [TA, TB])
        WP0 = sb("WP0", [F, F])
        WP0T = sb("WP0T", [F, F])
        WPRE = sb("WPRE", [F, 3, F])
        W11 = sb("W11", [F, P])
        WE = sb("WE", [F, F])
        WET = sb("WET", [F, P])
        WL = sb("WL", [F, F])
        WL_raw = sb("WL_raw", [F, F])
        WL_mean = sb("WL_mean", [F, 1])
        blin_mean = sb("blin_mean", [1, 1])
        blin_raw = sb("blin_raw", [1, F])
        ident_c = sb("ident_c", [F, F])
        be_c = sb("be_c", [F, 1])
        bpost_c = sb("bpost_c", [F, 1])
        bpre_c = sb("bpre_c", [P, 1])
        blin_r = sb("blin_r", [1, F])
        q_bias = sb("q_bias", [P, 1])
        RF = sb("RF", [P, 3, F])
        RM = sb("RM", [P, 3, F])
        QW = sb("QW", [P, P])
        WN1 = sb("WN1", [P, F])
        WN2 = sb("WN2", [P, F])
        std0 = sb("std0", [P, P])
        v0 = sb("v0", [P, F])
        split_in = sb("split_in", [3, 2, F])
        split_hi = sb("split_hi", [3, 2, F], bf16)
        split_r1 = sb("split_r1", [3, 2, F])
        split_mid = sb("split_mid", [3, 2, F], bf16)
        split_r2 = sb("split_r2", [3, 2, F])
        split_lo = sb("split_lo", [3, 2, F], bf16)
        split_acc = sb("split_acc", [3, 2, F])
        bias3 = sb("bias3", [3, 2, F], bf16)
        bv = sb("bv", [P, F])
        eps_c = sb("eps_c", [P, 1])

        dst_i = sb("dst_i", [P, L + 2], i32)
        dst_f = sb("dst_f", [P, L + 2])
        shared_x = sb("shared_x", [P, SLOTS, K * 4 * F])
        prep = shared_x[:, :, :].rearrange("p s n -> p (s n)")[:, 0:10 * L].rearrange("p (a l) -> p a l", a=10)
        edge_no, first, ends, starts, run_max, deg, log_deg, tmp = (prep[:, a, :] for a in range(8))
        ta_i, tb_i = (prep[:, a, :].bitcast(i32) for a in (8, 9))
        masks = sb("masks", [P, L, 2])
        masks_b = masks[:, :, :].bitcast(bf16)
        ta_b = sb("ta_b", [P, L], bf16)
        tb_b = sb("tb_b", [P, L], bf16)
        shared = sb("shared", [P, 2 * SLOTS, K * 2 * P])
        digits = shared[:, :, :].rearrange("p s n -> p (s n)").bitcast(bf16)
        oh_a = digits[:, 0:TA * L].rearrange("p (a l) -> p a l", a=TA)
        oh_b = digits[:, TA * L:(TA + TB) * L].rearrange("p (i b c) -> p i b c", b=TB, c=8)
        win_all = sb("win_all", [P, SLOTS, K * 2 * ROW])
        esc = win_all[:, :, :].rearrange("p s n -> p (s n)")[:, 0:8 * L].rearrange("p (l c) -> p l c", c=8)
        esc_b = esc.bitcast(bf16)
        carry_row = sb("carry_row", [1, P + 1])
        carry_in = sb("carry_in", [1, P])
        carry = sb("carry", [P, 1])
        log_sum = sb("log_sum", [P, 1])
        avg = sb("avg", [P, 4])
        m8 = sb("m8", [P, 8])
        sel16 = sb("sel16", [P, TB])
        hist = sb("hist", [P, TA, 8])
        hist_r = sb("hist_r", [P, TA])
        cnt = sb("cnt", [TA, 2, TB])
        cnt_sum = sb("cnt_sum", [TA, 2, TB])
        chunks_i = sb("chunks_i", [TA, TB], i32)
        zeros = sb("zeros", [P, TB])
        lo = sb("lo", [TA, TB])
        lo_read = sb("lo_read", [TA, TB])
        chunk0 = sb("chunk0", [TA, TB])
        lo_i = sb("lo_i", [TA, 3, TB], i32)
        flags = sb("flags", [TA, 2, TB])
        flag1 = sb("flag1", [TA, 1])
        flag_i = sb("flag_i", [1, 1], i32)
        lo_row = sb("lo_row", [1, 3, TA * TB], i32)
        pad_rows = sb("pad_rows", [P, 2 * ROW])
        esc_t = sb("esc_t", [P, NG, K, 8])

        idx = slots("idx", [P, K], i32)
        XA = slots("XA", [P, K, P])
        EM = slots("EM", [P, G, 2])
        EMB = [b[:, :, :].bitcast(bf16) for b in EM]
        XT = slots("XT", [P, G])
        QN = sb("QN", [P, G])
        SQ = slots("SQ", [P, G])
        SS = slots("SS", [P, G])
        MM = slots("MM", [P, G])
        MU = slots("MU", [P, G])
        VV = slots("VV", [P, G])
        Z = sb("Z", [P, K, 2, F])
        Z2 = sb("Z2", [P, K, F])
        C = [sb(f"C{s}", [P, K, 2, F]) for s in range(2)]
        CB = [b[:, :, :, :].rearrange("p k a f -> p k (a f)").bitcast(bf16) for b in C]
        R = slots("R", [P, K, ROW])
        RB = [b[:, :, :].bitcast(bf16) for b in R]
        WP = XT[0][:, 0:6 * F].rearrange("p (c f) -> p c f", c=6)
        WPT = [SQ[c][0:F, 0:3 * P].rearrange("p (c f) -> p c f", c=3) for c in range(2)]
        LF, LM = SQ[2][:, 0:P], SQ[2][:, P:2 * P]
        RMp = SQ[2][:, 2 * P:2 * P + 3 * F].rearrange("p (c f) -> p c f", c=3)
        bpost_b, W33 = SQ[3][0:F, 0:P], SQ[3][0:F, P:2 * P]
        WINB = [win_all[:, s, :].rearrange("p (k c) -> p k c", k=K) for s in range(SLOTS)]
        WINH = [w.bitcast(bf16) for w in WINB]
        keyl = slots("keyl", [P, K, 2], bf16)
        OH = [shared[:, s // 2, (s % 2) * G:(s % 2 + 1) * G].bitcast(bf16).rearrange("p (q w n) -> p q w n", q=K, w=2)
              for s in range(SLOTS)]
        node_iota_b = sb("node_iota_b", [P, P], bf16)
        S3 = slots("S3", [P, K, 3])
        X4 = [shared_x[:, s, :].rearrange("p (k u f) -> p k u f", k=K, u=4) for s in range(SLOTS)]
        XNT = [shared[:, SLOTS + s, :].rearrange("p (h q n) -> p h q n", h=2, q=K) for s in range(SLOTS)]
        Y = slots("Y", [P, K, F])
        YSQ = [sb(f"YSQ{s}", [P, K, F]) for s in range(2)]
        ss = slots("ss", [P, K])
        sd = slots("sd", [P, K])
        rsd = slots("rsd", [P, K])
        O = slots("O", [P, K, F])

        pX = ctx.enter_context(nc.psum_tensor("pX", [P, 512], f32))
        pQ = ctx.enter_context(nc.psum_tensor("pQ", [P, 512], f32))
        pT = ctx.enter_context(nc.psum_tensor("pT", [P, 2, 512], f32))
        T = pT[:, :, :].rearrange("p b (k c) -> p (b k) c", k=K // 2)     
        pN = ctx.enter_context(nc.psum_tensor("pN", [P, 2, 512], f32))
        pL = ctx.enter_context(nc.psum_tensor("pL", [P, 512], f32))
        pY = ctx.enter_context(nc.psum_tensor("pY", [P, 512], f32))

        s_dpad, s_dst, s_w, s_pool, s_ident = (sem(n) for n in ("dst_pad", "dst_in", "weights_in", "pool_step", "consts_ready"))
        s_esc_out, s_lo_out, s_prep_in, s_pad_out, s_lo_in = (sem(n) for n in (
            "scalars_stored", "windows_stored", "scalars_in", "pad_rows_stored", "windows_in"))
        (masks_made, scalars_made, windows_made, starts_scanned, carries_scanned, degrees_made, digits_made, tiles_made, logs_summed,
         weights_doubled, turned_copied, folded_copied, biases_split, hist_summed, counts_scanned, prep_done,
         carry_row_done, avg_done, weights_turned, weights_folded, node_weights_folded, hist_done, counts_done, prefix_done, flag_summed, carry_done, logs_done) = (sem(n) for n in (
            "masks_made", "scalars_made", "windows_made", "starts_scanned", "carries_scanned", "degrees_made", "digits_made", "tiles_made", "logs_summed",
            "weights_doubled", "turned_copied", "folded_copied", "biases_split", "hist_summed", "counts_scanned", "prep_done",
            "carry_row_done", "avg_done", "weights_turned", "weights_folded", "node_weights_folded", "hist_done", "counts_done", "prefix_done", "flag_summed", "carry_done", "logs_done"))
        s_d = sem("dve_prep_step")
        gathers_begun, masks_begun = sem("gathers_begun"), sem("masks_begun")

        (idx_in, attr_in, masks_in, gathered, c_stored, win_in, x_in, o_stored) = (slot_sems(n) for n in (
            "idx_in", "attr_in", "masks_in", "gathered", "c_stored", "win_in", "x_in", "o_stored"))
        x_turned, xt_copied, q_done, sq_done, sums_done, maxes_done = (sem(n) for n in (
            "x_turned", "xt_copied", "q_done", "sq_done", "sums_done", "maxes_done"))
        qn_done, mean_done, m2_done, var_done, relu_done, std_done, packed = (sem(n) for n in (
            "qn_done", "mean_done", "m2_done", "var_done", "relu_done", "std_done", "packed"))
        t_done, z_done, z2_done, c_done, rest_done, row_done, key_done, oh_done = (sem(n) for n in (
            "t_done", "z_done", "z2_done", "c_done", "rest_done", "row_done", "key_done", "oh_done"))
        sel_done, s3_done, xs_done, xn_turned, xn_copied = (sem(n) for n in (
            "sel_done", "s3_done", "xs_done", "xn_turned", "xn_copied"))
        y_done, ysq_done, ss_done, sd_done, rsd_done, o_done = (sem(n) for n in (
            "y_done", "ysq_done", "ss_done", "sd_done", "rsd_done", "o_done"))

        tile_base = sb("tile_base", [P, 1])
        g_key1 = sb("g_key1", [P, 1])
        g_row = Z[:, :, :, :].rearrange("p k j f -> p (k j f)")[:, 0:PICK]
        g_c = Z2[:, 0, :]
        g_s3 = sb("g_s3", [P, 3])
        g_iota = sb("g_iota", [P, P])
        g_y1 = Z2[:, 1, :]
        g_stats = sb("g_stats", [P, 6])
        g_mean_var = sb("g_mean_var", [P, 2])
        (g_x, g_win, g_stored, g_based, g_zeroed, g_key, g_oh, g_picked, g_sel, g_xs, g_turned, g_xnt, g_y, g_added,
         g_st, g_mv, g_root, g_inv, g_o) = (sem(f"general_{n}") for n in (
            "x_in", "win_in", "stored", "based", "zeroed", "key", "one_hot", "picked", "summed", "xs", "turned",
            "xnt", "y", "added", "stats", "mean_var", "root", "inverse", "out"))
        g_parts = sem("general_parts_summed")
        g_waited = [sem(f"general_waited{n}") for n in range(3)]

        def dram(ap, offset, pattern):
            return bass.AP(ap.tensor, offset, pattern)

        with nc.Block() as block:
            @block.sync
            def _(sp):
                def first_edge(t):
                    return t.number * G if isinstance(t.number, int) else sp.snap(t.number * G)

                def load_edges(t):
                    g = t.number
                    at = first_edge(t)
                    whole = not isinstance(g, int) or g < NG - 1
                    n = P if whole else E_TAIL
                    after(sp, gathered, t.back(SLOTS), 16 * K)
                    sp.dma_start(idx[t.slot][0:n, :], dram(src, at, [[K, n], [1, K]])).then_inc(idx_in[t.slot], 16)
                    after(sp, x_turned, t.back(SLOTS))
                    sp.dma_start(XA[t.slot][0:n, :, F:P],
                                 dram(attr, g * (G * F), [[K * F, n], [F, K], [1, F]])).then_inc(attr_in[t.slot], 16)

                def load_masks(t):
                    at = first_edge(t)
                    after(sp, mean_done, t.back(SLOTS))
                    after(sp, sums_done, t.back(SLOTS))
                    after(sp, maxes_done, t.back(SLOTS))
                    sp.sem_inc(masks_begun, 1)
                    sp.dma_start(EM[t.slot][:, :, :].rearrange("p e c -> p (e c)"),
                                 dram(mask_d, at * 2, [[0, P], [1, 2 * G]])).then_inc(masks_in[t.slot], 16)

                load_edges(Turn(0, 0))
                sp.wait_ge(s_dpad, 1)
                sp.dma_start(dst_i[1:P - 1, :], dram(dst, L - 1, [[L, P - 2], [1, L + 2]])).then_inc(s_dst, 16)
                sp.dma_start(dst_i[0:1, 1:L + 2], dram(dst, 0, [[0, 1], [1, L + 1]])).then_inc(s_dst, 16)
                last0 = (P - 1) * L - 1
                sp.dma_start(dst_i[P - 1:P, 0:E - last0], dram(dst, last0, [[0, 1], [1, E - last0]])).then_inc(s_dst, 16)
                for to, what in ((WP[:, :, :], dram(W_post, F * F, [[F, P], [P * F, 6], [1, F]])),
                                 (WP0[:, :], W_post[0:F, :]),
                                 (WPRE[:, :, :], dram(W_pre, 0, [[F, F], [F * F, 3], [1, F]])),
                                 (WE[:, :], W_e), (WL_raw[:, :], W_lin),
                                 (be_c[:, :], dram(b_e, 0, [[1, F], [1, 1]])),
                                 (bpost_c[:, :], dram(b_post, 0, [[1, F], [1, 1]])),
                                 (bpre_c[0:F, :], dram(b_pre, 0, [[1, F], [1, 1]])),
                                 (bpre_c[F:P, :], dram(b_pre, 0, [[1, F], [1, 1]])),
                                 (blin_raw[:, :], dram(b_lin, 0, [[0, 1], [1, F]]))):
                    sp.dma_start(to, what).then_inc(s_w, 16)
                for g in range(1, AHEAD + 1):
                    load_edges(Turn(0, g))
                sp.wait_ge(masks_made, 1)
                sp.dma_start(dram(mask_d, 0, [[2 * L, P], [1, 2 * L]]), masks[:, :, :].rearrange("p l c -> p (l c)")).then_inc(s_esc_out, 16)
                sp.wait_ge(s_esc_out, 16)
                load_masks(Turn(0, 0))
                load_masks(Turn(0, 1))
                def tables(i):
                    if i.number == 1:
                        sp.wait_ge(scalars_made, 1)
                        sp.dma_start(dram(esc_d, 0, [[L * 8, P], [1, L * 8]]), esc[:, :, :].rearrange("p l c -> p (l c)")).then_inc(s_esc_out, 16)
                        sp.dma_start(dram(rows_d, EP * ROW, [[2 * ROW, P], [1, 2 * ROW]]), pad_rows[:, :]).then_inc(s_pad_out, 16)
                    if i.number == 2:
                        sp.wait_ge(s_esc_out, 32)
                        sp.dma_start(esc_t[:, :, :, :].rearrange("p g k c -> p g (k c)"),
                                     dram(esc_d, 0, [[8 * K, P], [8 * G, NG], [1, 8 * K]])).then_inc(s_prep_in, 16)
                    if i.number == LAG_WIN - 1:
                        sp.wait_ge(windows_made, 1)
                        sp.dma_start(dram(lo_d, 0, [[TB, TA], [TA * TB, 3], [1, TB]]), lo_i[:, :, :]).then_inc(s_lo_out, 16)
                        sp.wait_ge(s_lo_out, 16)
                        sp.dma_start(lo_row[:, :, :], dram(lo_d, 0, [[0, 1], [TA * TB, 3], [1, TA * TB]])).then_inc(s_lo_in, 16)
                    if i.number == LAG_WIN:
                        sp.wait_ge(s_lo_in, 16)
                        sp.wait_ge(s_pad_out, 16)

                def step(i):
                    t = i.back(-AHEAD - 1)
                    if t.within(NG):
                        load_edges(t)
                    t = i.back(-AHEAD)
                    if t.within(NG):
                        load_masks(t)
                    if i.value is None:
                        tables(i)
                    t = i.back(LAG_WIN)
                    if t.within(NG):
                        _, los = nc.values_load_multi_w_load_instructions(
                            lo_row[0:1, 0, bass.ds(t.number * K, K)], engines=[mybir.EngineType.SP],
                            min_val=0, max_val=EP, skip_runtime_bounds_check_because="clamped on the chip")
                        after(sp, y_done, t.back(SLOTS))
                        newest = i.back(LAG_STORE + 1)
                        if newest.within(NG):
                            after(sp, c_stored, newest, 16)
                        for q in range(K):
                            sp.dma_start(WINB[t.slot][:, q, :],
                                         dram(rows_d, los[q] * ROW, [[2 * ROW, P], [1, 2 * ROW]])).then_inc(win_in[t.slot], 16)
                        after(sp, xn_turned, t.back(SLOTS))
                        n = t.number
                        if not isinstance(n, int) or n < NG - 1:
                            sp.dma_start(X4[t.slot][:, :, 0, :], dram(x, n * (G * F), [[F, P], [P * F, K], [1, F]])).then_inc(x_in[t.slot], 32)
                        else:
                            sp.dma_start(X4[t.slot][:, 0:LAST_TILES, 0, :],
                                         dram(x, n * G * F, [[F, P], [P * F, LAST_TILES], [1, F]])).then_inc(x_in[t.slot], 16)
                            sp.dma_start(X4[t.slot][0:LAST_ROWS, LAST_TILES, 0, :],
                                         dram(x, (n * G + LAST_TILES * P) * F, [[F, LAST_ROWS], [1, F]])).then_inc(x_in[t.slot], 16)
                    t = i.back(LAG_OUT)
                    if t.within(NG):
                        n = t.number
                        after(sp, o_done, t)
                        if not isinstance(n, int) or n < NG - 1:
                            sp.dma_start(dram(out, n * (G * F), [[F, P], [P * F, K], [1, F]]), O[t.slot][:, :, :]).then_inc(o_stored[t.slot], 32)
                        else:
                            sp.dma_start(dram(out, n * G * F, [[F, P], [P * F, LAST_TILES], [1, F]]),
                                         O[t.slot][:, 0:LAST_TILES, :]).then_inc(o_stored[t.slot], 16)
                            sp.dma_start(dram(out, (n * G + LAST_TILES * P) * F, [[F, LAST_ROWS], [1, F]]),
                                         O[t.slot][0:LAST_ROWS, LAST_TILES, :]).then_inc(o_stored[t.slot], 16)
                    t = i.back(LAG_STORE)
                    if t.within(NG):
                        after(sp, row_done, t)
                        after(sp, packed, t)
                        sp.dma_start(dram(rows_d, t.number * (G * ROW), [[K * ROW, P], [1, K * ROW]]),
                                     R[t.slot][:, :, :].rearrange("p k c -> p (k c)")).then_inc(c_stored[t.slot], 16)

                run(sp, FULL0, FULL1, TOTAL, step)
                for s in range(SLOTS):
                    sp.wait_ge(o_stored[s], 32 * len(range(s, NG, SLOTS)))

            @block.gpsimd
            def _(pool):
                nc.gpsimd.memset(ident[:, :], 1.0).then_inc(s_pool, 1)
                nc.gpsimd.memset(upper[:, :], 1.0).then_inc(s_pool, 1)
                pool.wait_ge(s_pool, 2)
                nc.gpsimd.affine_select(out=ident[:, :], in_=ident[:, :], compare_op=ALU.is_equal, fill=0.0, base=0,
                                        pattern=[[-1, P]], channel_multiplier=1).then_inc(s_ident, 1)
                nc.gpsimd.affine_select(out=upper[:, :], in_=upper[:, :], compare_op=ALU.is_gt, fill=0.0, base=0,
                                        pattern=[[1, TA]], channel_multiplier=-1).then_inc(s_ident, 1)
                nc.gpsimd.iota(edge_no[:, :], [[1, L]], base=0, channel_multiplier=L,
                               allow_small_or_imprecise_dtypes=True).then_inc(s_ident, 1)
                def gather(t):
                    after(pool, idx_in, t, 16)
                    after(pool, x_turned, t.back(SLOTS))
                    pool.wait_ge(s_ident, 3)
                    pool.sem_inc(gathers_begun, 1)
                    for k in range(K):
                        pool.indirect_dma_start(
                            out=XA[t.slot][:, k, 0:F], out_offset=None, in_=x[:, :],
                            in_offset=bass.IndirectOffsetOnAxis(ap=idx[t.slot][:, k:k + 1], axis=0)).then_inc(gathered[t.slot], 16)

                gather(Turn(0, 0))
                nc.gpsimd.iota(win_limit[:, :].rearrange("p (a b) -> p a b", a=TB // K), [[G, TB // K], [0, K]],
                               base=G * READY - WIN, channel_multiplier=TB // K * G,
                               allow_small_or_imprecise_dtypes=True).then_inc(s_ident, 1)
                nc.gpsimd.iota(g_iota[:, :], [[1, P]], base=0, channel_multiplier=0,
                               allow_small_or_imprecise_dtypes=True).then_inc(s_ident, 1)
                nc.gpsimd.iota(tile_base_c[:, :, :].rearrange("p a b -> p (a b)"), [[P, NG * K]], base=0, channel_multiplier=0,
                               allow_small_or_imprecise_dtypes=True).then_inc(s_ident, 1)
                for g in range(1, SLOTS - 1):
                    gather(Turn(0, g))
                pool.wait_ge(tiles_made, 1)
                for b in range(TB):
                    last = nc.gpsimd.tensor_scalar(oh_b[:, :, b, :], tb_b[:, :].rearrange("p (i c) -> p i c", c=8), float(b), None, ALU.is_equal)
                last.then_inc(digits_made, 1)
                gather(Turn(0, SLOTS - 1))
                with pool.Fori(1, NG // SLOTS) as r:
                    value = registers(pool, r)
                    for u in range(SLOTS):
                        gather(Turn(r, u, 0, value))
                for g in range(NG // SLOTS * SLOTS, NG):
                    gather(Turn(g // SLOTS, g % SLOTS))

            @block.vector
            def _(dve):
                seen = [0]

                def link(ins):
                    seen[0] += 1
                    ins.then_inc(s_d, 1)
                    dve.wait_ge(s_d, seen[0])

                def each(ins):
                    seen[0] += 1
                    ins.then_inc(s_d, 1)

                def mark(event):
                    V.engine_nop().then_inc(event, 1)

                V = nc.vector
                V.memset(dst_i[:, :], -1).then_inc(s_dpad, 1)
                each(V.memset(ones[:, :], 1.0))
                each(V.memset(ones_b[:, :], 1.0))
                each(V.memset(zeros[:, :], 0.0))
                each(V.memset(eps_c[:, :], EPS))
                each(V.memset(std0[0:F, :], 0.0))
                each(V.memset(std0[F:P, :], float(np.sqrt(np.float32(EPS)))))
                each(V.memset(pad_rows[:, :], -1.0))
                each(V.memset(carry_row[:, 0:1], 0.0))
                each(V.memset(SS[SLOTS - 1][:, G - 1:G], 0.0))
                each(V.memset(MM[SLOTS - 1][:, G - 1:G], 0.0))
                each(V.memset(esc_b[:, :, 1:2], 1.0))
                each(V.memset(esc_b[:, :, 4:5], 0.0))
                each(V.memset(esc_b[:, :, 7:8], 0.0))
                each(V.memset(esc_b[:, :, 9:10], 0.0))
                dve.wait_ge(s_ident, 3)
                each(V.tensor_reduce(m8[:, :], ident[:, :].rearrange("p (b c) -> p c b", c=8), AX.X, ALU.add))
                each(V.tensor_reduce(sel16[:, :], ident[:, :].rearrange("p (b c) -> p b c", c=8), AX.X, ALU.add))
                dve.wait_ge(s_dst, 48)
                link(V.tensor_copy(dst_f[:, :], dst_i[:, :]))
                link(V.tensor_tensor(first[:, :], dst_f[:, 1:L + 1], dst_f[:, 0:L], ALU.not_equal))
                each(V.tensor_scalar(masks_b[:, :, 2], first[:, :], -1.0, 1.0, ALU.mult, ALU.add))
                each(V.tensor_scalar(masks_b[:, :, 3], first[:, :], -2 * BIG, BIG, ALU.mult, ALU.add))
                link(V.tensor_tensor(starts[:, :], first[:, :], edge_no[:, :], ALU.mult))
                link(V.tensor_tensor_scan(run_max[:, :], starts[:, :], starts[:, :], 0.0, ALU.max, ALU.max))
                mark(starts_scanned)
                link(V.tensor_tensor(ends[:, :], dst_f[:, 1:L + 1], dst_f[:, 2:L + 2], ALU.not_equal))
                link(V.scalar_tensor_tensor(tmp[:, :], dst_f[:, 1:L + 1], 1.0, ends[:, :], ALU.add, ALU.mult))
                link(V.tensor_scalar(esc[:, :, 5], tmp[:, :], 1.0, None, ALU.subtract))
                dve.wait_ge(s_w, 16 * 10)
                link(V.reduce_sum(WL_mean[:, :], WL_raw[:, :], axis=AX.X))
                link(V.tensor_scalar(WL_mean[:, :], WL_mean[:, :], 1.0 / F, None, ALU.mult))
                each(V.tensor_scalar(WL[:, :], WL_raw[:, :], WL_mean[:, :], None, ALU.subtract))
                link(V.reduce_sum(blin_mean[:, :], blin_raw[:, :], axis=AX.X))
                link(V.tensor_scalar(blin_mean[:, :], blin_mean[:, :], 1.0 / F, None, ALU.mult))
                each(V.tensor_scalar(blin_r[:, :], blin_raw[:, :], blin_mean[:, :], None, ALU.subtract))
                each(V.tensor_scalar(ident_c[:, :], ident[0:F, 0:F], 1.0 / F, None, ALU.subtract))
                each(V.tensor_copy(W11[:, 0:F], WPRE[:, 0, :]))
                each(V.tensor_copy(W11[:, F:P], WPRE[:, 0, :]))
                each(V.tensor_copy(W33[:, 0:F], WPRE[:, 2, :]))
                each(V.tensor_copy(W33[:, F:P], WPRE[:, 2, :]))
                link(V.tensor_copy(bpost_b[:, :], bpost_c[:, :].broadcast_to([F, P])))
                mark(weights_doubled)
                each(V.tensor_scalar(ta_i[:, :], dst_i[:, 1:L + 1], 11, None, ALU.arith_shift_right))
                link(V.tensor_scalar(tb_i[:, :], dst_i[:, 1:L + 1], 7, TB - 1, ALU.arith_shift_right, ALU.bitwise_and))
                each(V.tensor_copy(ta_b[:, :], ta_i[:, :]))
                link(V.tensor_copy(tb_b[:, :], tb_i[:, :]))
                mark(tiles_made)
                dve.wait_ge(carry_row_done, 1)
                link(V.tensor_copy(carry_in[:, :], pX[0:1, 0:P]))
                link(V.tensor_tensor_scan(carry_row[:, 1:P + 1], carry_in[:, :], carry_in[:, :], 0.0, ALU.max, ALU.max))
                mark(carries_scanned)
                dve.wait_ge(carry_done, 1)
                link(V.tensor_copy(carry[:, :], pX[:, 0:1]))
                link(V.tensor_scalar(starts[:, :], run_max[:, :], carry[:, :], None, ALU.max))
                link(V.scalar_tensor_tensor(deg[:, :], edge_no[:, :], 1.0, starts[:, :], ALU.add, ALU.subtract))
                mark(degrees_made)
                dve.wait_ge(weights_turned, 1)
                each(V.tensor_copy(WPT[0], pT[0:F, 0, 0:3 * P].rearrange("p (a b) -> p a b", a=3)))
                each(V.tensor_copy(WPT[1], pT[0:F, 1, 0:3 * P].rearrange("p (a b) -> p a b", a=3)))
                each(V.tensor_copy(WP0T[:, :], pN[0:F, 0, 0:F]))
                for h in range(2):
                    each(V.tensor_copy(WET[:, h * F:h * F + F], pN[0:F, 0, F:2 * F]))
                    link(V.tensor_copy(LM[:, h * F:h * F + F], pN[:, 0, 2 * F:3 * F]))
                link(V.memset(LF[:, :], 0.0))
                link(V.tensor_copy(LF[0:F, :], LM[0:F, :]))
                mark(turned_copied)
                link(V.reciprocal(masks[:, :, 0], deg[:, :]))
                mark(masks_made)
                dve.wait_ge(logs_done, 1)
                link(V.tensor_tensor(tmp[:, :], log_deg[:, :], ends[:, :], ALU.mult))
                link(V.reduce_sum(log_sum[:, :], tmp[:, :], axis=AX.X))
                mark(logs_summed)
                dve.wait_ge(weights_folded, 1)
                for u in range(3):
                    each(V.tensor_copy(RF[:, u, :], pT[:, 0, 2 * u * F:(2 * u + 1) * F]))
                    link(V.tensor_copy(RMp[:, u, :], pT[:, 0, (2 * u + 1) * F:(2 * u + 2) * F]))
                each(V.tensor_copy(RM[0:F, :, :], RMp[0:F, :, :]))
                each(V.tensor_scalar(RM[F:P, :, :], RMp[F:P, :, :], -1.0, None, ALU.mult))
                each(V.tensor_tensor(WN1[0:F, :], pN[0:F, 0, 0:F], ident_c[:, :], ALU.add))
                each(V.tensor_copy(QW[0:F, 0:F], WPRE[:, 1, :]))
                each(V.tensor_scalar(QW[0:F, F:P], WPRE[:, 1, :], -1.0, None, ALU.mult))
                each(V.tensor_copy(QW[F:P, 0:F], pN[F:P, 0, F:2 * F]))
                each(V.tensor_scalar(QW[F:P, F:P], pN[F:P, 0, F:2 * F], -1.0, None, ALU.mult))
                link(V.tensor_tensor(q_bias[:, :], pN[:, 0, 2 * F:2 * F + 1], bpre_c[:, :], ALU.add))
                link(V.tensor_scalar(q_bias[F:P, :], q_bias[F:P, :], -1.0, None, ALU.mult))
                mark(folded_copied)
                dve.wait_ge(avg_done, 1)
                link(V.tensor_scalar(avg[:, 0:1], pX[:, 0:1], 1.0 / N, None, ALU.mult))
                link(V.reciprocal(avg[:, 1:2], avg[:, 0:1]))
                link(V.tensor_scalar(avg[:, 2:3], avg[:, 1:2], LN2, None, ALU.mult))
                link(V.tensor_scalar(avg[:, 3:4], avg[:, 0:1], 1.0 / LN2, None, ALU.mult))
                link(V.reciprocal(tmp[:, :], log_deg[:, :]))
                dve.wait_ge(node_weights_folded, 1)
                each(V.tensor_copy(WN1[F:P, :], pT[F:P, 0, F:2 * F]))
                each(V.tensor_copy(WN2[0:F, :], pT[0:F, 0, 0:F]))
                each(V.tensor_copy(WN2[F:P, :], pT[F:P, 0, 2 * F:3 * F]))
                each(V.tensor_scalar(v0[:, :], pN[:, 0, F:2 * F], avg[:, 2:3], None, ALU.mult))
                link(V.tensor_scalar(bv[:, :], pN[:, 0, 2 * F:3 * F], avg[:, 3:4], None, ALU.mult))
                link(V.tensor_tensor(v0[:, :], v0[:, :], bv[:, :], ALU.add))
                link(V.tensor_tensor(v0[:, :], v0[:, :], pN[:, 0, 0:F], ALU.add))
                link(V.tensor_scalar(split_in[:, 0, :], v0[0:3, :], -1.0, None, ALU.mult))
                link(V.tensor_tensor(split_in[:, 1, :], pN[0:3, 0, 3 * F:4 * F], v0[0:3, :], ALU.add))
                link(V.tensor_copy(split_hi[:, :, :], split_in[:, :, :]))
                link(V.tensor_tensor(split_r1[:, :, :], split_in[:, :, :], split_hi[:, :, :], ALU.subtract))
                link(V.tensor_copy(split_mid[:, :, :], split_r1[:, :, :]))
                link(V.tensor_tensor(split_r2[:, :, :], split_r1[:, :, :], split_mid[:, :, :], ALU.subtract))
                link(V.tensor_scalar(split_acc[:, :, :], split_hi[:, :, :], ident[0:3, 0:1], None, ALU.mult))
                link(V.scalar_tensor_tensor(split_in[:, :, :], split_mid[:, :, :], ident[0:3, 1:2], split_acc[:, :, :], ALU.mult, ALU.add))
                link(V.tensor_copy(split_lo[:, :, :], split_r2[:, :, :]))
                link(V.scalar_tensor_tensor(bias3[:, :, :], split_lo[:, :, :], ident[0:3, 2:3], split_in[:, :, :], ALU.mult, ALU.add))
                mark(biases_split)
                mark(prep_done)

                def windows(i):
                    n = i.number
                    if n == 0:
                        each(V.tensor_scalar(esc[:, :, 6], log_deg[:, :], avg[:, 1:2], None, ALU.mult))
                        link(V.tensor_scalar(esc[:, :, 7], tmp[:, :], avg[:, 0:1], None, ALU.mult))
                        tmp_b = tmp.bitcast(bf16)
                        for u, w in ((0, 6), (2, 7)):
                            each(V.tensor_copy(esc_b[:, :, u], esc_b[:, :, 2 * w + 1]))
                            link(V.tensor_tensor(tmp[:, :], esc[:, :, w], esc_b[:, :, 2 * w + 1], ALU.subtract))
                            each(V.tensor_copy(esc_b[:, :, 3 + u], tmp_b[:, 1::2]))
                            link(V.tensor_tensor(esc_b[:, :, 6 + u], tmp[:, :], tmp_b[:, 1::2], ALU.subtract))
                        mark(scalars_made)
                    if n == LAG_TT - 1:
                        dve.wait_ge(s_prep_in, 16)
                    if n == 1:
                        for a in range(TA):
                            each(V.tensor_scalar(oh_a[:, a, :], ta_b[:, :], float(a), None, ALU.is_equal))
                        dve.wait_ge(s_d, seen[0])
                        mark(digits_made)
                        dve.wait_ge(s_ident, 6)
                        each(V.tensor_copy(node_iota_b[:, :], g_iota[:, :]))
                    if n == HIST + 1:
                        dve.wait_ge(hist_done, 1)
                        link(V.tensor_tensor(hist[:, :, :], pL[:, 0:TA * 8].rearrange("p (a c) -> p a c", c=8),
                                             m8[:, :].unsqueeze(1).broadcast_to([P, TA, 8]), ALU.mult))
                        link(V.tensor_reduce(hist_r[:, :], hist[:, :, :], AX.X, ALU.add))
                        mark(hist_summed)
                    if n == HIST + 2:
                        dve.wait_ge(counts_done, 1)
                        link(V.tensor_copy(cnt[:, 0, :], pL[0:TA, 0:TB]))
                        link(V.tensor_scalar(lo[:, :], cnt[:, 0, :], float(P - 1), None, ALU.add))
                        link(V.tensor_copy(chunks_i[:, :], lo[:, :]))
                        link(V.tensor_scalar(chunks_i[:, :], chunks_i[:, :], 7, None, ALU.arith_shift_right))
                        link(V.tensor_copy(cnt[:, 1, :], chunks_i[:, :]))
                        link(V.tensor_scalar(cnt[:, 1, :], cnt[:, 1, :], 1.0, None, ALU.max))
                        for a in range(2):
                            link(V.tensor_tensor_scan(cnt_sum[:, a, :], zeros[0:TA, :], cnt[:, a, :], 0.0, ALU.add, ALU.add))
                        mark(counts_scanned)
                    if n == HIST + 3:
                        dve.wait_ge(prefix_done, 1)
                        dve.wait_ge(s_ident, 6)
                        link(V.tensor_tensor(lo[:, :], cnt_sum[:, 0, :], cnt[:, 0, :], ALU.subtract))
                        link(V.tensor_scalar(lo[:, :], lo[:, :], pL[0:TA, 0:1], None, ALU.add))
                        link(V.tensor_tensor(chunk0[:, :], cnt_sum[:, 1, :], cnt[:, 1, :], ALU.subtract))
                        link(V.tensor_scalar(chunk0[:, :], chunk0[:, :], pL[0:TA, 1:2], None, ALU.add))
                        link(V.tensor_scalar(lo_read[:, :], win_limit[:, :], float(EP), None, ALU.min))
                        link(V.tensor_tensor(lo_read[:, :], lo_read[:, :], lo[:, :], ALU.min))
                        link(V.tensor_copy(lo_i[:, 0, :], lo_read[:, :]))
                        link(V.tensor_copy(lo_i[:, 1, :], lo[:, :]))
                        link(V.tensor_copy(lo_i[:, 2, :], chunk0[:, :]))
                        link(V.tensor_tensor(flags[:, 0, :], lo_read[:, :], lo[:, :], ALU.not_equal))
                        link(V.tensor_scalar(flags[:, 1, :], cnt[:, 0, :], float(WIN), None, ALU.is_gt))
                        link(V.tensor_reduce(flag1[:, :], flags[:, :, :], AX.XY, ALU.add))
                        mark(windows_made)
                    if n == HIST + 4:
                        dve.wait_ge(flag_summed, 1)
                        link(V.tensor_copy(flag_i[:, :], pL[0:1, 0:1]))

                def step(i):
                    t = i.back(LAG_OH)
                    if t.within(NG):
                        j = t.number
                        after(dve, win_in, t, 16 * K)
                        after(dve, oh_done, t.back(SLOTS))
                        V.tensor_tensor(keyl[t.slot][:, :, :], WINB[t.slot][:, :, KEY_::ROW],
                                        tile_base_c[:, bass.ds(j, 1), :].rearrange("p o k -> p (o k)").unsqueeze(2).broadcast_to([P, K, 2]),
                                        ALU.subtract).then_inc(key_done, 1)
                    t = i.back(LAG_SUM)
                    if t.within(NG):
                        after(dve, ysq_done, t)
                        after(dve, sd_done, t.back(SLOTS))
                        V.tensor_reduce(ss[t.slot][:, :], YSQ[t.slot % 2][:, :, :], AX.X, ALU.add).then_inc(ss_done, 1)
                    t = i.back(LAG_MEAN)
                    if t.within(NG):
                        after(dve, sums_done, t)
                        after(dve, t_done, t.back(SLOTS))
                        V.tensor_tensor(MU[t.slot][:, :], SS[t.slot][:, :], EM[t.slot][:, :, 0], ALU.mult).then_inc(mean_done, 1)
                    t = i.back(LAG_OH)
                    if t.within(NG):
                        after(dve, key_done, t)
                        after(dve, y_done, t.back(SLOTS))
                        V.tensor_tensor(OH[t.slot], node_iota_b[:, :].unsqueeze(1).broadcast_to([P, 2 * K, P]).rearrange("p (q w) n -> p q w n", q=K),
                                        keyl[t.slot][:, :, :].unsqueeze(3).broadcast_to([P, K, 2, P]),
                                        ALU.is_equal).then_inc(oh_done, 1)
                    t = i.back(LAG_NORM)
                    if t.within(NG):
                        after(dve, sd_done, t)
                        after(dve, o_done, t.back(SLOTS))
                        V.reciprocal(rsd[t.slot][:, :], sd[t.slot][:, :]).then_inc(rsd_done, 1)
                    t = i.back(LAG_VAR)
                    if t.within(NG):
                        after(dve, m2_done, t)
                        V.tensor_tensor(VV[t.slot][F:P, :], MU[t.slot][F:P, :], VV[t.slot][F:P, :], ALU.subtract).then_inc(var_done, 1)
                    c = i.back(LAG_TT)
                    if c.within(NG):
                        g = c.number
                        after(dve, t_done, c)
                        V.tensor_tensor(Z[:, :, :, :], T[:, :, F:3 * F].rearrange("p k (j f) -> p k j f", j=2),
                                        esc_t[:, bass.ds(g, 1), :, 6:8].rearrange("p o k c -> p (o k) c").unsqueeze(3).broadcast_to([P, K, 2, F]),
                                        ALU.mult).then_inc(z_done, 1)
                    if c.within(NG):
                        after(dve, c_stored, c.back(SLOTS), 16)
                        V.tensor_copy(R[c.slot][:, :, SC // 2:ROW], esc_t[:, bass.ds(g, 1), :, 0:6].rearrange("p o k c -> p (o k) c"))
                    if c.within(NG):
                        after(dve, z_done, c)
                        V.tensor_tensor(Z2[:, :, :], T[:, :, 0:F], Z[:, :, 0, :], ALU.add).then_inc(z2_done, 1)
                    t = i.back(LAG_Q)
                    if t.within(NG):
                        after(dve, masks_in, t, 16)
                        after(dve, qn_done, t)
                        after(dve, t_done, t.back(SLOTS))
                        before = t.back(1)
                        after(dve, maxes_done, before)
                        V.tensor_tensor_scan(MM[t.slot][:, :], EMB[t.slot][:, :, 3], QN[:, :], MM[before.slot][:, G - 1:G],
                                             ALU.min, ALU.max).then_inc(maxes_done, 1)
                    if c.within(NG):
                        after(dve, z2_done, c)
                        after(dve, packed, c.back(2))
                        V.tensor_tensor(C[c.slot % 2][:, :, 0, :], Z[:, :, 1, :], Z2[:, :, :], ALU.add).then_inc(c_done, 1)
                    if t.within(NG):
                        after(dve, sq_done, t)
                        after(dve, sums_done, before)
                        V.tensor_tensor_scan(SS[t.slot][:, :], EMB[t.slot][:, :, 2], SQ[t.slot][:, :], SS[before.slot][:, G - 1:G],
                                             ALU.mult, ALU.add).then_inc(sums_done, 1)
                    if c.within(NG):
                        after(dve, c_done, c)
                        V.tensor_tensor(C[c.slot % 2][:, :, 1, :], C[c.slot % 2][:, :, 0, :], CB[c.slot % 2][:, :, 1:2 * F:2], ALU.subtract).then_inc(rest_done, 1)
                    t = i.back(LAG_XS)
                    if t.within(NG):
                        after(dve, sel_done, t)
                        after(dve, xs_done, t.back(SLOTS))
                        V.tensor_reduce(S3[t.slot][:, :, :], pL[:, 0:9 * K].rearrange("p (q a u) -> p q u a", q=K, a=3),
                                        AX.X, ALU.add).then_inc(s3_done, 1)
                    if c.within(NG):
                        after(dve, rest_done, c)
                        V.tensor_tensor(RB[c.slot][:, :, 2 * F:3 * F], C[c.slot % 2][:, :, 1, :], CB[c.slot % 2][:, :, 2 * F + 1:4 * F:2],
                                        ALU.subtract).then_inc(row_done, 1)
                    x = i.back(LAG_XS)
                    if x.within(NG):
                        after(dve, x_in, x, 32)
                        after(dve, s3_done, x)
                        V.tensor_tensor(X4[x.slot][:, :, 1:4, :], X4[x.slot][:, :, 0, :].unsqueeze(2).broadcast_to([P, K, 3, F]),
                                        S3[x.slot][:, :, :].unsqueeze(3).broadcast_to([P, K, 3, F]), ALU.mult).then_inc(xs_done, 1)

                    if i.value is None:
                        windows(i)

                run(dve, FULL0, FULL1, TOTAL, step)

            @block.tensor
            def _(pe):
                mm, tr = nc.tensor.matmul, nc.tensor.transpose
                pe.wait_ge(s_ident, 3)
                pe.wait_ge(starts_scanned, 1)
                tr(pX[0:1, 0:P], run_max[:, L - 1:L], ident[:, :]).then_inc(carry_row_done, 1)
                pe.wait_ge(s_w, 16 * 10)
                pe.wait_ge(weights_doubled, 1)
                for c in range(6):
                    tr(pT[0:F, c // 3, (c % 3) * P:(c % 3 + 1) * P], WP[:, c, :], ident[:, :])
                tr(pN[0:F, 0, 0:F], WP0[:, :], ident[0:F, 0:F])
                tr(pN[0:F, 0, F:2 * F], WE[:, :], ident[0:F, 0:F])
                tr(pN[:, 0, 2 * F:3 * F], W11[:, :], ident[0:F, 0:F]).then_inc(weights_turned, 1)
                pe.wait_ge(carries_scanned, 1)
                tr(pX[:, 0:1], carry_row[0:1, 0:P], ident[0:1, 0:1]).then_inc(carry_done, 1)
                pe.wait_ge(turned_copied, 1)
                for c in range(6):
                    mm(pT[:, 0, c * F:(c + 1) * F], WPT[c // 3][:, c % 3, :], WL[:, :], start=True, stop=True)
                mm(pN[0:F, 0, 0:F], WP0T[:, :], WL[:, :], start=True, stop=True)
                mm(pN[:, 0, F:2 * F], WET[:, :], WPRE[:, 2, :], start=True, stop=True)
                mm(pN[:, 0, 2 * F:2 * F + 1], W33, be_c[:, :], start=True, stop=True).then_inc(weights_folded, 1)
                pe.wait_ge(logs_summed, 1)
                mm(pX[:, 0:1], ones[:, :], log_sum[:, :], start=True, stop=True).then_inc(avg_done, 1)
                pe.wait_ge(folded_copied, 1)
                mm(pT[:, 0, 0:3 * F], LF[:, :], RF[:, :, :].rearrange("p a b -> p (a b)"), start=True, stop=False)
                mm(pT[:, 0, 0:3 * F], LM[:, :], RMp[:, :, :].rearrange("p a b -> p (a b)"), start=False, stop=True)
                mm(pN[:, 0, 0:3 * F], std0[:, :], RF[:, :, :].rearrange("p a b -> p (a b)"), start=True, stop=True)
                mm(pN[:, 0, 3 * F:4 * F], bpost_b[:, :], WL[:, :], start=True, stop=False)
                mm(pN[:, 0, 3 * F:4 * F], ones[0:1, :], blin_r[:, :], start=False, stop=True).then_inc(node_weights_folded, 1)
                pe.wait_ge(prep_done, 1)

                def windows(i):
                    if i.number == HIST:
                        pe.wait_ge(digits_made, 2)
                        for c in range(L // 8):
                            last = mm(pL[:, 0:TA * 8], oh_b[:, c, :, :].rearrange("p b c -> p (b c)"), oh_a[:, :, 8 * c:8 * c + 8],
                                      start=(c == 0), stop=(c == L // 8 - 1))
                        last.then_inc(hist_done, 1)
                    if i.number == HIST + 2:
                        pe.wait_ge(hist_summed, 1)
                        mm(pL[0:TA, 0:TB], hist_r[:, :], sel16[:, :], start=True, stop=True).then_inc(counts_done, 1)
                    if i.number == HIST + 3:
                        pe.wait_ge(counts_scanned, 1)
                        mm(pL[0:TA, 0:2], upper[:, :], cnt_sum[:, :, TB - 1], start=True, stop=True).then_inc(prefix_done, 1)
                    if i.number == HIST + 4:
                        pe.wait_ge(windows_made, 1)
                        mm(pL[0:1, 0:1], flag1[:, :], ones[0:TA, 0:1], start=True, stop=True).then_inc(flag_summed, 1)

                def step(i):
                    t = i.back(LAG_TT)
                    if t.within(NG):
                        after(pe, std_done, t)
                        after(pe, maxes_done, t)
                        after(pe, z2_done, t.back(1))
                        for k in range(K):
                            o = T[:, k, 0:3 * F]
                            mm(o, MM[t.slot][:, k::K], RM[:, :, :].rearrange("p a b -> p (a b)"),
                               start=(k % (K // 2) == 0), stop=False)
                            mm(o, MU[t.slot][:, k::K], RF[:, :, :].rearrange("p a b -> p (a b)"), start=False, stop=False)
                    t = i
                    if t.within(NG):
                        after(pe, gathered, t, 16 * K)
                        after(pe, attr_in, t, 16)
                        after(pe, xt_copied, t.back(1))
                        for k in range(K):
                            last = tr(pX[:, k * P:(k + 1) * P], XA[t.slot][:, k, :], ident[:, :])
                        last.then_inc(x_turned, 1)
                    t = i.back(LAG_Y)
                    if t.within(NG):
                        after(pe, xs_done, t)
                        after(pe, xn_copied, t.back(1))
                        for h in range(2):
                            for q in range(K):
                                last = tr(pN[:, h, q * P:(q + 1) * P], X4[t.slot][:, q, 2 * h:2 * h + 2, :].rearrange("p a b -> p (a b)"), ident[:, :])
                        last.then_inc(xn_turned, 1)
                    t = i.back(LAG_Q)
                    if t.within(NG):
                        after(pe, xt_copied, t)
                        after(pe, sq_done, t.back(1))
                        mm(pQ[:, :], QW[:, :], XT[t.slot][:, :], start=True, stop=True).then_inc(q_done, 1)
                    t = i.back(LAG_TT)
                    if t.within(NG):
                        for k in range(K):
                            last = mm(T[:, k, 0:F], ones_b[:, 0:P], bias3[:, 0, :], start=False,
                                      stop=(k % (K // 2) == K // 2 - 1))
                        last.then_inc(t_done, 1)
                    t = i.back(LAG_Y)
                    if t.within(NG):
                        after(pe, ysq_done, t.back(1))
                        for q in range(K):
                            o = pY[:, q * F:(q + 1) * F]
                            mm(o, ones_b[:, 0:P], bias3[:, 1, :], start=(q == 0), stop=False)
                            for w in range(2):
                                for a in range(3):
                                    h = (w * ROW) * 2 + a * F
                                    mm(o, OH[t.slot][:, q, w, :], WINH[t.slot][:, q, h:h + F], start=False, stop=False)
                    t = i.back(LAG_XS)
                    if t.within(NG):
                        after(pe, oh_done, t)
                        after(pe, s3_done, t.back(1))
                        for q in range(K):
                            for w in range(2):
                                h = (w * ROW) * 2 + SC
                                last = mm(pL[:, q * 9:(q + 1) * 9], OH[t.slot][:, q, w, :], WINH[t.slot][:, q, h:h + 9],
                                          start=(w == 0), stop=(w == 1))
                        last.then_inc(sel_done, 1)
                    t = i.back(LAG_Y)
                    if t.within(NG):
                        after(pe, xn_copied, t)
                        for q in range(K):
                            o = pY[:, q * F:(q + 1) * F]
                            mm(o, XNT[t.slot][:, 0, q, :], WN1[:, :], start=False, stop=False)
                            last = mm(o, XNT[t.slot][:, 1, q, :], WN2[:, :], start=False, stop=(q == K - 1))
                        last.then_inc(y_done, 1)

                    if i.value is None:
                        windows(i)

                run(pe, FULL0, FULL1, TOTAL, step)

            @block.scalar
            def _(act):
                A = nc.scalar.activation
                act.wait_ge(degrees_made, 1)
                A(log_deg[:, :], deg[:, :], ACT.Ln, bias=1.0).then_inc(logs_done, 1)
                act.wait_ge(prep_done, 1)

                def own_wait():
                    act.wait_ge(s_ident, 3)

                def step(i):
                    t = i.back(LAG_SUM)
                    if t.within(NG):
                        after(act, ss_done, t.back(2))
                        after(act, o_done, t.back(SLOTS))
                        after(act, y_done, t)
                        own_wait()
                        A(Y[t.slot][:, :, :].rearrange("p a b -> p (a b)"), pY[:, 0:K * F], ACT.Copy)
                        A(YSQ[t.slot % 2][:, :, :].rearrange("p a b -> p (a b)"), pY[:, 0:K * F], ACT.Square).then_inc(ysq_done, 1)
                    t = i.back(LAG_STD)
                    if t.within(NG):
                        after(act, var_done, t)
                        own_wait()
                        A(VV[t.slot][F:P, :], VV[t.slot][F:P, :], ACT.Relu).then_inc(relu_done, 1)
                    t = i.back(LAG_NORM)
                    if t.within(NG):
                        after(act, rsd_done, t.back(SLOTS))
                        after(act, ss_done, t)
                        own_wait()
                        A(sd[t.slot][:, :], ss[t.slot][:, :], ACT.Sqrt, bias=eps_c[:, :], scale=1.0 / F).then_inc(sd_done, 1)
                    t = i.back(LAG_STD)
                    if t.within(NG):
                        after(act, relu_done, t)
                        own_wait()
                        A(MU[t.slot][F:P, :], VV[t.slot][F:P, :], ACT.Sqrt, bias=eps_c[F:P, :]).then_inc(std_done, 1)
                    t = i
                    if t.within(NG):
                        after(act, q_done, t.back(SLOTS))
                        after(act, x_turned, t)
                        own_wait()
                        A(XT[t.slot][:, :].rearrange("f (p k) -> f k p", k=K), pX[:, :].rearrange("f (k p) -> f k p", k=K),
                          ACT.Copy).then_inc(xt_copied, 1)
                    t = i.back(LAG_Y)
                    if t.within(NG):
                        after(act, y_done, t.back(SLOTS))
                        after(act, xn_turned, t)
                        own_wait()
                        A(XNT[t.slot][:, 0, :, :].rearrange("p a b -> p (a b)"), pN[:, 0, :], ACT.Copy)
                        A(XNT[t.slot][:, 1, :, :].rearrange("p a b -> p (a b)"), pN[:, 1, :], ACT.Copy).then_inc(xn_copied, 1)
                    t = i.back(LAG_STORE)
                    if t.within(NG):
                        after(act, c_stored, t.back(SLOTS), 16)
                        after(act, rest_done, t)
                        own_wait()
                        A(RB[t.slot][:, :, 0:2 * F], CB[t.slot % 2][:, :, 1::2], ACT.Copy).then_inc(packed, 1)
                    t = i.back(LAG_Q)
                    if t.within(NG):
                        after(act, sums_done, t.back(SLOTS))
                        after(act, maxes_done, t.back(1))
                        after(act, q_done, t)
                        own_wait()
                        A(QN[:, :], pQ[:, :], ACT.Identity, bias=q_bias[:, :]).then_inc(qn_done, 1)
                        A(SQ[t.slot][0:F, :], pQ[0:F, :], ACT.Identity, bias=q_bias[0:F, :])
                        A(SQ[t.slot][F:P, :], pQ[F:P, :], ACT.Square, bias=q_bias[F:P, :]).then_inc(sq_done, 1)
                    t = i.back(LAG_MEAN)
                    if t.within(NG):
                        after(act, std_done, t.back(SLOTS))
                        after(act, mean_done, t)
                        own_wait()
                        A(VV[t.slot][F:P, :], MU[t.slot][0:F, :], ACT.Square).then_inc(m2_done, 1)
                    t = i.back(LAG_NORM)
                    if t.within(NG):
                        after(act, o_stored, t.back(SLOTS), 32)
                        after(act, rsd_done, t)
                        own_wait()
                        for q in range(K):
                            last = A(O[t.slot][:, q, :], Y[t.slot][:, q, :], ACT.Copy, scale=rsd[t.slot][:, q:q + 1])
                        last.then_inc(o_done, 1)

                run(act, FULL0, FULL1, TOTAL, step)

        TILES = -(-N // P)
        win, win_b, oh, sel = WINB[0][:, 0, 0:ROW], WINH[0][:, 0, 0:PICK], OH[0][:, 0, 0, :], g_row
        x4, xnt = X4[0][:, 0, :, :], XNT[0][:, :, 0, :]
        key, y, st, mean_var, root, inv, o = (g_key1[:, :], g_y1, g_stats[:, :], g_mean_var[:, :],
                                              sd[0][:, 0:1], rsd[0][:, 0:1], O[0][:, 0, :])

        def tiles(eng, needs, start, chunk, end):
            flag = eng.value_load(flag_i[0:1, 0:1], min_val=0, max_val=2 * TA * TB)
            with eng.If(flag > 0):
                def tile(t, rows):
                    first = eng.value_load(lo_row[0:1, 2, bass.ds(t, 1)], min_val=0, max_val=4 * TA * TB)
                    past = eng.value_load(lo_row[0:1, 2, bass.ds(t + 1, 1)], min_val=0, max_val=4 * TA * TB)
                    low = eng.value_load(lo_row[0:1, 1, bass.ds(t, 1)], min_val=0, max_val=E) if needs else None
                    start(t, rows)
                    with eng.Fori(first, past) as c:
                        chunk(t, c, low, first)
                    end(t, rows)
                with eng.Fori(0, TILES - 1) as t:
                    tile(t, P)
                tile(TILES - 1, N - (TILES - 1) * P)

        nothing = lambda *_: None

        with nc.Block() as block:
            @block.sync
            def _(sp):
                def start(t, rows):
                    sp.wait_ge(g_turned, t + 1)
                    sp.sem_inc(g_waited[0], 1)
                    sp.dma_start(x4[0:rows, 0, :], dram(x, t * (P * F), [[F, rows], [1, F]])).then_inc(g_x, 16)

                def chunk(t, c, low, first):
                    sp.wait_ge(g_picked, c + 1)
                    sp.sem_inc(g_waited[0], 1)
                    sp.dma_start(win, dram(rows_d, (low + (c - first) * P) * ROW, [[ROW, P], [1, ROW]])).then_inc(g_win, 16)

                def end(t, rows):
                    sp.wait_ge(g_o, t + 1)
                    sp.sem_inc(g_waited[0], 1)
                    sp.dma_start(dram(out, t * (P * F), [[F, rows], [1, F]]), o[0:rows, :]).then_inc(g_stored, 16)
                    sp.wait_ge(g_stored, t * 16 + 16)
                    sp.sem_inc(g_waited[0], 1)
                tiles(sp, True, start, chunk, end)

            @block.vector
            def _(dve):
                V = nc.vector
                dve.sem_inc(g_sel, 1)
                V.memset(tile_base[:, :], 0.0).then_inc(g_based, 1)

                def start(t, rows):
                    V.memset(sel, 0.0).then_inc(g_zeroed, 1)
                    dve.wait_ge(g_zeroed, t + 1)
                    dve.sem_inc(g_waited[1], 1)

                def chunk(t, c, low, first):
                    dve.wait_ge(g_win, c * 16 + 16)
                    dve.wait_ge(g_based, t + 1)
                    V.tensor_scalar(key, win[:, KEY_:KEY_ + 1], tile_base[:, :], None, ALU.subtract).then_inc(g_key, 1)
                    dve.wait_ge(g_key, c + 1)
                    V.tensor_scalar(oh, g_iota[:, :], key, None, ALU.is_equal).then_inc(g_oh, 1)
                    dve.wait_ge(g_picked, c + 2)
                    V.tensor_tensor(sel, pX[:, 0:PICK], sel, ALU.add).then_inc(g_sel, 1)
                    dve.wait_ge(g_sel, c + 2)

                def end(t, rows):
                    V.tensor_scalar(tile_base[:, :], tile_base[:, :], float(P), None, ALU.add).then_inc(g_based, 1)
                    dve.wait_ge(g_x, t * 16 + 16)
                    V.tensor_reduce(g_c, sel[:, 0:SC].rearrange("p (a f) -> p f a", a=3), AX.X, ALU.add)
                    V.tensor_reduce(g_s3[:, :], sel[:, SC:PICK].rearrange("p (a u) -> p u a", a=3), AX.X, ALU.add).then_inc(g_parts, 1)
                    dve.wait_ge(g_parts, t + 1)
                    for u in range(3):
                        last = V.tensor_scalar(x4[:, u + 1, :], x4[:, 0, :], g_s3[:, u:u + 1], None, ALU.mult)
                    last.then_inc(g_xs, 1)
                    dve.wait_ge(g_turned, t + 2)
                    V.tensor_copy(xnt, pN[:, 0, 0:2 * P].rearrange("p (a b) -> p a b", a=2)).then_inc(g_xnt, 1)
                    dve.wait_ge(g_y, t + 1)
                    V.tensor_tensor(y, pY[:, 0:F], g_c, ALU.add).then_inc(g_added, 1)
                    dve.wait_ge(g_added, t + 1)
                    V.bn_stats(st, y).then_inc(g_st, 1)
                    dve.wait_ge(g_st, t + 1)
                    dve.sem_inc(g_waited[1], 1)
                    V.bn_aggr(mean_var, st).then_inc(g_mv, 1)
                    dve.wait_ge(g_root, t + 1)
                    V.reciprocal(inv, root).then_inc(g_inv, 1)
                    dve.wait_ge(g_inv, t + 1)
                    V.tensor_scalar(o, y, mean_var[:, 0:1], inv, ALU.subtract, ALU.mult).then_inc(g_o, 1)
                    dve.wait_ge(g_stored, t * 16 + 16)
                    dve.sem_inc(g_waited[1], 1)
                tiles(dve, False, start, chunk, end)

            @block.tensor
            def _(pe):
                pe.sem_inc(g_turned, 1)
                pe.sem_inc(g_picked, 1)

                def chunk(t, c, low, first):
                    pe.wait_ge(g_sel, c + 1)
                    pe.wait_ge(g_oh, c + 1)
                    nc.tensor.matmul(pX[:, 0:PICK], oh, win_b, start=True, stop=True).then_inc(g_picked, 1)

                def end(t, rows):
                    pe.wait_ge(g_xs, t + 1)
                    nc.tensor.transpose(pN[:, 0, 0:P], x4[:, 0:2, :].rearrange("p a b -> p (a b)"), ident[:, :])
                    nc.tensor.transpose(pN[:, 0, P:2 * P], x4[:, 2:4, :].rearrange("p a b -> p (a b)"), ident[:, :]).then_inc(g_turned, 1)
                    pe.wait_ge(g_xnt, t + 1)
                    nc.tensor.matmul(pY[:, 0:F], xnt[:, 0, :], WN1[:, :], start=True, stop=False)
                    nc.tensor.matmul(pY[:, 0:F], xnt[:, 1, :], WN2[:, :], start=False, stop=False)
                    nc.tensor.matmul(pY[:, 0:F], ones_b[:, 0:P], bias3[:, 1, :], start=False, stop=True).then_inc(g_y, 1)
                tiles(pe, False, nothing, chunk, end)

            @block.scalar
            def _(act):
                def end(t, rows):
                    act.wait_ge(g_mv, t + 1)
                    act.sem_inc(g_waited[2], 1)
                    nc.scalar.activation(root, mean_var[:, 1:2], ACT.Sqrt, bias=eps_c[:, :]).then_inc(g_root, 1)
                flag = act.value_load(flag_i[0:1, 0:1], min_val=0, max_val=2 * TA * TB)
                with act.If(flag > 0):
                    with act.Fori(0, TILES) as t:
                        end(t, P)


_INS = ["x", "src", "dst", "edge_attr_64", "L0_gnn_W_e", "L0_gnn_b_e", "L0_gnn_W_pre", "L0_gnn_b_pre",
        "L0_gnn_W_post", "L0_gnn_b_post", "L0_gnn_W_lin", "L0_gnn_b_lin"]


def kernel(**inputs):
    import numpy as _np
    import concourse.bacc as _bacc
    from concourse import mybir as _mybir
    from concourse.bass_utils import run_bass_kernel_spmd as _run

    nc = _bacc.Bacc("TRN2", target_bir_lowering=False, num_devices=1)
    arrays, args = {}, []
    for name in _INS:
        a = _np.ascontiguousarray(inputs[name])
        arrays[f"in_{name}"] = a
        args.append(nc.dram_tensor(f"in_{name}", a.shape, _mybir.dt.from_np(a.dtype), kind="ExternalInput").ap())
    shape = inputs["x"].shape
    out = nc.dram_tensor("out_0", shape, _mybir.dt.float32, kind="ExternalOutput").ap()
    build(nc, *args, out)
    return _run(nc, [arrays], core_ids=[0]).results[0]["out_0"]
```
